# Optimizing a Trainium2 kernel written in Bass

```python
import numpy as np
import jax
import jax.numpy as jnp

def _softmax(x, axis=-1):
    return jax.nn.softmax(x, axis=axis)

def _gelu(x):
    return jax.nn.gelu(x, approximate=True)

def _silu(x):
    return jax.nn.silu(x)

def _sigmoid(x):
    return jax.nn.sigmoid(x)

def _layernorm(x, axis=-1, eps=1e-05):
    m = jnp.mean(x, axis=axis, keepdims=True)
    v = jnp.var(x, axis=axis, keepdims=True)
    return (x - m) / jnp.sqrt(v + eps)

def _scatter_add(tgt, idx, src, axis=0):
    return tgt.at[idx].add(src)

def _segment_sum(src, seg, n):
    return jax.ops.segment_sum(src, seg, n)
kernel_name = 'mk_sandwich_d2_jaxref_r8_425030'

def setup_inputs(seed: int=0):
    np.random.seed(seed)
    _w = jnp.asarray

    def _L0_attn_setup():
        import jax, jax.numpy as jnp
        import numpy as np
        HIDDEN = 512
        N_HEADS = 32
        N_KV = 8
        HEAD_DIM = HIDDEN // N_HEADS
        Q_PER_KV = N_HEADS // N_KV
        SEQ = 256
        ROPE_BASE = 1000000.0
        POS_SCALE = 1.0
        SM_SCALE = 1.0 / HEAD_DIM
        BLOCK = 64
        LOCAL_BLOCKS = 16
        VERT_STRIDE = 8

        def _blocksparse_mask(seq_len):
            nb = seq_len // BLOCK
            qb = np.arange(nb)[:, None]
            kb = np.arange(nb)[None, :]
            bmask = (kb <= qb) & ((qb - kb < LOCAL_BLOCKS) | ((kb + 1) % VERT_STRIDE == 0))
            emask = np.kron(bmask, np.ones((BLOCK, BLOCK), dtype=bool))
            i = np.arange(seq_len)
            emask &= i[:, None] >= i[None, :]
            return jnp.asarray(emask)

        def _rope(x, cos, sin):
            x1, x2 = jnp.split(x, 2, axis=-1)
            rot = jnp.concatenate([-x2, x1], axis=-1)
            return x * cos[None, :, None, :] + rot * sin[None, :, None, :]
        key = jax.random.key(seed)
        k1, k2, k3, k4, k5 = jax.random.split(key, 5)
        qkv_out = (N_HEADS + 2 * N_KV) * HEAD_DIM
        return {'hidden_states': jax.random.normal(k1, (1, SEQ, HIDDEN), dtype=jnp.float32), 'w_qkv': jax.random.normal(k2, (qkv_out, HIDDEN), dtype=jnp.float32) * 0.02, 'b_qkv': jnp.zeros((qkv_out,), dtype=jnp.float32), 'w_dense': jax.random.normal(k3, (HIDDEN, HIDDEN), dtype=jnp.float32) * 0.02, 'b_dense': jnp.zeros((HIDDEN,), dtype=jnp.float32)}
    _L0_attn_in = _L0_attn_setup()

    def _L0_ffn_setup():
        import jax, jax.numpy as jnp
        import numpy as np
        N_EXPERTS = 28
        TOP_K = 2
        RANK = 8
        LORA_ALPHA = 16
        SCALING = LORA_ALPHA / RANK
        TEMP = 1.0
        key = jax.random.key(seed)
        ks = jax.random.split(key, 5)
        B, S, D_IN, D_OUT = (4, 256, 512, 512)
        x = jax.random.normal(ks[0], (B, S, D_IN), dtype=jnp.float32)
        base_W = jax.random.normal(ks[1], (D_OUT, D_IN), dtype=jnp.float32) * (1.0 / np.sqrt(D_IN))
        gate_W = jax.random.normal(ks[2], (N_EXPERTS, D_IN), dtype=jnp.float32) * (1.0 / np.sqrt(D_IN))
        lora_A = jax.random.normal(ks[3], (N_EXPERTS, RANK, D_IN), dtype=jnp.float32) * (1.0 / np.sqrt(D_IN))
        lora_B = jax.random.normal(ks[4], (N_EXPERTS, D_OUT, RANK), dtype=jnp.float32) * 0.01
        return {'x': x, 'base_W': base_W, 'gate_W': gate_W, 'lora_A': lora_A, 'lora_B': lora_B}
    _L0_ffn_in = _L0_ffn_setup()

    def _L1_attn_setup():
        import jax, jax.numpy as jnp
        import numpy as np
        B, T, H, S, F, G = (2, 256, 512, 128, 1248, 6)
        GRAD_ORDER_MIN = 4
        THD = 2.5
        key = jax.random.key(seed)
        ks = jax.random.split(key, 9)
        sc = 0.02
        hidden_states = jax.random.normal(ks[0], (B, T, H), jnp.float32)
        up_w = jax.random.normal(ks[1], (S, H), jnp.float32) * sc
        gate_w = jax.random.normal(ks[2], (S, H), jnp.float32) / np.sqrt(H)
        local_point = jax.random.normal(ks[3], (S,), jnp.float32)
        local_approx_output = jax.random.normal(ks[4], (H, S), jnp.float32) * sc
        fuse_weight = jax.random.normal(ks[5], (H, S, G), jnp.float32) * sc
        discount_factor = jnp.asarray(np.cumsum(np.log(np.arange(1, G + 1, dtype=np.float64))), jnp.float32)
        ffn_gate_w = jax.random.normal(ks[6], (F, H), jnp.float32) * sc
        ffn_up_w = jax.random.normal(ks[7], (F, H), jnp.float32) * sc
        ffn_down_w = jax.random.normal(ks[8], (H, F), jnp.float32) * sc
        return {'hidden_states': hidden_states, 'up_w': up_w, 'gate_w': gate_w, 'local_point': local_point, 'local_approx_output': local_approx_output, 'fuse_weight': fuse_weight, 'discount_factor': discount_factor, 'ffn_gate_w': ffn_gate_w, 'ffn_up_w': ffn_up_w, 'ffn_down_w': ffn_down_w}
    _L1_attn_in = _L1_attn_setup()

    def _L1_ffn_setup():
        import jax, jax.numpy as jnp
        import numpy as np
        M = 512
        K = 512

        def _make_2to4_mask(key, shape):
            scores = jax.random.normal(key, shape)
            g = scores.reshape(shape[0], shape[1] // 4, 4)
            rank = jnp.argsort(jnp.argsort(-jnp.abs(g), axis=-1), axis=-1)
            return (rank < 2).reshape(shape).astype(jnp.float32)
        key = jax.random.key(seed)
        k_x, k_w12, k_b12, k_w3, k_b3, k_m = jax.random.split(key, 6)
        x = jax.random.normal(k_x, (4, 256, K), dtype=jnp.float32)
        w12_dense = jax.random.normal(k_w12, (2 * M, K), dtype=jnp.float32) * (1.0 / np.sqrt(K))
        mask12 = _make_2to4_mask(k_m, (2 * M, K))
        w12 = w12_dense * mask12
        b12 = jax.random.normal(k_b12, (2 * M,), dtype=jnp.float32) * 0.01
        w3 = jax.random.normal(k_w3, (M, M), dtype=jnp.float32) * (1.0 / np.sqrt(M))
        b3 = jax.random.normal(k_b3, (M,), dtype=jnp.float32) * 0.01
        return {'x': x, 'w12': w12, 'b12': b12, 'w3': w3, 'b3': b3}
    _L1_ffn_in = _L1_ffn_setup()
    _d = {'L0_attn_hidden_states': _L0_attn_in['hidden_states'], 'L0_attn_w_qkv': _L0_attn_in['w_qkv'], 'L0_attn_b_qkv': _L0_attn_in['b_qkv'], 'L0_attn_w_dense': _L0_attn_in['w_dense'], 'L0_attn_b_dense': _L0_attn_in['b_dense'], 'L0_ffn_base_W': _L0_ffn_in['base_W'], 'L0_ffn_gate_W': _L0_ffn_in['gate_W'], 'L0_ffn_lora_A': _L0_ffn_in['lora_A'], 'L0_ffn_lora_B': _L0_ffn_in['lora_B'], 'L1_attn_up_w': _L1_attn_in['up_w'], 'L1_attn_gate_w': _L1_attn_in['gate_w'], 'L1_attn_local_point': _L1_attn_in['local_point'], 'L1_attn_local_approx_output': _L1_attn_in['local_approx_output'], 'L1_attn_fuse_weight': _L1_attn_in['fuse_weight'], 'L1_attn_discount_factor': _L1_attn_in['discount_factor'], 'L1_attn_ffn_gate_w': _L1_attn_in['ffn_gate_w'], 'L1_attn_ffn_up_w': _L1_attn_in['ffn_up_w'], 'L1_attn_ffn_down_w': _L1_attn_in['ffn_down_w'], 'L1_ffn_w12': _L1_ffn_in['w12'], 'L1_ffn_b12': _L1_ffn_in['b12'], 'L1_ffn_w3': _L1_ffn_in['w3'], 'L1_ffn_b3': _L1_ffn_in['b3']}
    _x0 = _d['L0_attn_hidden_states']
    _d['L0_attn_hidden_states'] = jax.random.normal(jax.random.fold_in(jax.random.key(seed), 1), (8, 256, 512), dtype=_x0.dtype)
    del _x0
    return _d

def reference(L0_attn_hidden_states, L0_attn_w_qkv, L0_attn_b_qkv, L0_attn_w_dense, L0_attn_b_dense, L0_ffn_base_W, L0_ffn_gate_W, L0_ffn_lora_A, L0_ffn_lora_B, L1_attn_up_w, L1_attn_gate_w, L1_attn_local_point, L1_attn_local_approx_output, L1_attn_fuse_weight, L1_attn_discount_factor, L1_attn_ffn_gate_w, L1_attn_ffn_up_w, L1_attn_ffn_down_w, L1_ffn_w12, L1_ffn_b12, L1_ffn_w3, L1_ffn_b3):

    def _L0_attn_ref(hidden_states, w_qkv, b_qkv, w_dense, b_dense):
        import jax, jax.numpy as jnp
        import numpy as np
        HIDDEN = 512
        N_HEADS = 32
        N_KV = 8
        HEAD_DIM = HIDDEN // N_HEADS
        Q_PER_KV = N_HEADS // N_KV
        SEQ = 256
        ROPE_BASE = 1000000.0
        POS_SCALE = 1.0
        SM_SCALE = 1.0 / HEAD_DIM
        BLOCK = 64
        LOCAL_BLOCKS = 16
        VERT_STRIDE = 8

        def _blocksparse_mask(seq_len):
            nb = seq_len // BLOCK
            qb = np.arange(nb)[:, None]
            kb = np.arange(nb)[None, :]
            bmask = (kb <= qb) & ((qb - kb < LOCAL_BLOCKS) | ((kb + 1) % VERT_STRIDE == 0))
            emask = np.kron(bmask, np.ones((BLOCK, BLOCK), dtype=bool))
            i = np.arange(seq_len)
            emask &= i[:, None] >= i[None, :]
            return jnp.asarray(emask)

        def _rope(x, cos, sin):
            x1, x2 = jnp.split(x, 2, axis=-1)
            rot = jnp.concatenate([-x2, x1], axis=-1)
            return x * cos[None, :, None, :] + rot * sin[None, :, None, :]
        B, S, _ = hidden_states.shape
        qkv = jnp.einsum('bsh,oh->bso', hidden_states, w_qkv) + b_qkv
        qkv = qkv.reshape(B, S, N_KV, Q_PER_KV + 2, HEAD_DIM)
        q = qkv[:, :, :, :Q_PER_KV].reshape(B, S, N_HEADS, HEAD_DIM)
        k = qkv[:, :, :, Q_PER_KV]
        v = qkv[:, :, :, Q_PER_KV + 1]
        inv_freq = 1.0 / ROPE_BASE ** (jnp.arange(0, HEAD_DIM, 2, dtype=jnp.float32) / HEAD_DIM)
        t = jnp.arange(S, dtype=jnp.float32) * POS_SCALE
        freqs = jnp.outer(t, inv_freq)
        emb = jnp.concatenate([freqs, freqs], axis=-1)
        cos, sin = (jnp.cos(emb), jnp.sin(emb))
        q = _rope(q, cos, sin)
        k = _rope(k, cos, sin)
        k = jnp.repeat(k, Q_PER_KV, axis=2)
        v = jnp.repeat(v, Q_PER_KV, axis=2)
        mask = _blocksparse_mask(S)
        scores = jnp.einsum('bqhd,bkhd->bhqk', q, k) * SM_SCALE
        scores = jnp.where(mask[None, None], scores, jnp.finfo(scores.dtype).min)
        probs = jax.nn.softmax(scores, axis=-1)
        ctx = jnp.einsum('bhqk,bkhd->bqhd', probs, v).reshape(B, S, HIDDEN)
        out = jnp.einsum('bsh,oh->bso', ctx, w_dense) + b_dense
        return out

    def _L0_ffn_ref(x, base_W, gate_W, lora_A, lora_B):
        import jax, jax.numpy as jnp
        import numpy as np
        N_EXPERTS = 28
        TOP_K = 2
        RANK = 8
        LORA_ALPHA = 16
        SCALING = LORA_ALPHA / RANK
        TEMP = 1.0
        B, S, D_in = x.shape
        xf = x.reshape(B * S, D_in)
        base = xf @ base_W.T
        logits = xf @ gate_W.T
        top_vals, top_idx = jax.lax.top_k(logits, TOP_K)
        top_probs = jax.nn.softmax(top_vals / TEMP, axis=-1)
        N = xf.shape[0]
        gate_full = jnp.zeros((N, N_EXPERTS), dtype=xf.dtype).at[jnp.arange(N)[:, None], top_idx].add(top_probs)
        h = jnp.einsum('nd,erd->ner', xf, lora_A)
        h = h * (gate_full * SCALING)[:, :, None]
        lora_out = jnp.einsum('ner,eor->no', h, lora_B)
        out = base + lora_out
        return out.reshape(B, S, -1)

    def _L1_attn_ref(hidden_states, up_w, gate_w, local_point, local_approx_output, fuse_weight, discount_factor, ffn_gate_w, ffn_up_w, ffn_down_w):
        import jax, jax.numpy as jnp
        import numpy as np
        B, T, H, S, F, G = (2, 256, 512, 128, 1248, 6)
        GRAD_ORDER_MIN = 4
        THD = 2.5
        approx_up = hidden_states @ up_w.T
        gate_pre = hidden_states @ gate_w.T
        delta = gate_pre - local_point
        neg_factor = jnp.where(delta > 0, 1.0, -1.0).astype(hidden_states.dtype)
        delta_abs = jnp.abs(delta)
        log_delta = jnp.log(delta_abs)
        keep = (delta_abs <= THD).astype(hidden_states.dtype)
        approx_out = approx_up @ local_approx_output.T
        for idx in range(G):
            m = idx + 1
            dterm = jnp.exp(log_delta * m - discount_factor[idx])
            if m % 2 == 1:
                dterm = dterm * neg_factor
            tmp = dterm * approx_up
            if m > GRAD_ORDER_MIN:
                tmp = tmp * keep
            approx_out = approx_out + tmp @ fuse_weight[:, :, idx].T
        ffn_out = jax.nn.silu(hidden_states @ ffn_gate_w.T) * (hidden_states @ ffn_up_w.T) @ ffn_down_w.T
        return approx_out + ffn_out

    def _L1_ffn_ref(x, w12, b12, w3, b3):
        import jax, jax.numpy as jnp
        import numpy as np
        M = 512
        K = 512

        def _make_2to4_mask(key, shape):
            scores = jax.random.normal(key, shape)
            g = scores.reshape(shape[0], shape[1] // 4, 4)
            rank = jnp.argsort(jnp.argsort(-jnp.abs(g), axis=-1), axis=-1)
            return (rank < 2).reshape(shape).astype(jnp.float32)
        x12 = jnp.einsum('bsk,mk->bsm', x, w12) + b12
        x1, x2 = jnp.split(x12, 2, axis=-1)
        x4 = jax.nn.silu(x1) * x2
        return jnp.einsum('bsm,nm->bsn', x4, w3) + b3
    x = L0_attn_hidden_states
    x = x + _layernorm(_L0_attn_ref(_layernorm(x, axis=-1), L0_attn_w_qkv, L0_attn_b_qkv, L0_attn_w_dense, L0_attn_b_dense), axis=-1)
    x = x + _layernorm(_L0_ffn_ref(_layernorm(x, axis=-1), L0_ffn_base_W, L0_ffn_gate_W, L0_ffn_lora_A, L0_ffn_lora_B), axis=-1)
    x = x + _layernorm(_L1_attn_ref(_layernorm(x, axis=-1), L1_attn_up_w, L1_attn_gate_w, L1_attn_local_point, L1_attn_local_approx_output, L1_attn_fuse_weight, L1_attn_discount_factor, L1_attn_ffn_gate_w, L1_attn_ffn_up_w, L1_attn_ffn_down_w), axis=-1)
    x = x + _layernorm(_L1_ffn_ref(_layernorm(x, axis=-1), L1_ffn_w12, L1_ffn_b12, L1_ffn_w3, L1_ffn_b3), axis=-1)
    return x

_drawn_inputs = setup_inputs


def setup_inputs(seed=0):
    import zlib

    import numpy as np

    out = dict(_drawn_inputs(seed))
    spreads = {'L0_attn_b_qkv': (0.0, 0.1), 'L0_attn_b_dense': (0.0, 0.1)}
    factors = {'L1_ffn_b12': 6.299, 'L1_ffn_b3': 3.748}
    for name, (base, spread) in spreads.items():
        noise = np.random.default_rng([zlib.crc32(name.encode()), seed]).standard_normal(out[name].shape)
        drawn = base * np.exp(spread * noise) if base else spread * noise
        out[name] = jnp.asarray(drawn.astype(out[name].dtype))
    for name, factor in factors.items():
        out[name] = (out[name] * factor).astype(out[name].dtype)
    return out
```

```python
from contextlib import ExitStack

import concourse.bass as bass
from concourse import mybir

P = 128
F32 = mybir.dt.float32
F32R = mybir.dt.float32r
BF16 = mybir.dt.bfloat16
U32 = mybir.dt.uint32
ALU = mybir.AluOpType
ACT = mybir.ActivationFunctionType
AX_X = mybir.AxisListType.X

H = 512
KT = H // P
NG = 4
TG = 4
NKV, QPK, HD = 8, 4, 16
NPAIR = NKV // 2
STEPS = 2 * NPAIR
NE, RANK = 28, 8
LR = NE * RANK
LH = LR // 2
NORD = 6
THD = 2.5
EPS = 1e-5
MASKED = -1e30

PHASES = [("attn", 10, 0), ("moe", 9, 1), ("taylor", 9, 0), ("glu_a", 9, 1), ("glu_b", 12, 0), ("glu_c", 9, 1),
          ("glu_d", 12, 0)]
CHUNK0 = [sum(n for _, n, _ in PHASES[:i]) for i in range(len(PHASES) + 1)]


class Signal:

    def __init__(self, handle, per, credit=0, base=0):
        self.h, self.per, self.credit, self.base = handle, per, credit, base

    def done(self, it, n):
        return it * self.per + (self.base + self.credit + n + 1)

    def free(self, it, n, bufs):
        assert bufs <= self.credit
        return it * self.per + (self.base + self.credit + n + 1 - bufs)


def lone(eng):
    eng.nop(nofuse=True)


class Chain:

    def __init__(self, eng, handle):
        self.eng, self.h, self.total, self.it, self.per, self.n = eng, handle, 0, 0, 0, 0

    def link(self, ins):
        self.n += 1
        ins.then_inc(self.h, 1)
        self.eng.wait_ge(self.h, self.it * self.per + (self.total + self.n))

    def commit(self):
        self.total, self.n = self.total + self.n, 0

    def begin(self, it, last, per):
        if last:
            self.total, self.it, self.per = self.total + (NG - 1) * per, 0, 0
        else:
            self.it, self.per = it, per

    def end(self, last):
        assert last or self.n == self.per, ("chained in one iteration:", self.n, "expected", self.per)
        self.total, self.n = self.total + (self.n if last else 0), 0


def build(nc, x_in, w_in, cons_f, cons_b, biases, out):
    with ExitStack() as top:
        def sb(stack, name, shape, dt):
            return stack.enter_context(nc.sbuf_tensor(name, shape, dt))

        def sem(name):
            return top.enter_context(nc.semaphore(name))

        def signal(name, per, credit=0, base=0):
            s = Signal(sem(name), per, credit, base)
            if credit:
                credits.append(s)
            return s

        credits = []
        X = sb(top, "x_resident", [P, NG * TG, H], F32)
        W = [sb(top, "weights_even", [P, 12, 2, H], F32R), sb(top, "weights_odd", [P, 9, 2, H], F32R)]
        stage = sb(top, "weight_stage", [P, 2, H], F32)
        xn = sb(top, "x_normed", [P, 2, H], F32)
        xT = sb(top, "xT_hi_lo", [P, 2, KT, H], F32R)
        cf = sb(top, "constants_f32", list(cons_f.shape), F32)
        cb = sb(top, "constants_bf16", list(cons_b.shape), BF16)
        fst = sb(top, "front_stats", [P, 2, 6], F32)
        fmv = sb(top, "front_mean_var", [P, TG, 2], F32)
        frs = sb(top, "front_rstd", [P, 2, TG], F32)
        bst = sb(top, "back_stats", [P, 2, 6], F32)
        bmv = sb(top, "back_mean_var", [P, TG, 2], F32)
        brs = sb(top, "back_rstd", [P, 2, TG], F32)
        mhalf = sb(top, "minus_half", [P, TG], F32)
        cfac = sb(top, "order_factor", [P, 8], F32)
        banks = [top.enter_context(nc.psum_tensor(f"bank{i}", [P, 512], F32)) for i in range(8)]
        Hb, Ob = banks[:4], banks[4:]

        identf = cf[:, 0:128]
        cos_t = cf[:, 128:160].rearrange("p (t d) -> p t d", t=2)
        sin_t = cf[:, 160:176].rearrange("p (t d) -> p t d", t=2)
        nsin_t = cf[:, 176:192].rearrange("p (t d) -> p t d", t=2)
        iota = cf[:, 192:192 + NE]
        headsel = cf[:, 220:224]
        lp = cf[:, 224:225]
        disc = cf[:, 225:231]
        b12 = cf[:, 231:239]
        zero8 = cf[:, 239:247]
        identb = cb[:, 0:128]
        mask_qk = cb[:, 128:256]
        mask_kq = cb[:, 256:384]
        sel = cb[:, 384:640].rearrange("p (a k) -> p a k", a=2)

        s_x = [sem(f"s_x_loaded{g}") for g in range(NG)]
        s_const = sem("s_const")
        s_init = sem("s_init")
        s_wdma = [sem("s_wdma_even"), sem("s_wdma_odd")]
        s_wsplit = [sem("s_wsplit_even"), sem("s_wsplit_odd")]
        s_out = sem("s_out")
        s_fmv, s_frs = sem("s_front_meanvar"), sem("s_front_rstd")
        s_xn, s_fhi, s_flo = sem("s_xn"), sem("s_front_hi"), sem("s_front_lo")
        s_xntr = sem("s_xn_transposed")
        chain_dve, chain_pool, chain_act = sem("chain_dve"), sem("chain_pool"), sem("chain_act")

        def front_signals(ph):
            b = NG * ph
            return dict(mv=Signal(s_fmv, 1, 0, b), rs=Signal(s_frs, 1, 0, b), xn=Signal(s_xn, 4, 0, 4 * b),
                        tr=Signal(s_xntr, 4, 2, 4 * b), hi=Signal(s_fhi, 4, 0, 4 * b), lo=Signal(s_flo, 4, 0, 4 * b))

        fr = [front_signals(ph) for ph in range(len(PHASES))]

        class Ph:
            pass

        phs = []
        for i, (name, nchunk, wb) in enumerate(PHASES):
            s = Ph()
            s.i, s.name, s.W = i, name, W[wb]
            s.updates = name in ("attn", "moe", "glu_c", "glu_d")
            nf = {"attn": 0, "moe": 2, "taylor": NORD + 1}.get(name, nchunk // 3)
            s.nf = nf
            s.o_ready = signal(f"{name}_o_ready", 4)
            s.o_free = signal(f"{name}_o_free", 4, 4)
            s.bmv = signal(f"{name}_bmv", 2 if name == "attn" else 1)
            s.brs = signal(f"{name}_brs", 2 if name == "attn" else 1)
            s.z_ready = signal(f"{name}_z_ready", 4)
            s.xupd = signal(f"{name}_xupd", 4, 4)
            s.pe_end = sem(f"{name}_pe_end")
            if name == "attn":
                s.qkv = signal("attn_qkv_ready", 8)
                s.qkv_free = signal("attn_qkv_free", 4, 2)
                s.rope = signal("attn_rope", 4, 1)
                s.stack = signal("attn_stack", 8)
                s.tr = signal("attn_stack_transposed", 8, 2)
                s.tev = signal("attn_transposed_kept", 8)
                s.sq = signal("attn_scores_q", 48)
                s.red = signal("attn_reduced", 48)
                s.mp = signal("attn_max_parts", 8)
                s.mt = signal("attn_max_transposed", 8)
                s.rr = signal("attn_max_rows", 8)
                s.st = signal("attn_scores_k", 48)
                s.ex = signal("attn_exp", 48)
                s.pv = signal("attn_pv", 16, 2)
                s.nrm = signal("attn_ctx_normed", 8, 1)
                s.ct = signal("attn_ctx_transposed", 4)
                s.chi = signal("attn_ctx_hi", 4)
                s.clo = signal("attn_ctx_lo", 4)
            else:
                s.in_ready = signal(f"{name}_in_ready", {"moe": 4, "taylor": 2}.get(name, 2 * nf))
                s.sg = signal(f"{name}_sg", 1 if name == "taylor" else nf)
                s.hf = signal(f"{name}_hf", nf, 2)
                s.hhi = signal(f"{name}_hhi", nf)
                s.hlo = signal(f"{name}_hlo", nf)
                s.hused = signal(f"{name}_hused", nf, 2)
                if name == "moe":
                    s.rt = signal("moe_route_diff", 1)
                    s.re = signal("moe_route_exp", 1)
                    s.hs = signal("moe_h_scaled", 4)
                    s.ht = signal("moe_h_transposed", 1)
            phs.append(s)

        def x_writer(ph):
            w = [p for p in phs[:ph] if p.updates]
            return w[-1] if w else None

        def wait_x(eng, ph, group, tile):
            w = x_writer(ph)
            if w is not None:
                eng.wait_ge(w.xupd.h, w.xupd.done(group, tile))

        def nxt(ph, it, last):
            return (ph + 1, 0) if last else (ph, it + 1)

        def front_stats(dve, ch, fph, fit):
            for t in range(TG):
                wait_x(dve, fph, fit, t)
                lone(dve)
                ch.link(dve.bn_stats(fst[:, t % 2, :], X[:, fit * TG + t, :]))
                lone(dve)
                ins = dve.bn_aggr(fmv[:, t, :], fst[:, t % 2, :])
            ins.then_inc(fr[fph]["mv"].h, 1)

        def front_norm(dve, fph, fit, tiles):
            f = fr[fph]
            for t in tiles:
                if t == 0:
                    dve.wait_ge(f["rs"].h, f["rs"].done(fit, 0))
                dve.wait_ge(f["tr"].h, f["tr"].free(fit, t, 2))
                dve.tensor_scalar(xn[:, t % 2, :], X[:, fit * TG + t, :], fmv[:, t, 0:1], frs[:, 1, t:t + 1],
                                  ALU.subtract, ALU.mult).then_inc(f["xn"].h, 1)

        def front_rstd(pool, ch, fph, fit):
            f = fr[fph]
            pool.wait_ge(f["mv"].h, f["mv"].done(fit, 0))
            lone(pool)
            ch.link(pool.tensor_scalar(frs[:, 0, :], fmv[:, :, 1], 1.0, EPS, ALU.mult, ALU.add))
            pool.tensor_tensor(frs[:, 1, :], frs[:, 0, :], mhalf[:, :], ALU.pow).then_inc(f["rs"].h, 1)

        def front_transpose(pe, fph, fit):
            f = fr[fph]
            for t in range(TG):
                pe.wait_ge(f["xn"].h, f["xn"].done(fit, t))
                for k in range(KT):
                    ins = pe.transpose(Hb[k][:, t * P:(t + 1) * P], xn[:, t % 2, k * P:(k + 1) * P], identf)
                ins.then_inc(f["tr"].h, 1)

        def front_hi(act, fph, fit):
            f = fr[fph]
            act.wait_ge(f["tr"].h, f["tr"].done(fit, 3))
            for k in range(KT):
                act.activation(xT[:, 0, k, :], Hb[k][:, :], ACT.Copy).then_inc(f["hi"].h, 1)

        def front_lo(dve, fph, fit):
            f = fr[fph]
            for k in range(KT):
                dve.wait_ge(f["hi"].h, f["hi"].done(fit, k))
                dve.tensor_tensor(xT[:, 1, k, :], Hb[k][:, :], xT[:, 0, k, :].bitcast(F32),
                                  ALU.subtract).then_inc(f["lo"].h, 1)

        PASSES = ((0, 0), (0, 1), (1, 0))

        def tokens_by_weights(pe, bank, cols, t, chunk_of, first=True, final=True):
            for k in range(KT):
                w = chunk_of(k)
                for n, (a, b) in enumerate(PASSES):
                    ins = pe.matmul(bank[:, 0:cols], xT[:, b, k, t * P:(t + 1) * P], w[a],
                                    start=first and k == 0 and n == 0, stop=final and k == KT - 1 and n == 2)
            return ins

        def features(pe, bank, chunk_of):
            for k in range(KT):
                w = chunk_of(k)
                for n, (a, b) in enumerate(PASSES):
                    ins = pe.matmul(bank[:, :], w[a], xT[:, b, k, :], start=k == 0 and n == 0,
                                    stop=k == KT - 1 and n == 2)
            return ins

        def weights_wait(pe, ph):
            for s in range(2):
                pe.wait_ge(s_wsplit[s], wcount(ph + 1, s))

        def wper(ph):
            return PHASES[ph][1] if ph == 0 else PHASES[ph][1] // 3

        def wslot(per, s):
            return (per + 1 - s) // 2

        def wcount(ph, s):
            return sum(wslot(wper(p), s) * (1 if p == 0 else 3) for p in range(ph))

        def w_load(sp, ph, it):
            per = wper(ph)
            for j in range(per):
                s, n = j % 2, j // 2
                before = it * wslot(per, s) + (wcount(ph, s) + n)
                if not (ph == 0 and n == 0):
                    sp.wait_ge(s_wsplit[s], before)
                sp.dma_start(stage[:, s, :], w_in[it * per + (CHUNK0[ph] + j)]).then_inc(s_wdma[s], 16)

        def w_split(pool, ch, ph, it, js=None):
            per = wper(ph)
            for j in range(per) if js is None else js:
                s, n = j % 2, j // 2
                now = it * (16 * wslot(per, s)) + 16 * (wcount(ph, s) + n + 1)
                hi, lo = (W[PHASES[ph][2]][:, it * per + j, a, :] for a in range(2))
                pool.wait_ge(s_wdma[s], now)
                lone(pool)
                ch.link(pool.tensor_copy(hi, stage[:, s, :]))
                pool.tensor_tensor(lo, stage[:, s, :], hi.bitcast(F32), ALU.subtract).then_inc(s_wsplit[s], 1)

        def back_stats(dve, ch, s, it, tiles, n, src):
            for t in tiles:
                lone(dve)
                ch.link(dve.bn_stats(bst[:, t % 2, :], src(t)))
                lone(dve)
                ins = dve.bn_aggr(bmv[:, t, :], bst[:, t % 2, :])
            ins.then_inc(s.bmv.h, 1)

        def back_rstd(pool, ch, s, it, tiles, n):
            a, b = tiles[0], tiles[-1] + 1
            pool.wait_ge(s.bmv.h, s.bmv.done(it, n))
            lone(pool)
            ch.link(pool.tensor_scalar(brs[:, 0, a:b], bmv[:, a:b, 1], 1.0, EPS, ALU.mult, ALU.add))
            pool.tensor_tensor(brs[:, 1, a:b], brs[:, 0, a:b], mhalf[:, a:b], ALU.pow).then_inc(s.brs.h, 1)

        def back_norm(dve, s, it, tiles, n, src, dst, frees_o=False):
            dve.wait_ge(s.brs.h, s.brs.done(it, n))
            for t in tiles:
                if frees_o:
                    dve.wait_ge(s.xupd.h, s.xupd.free(it, t, 4))
                ins = dve.tensor_scalar(dst(t), src(t), bmv[:, t, 0:1], brs[:, 1, t:t + 1], ALU.subtract, ALU.mult)
                ins.then_inc(s.z_ready.h, 1)

        def back_update(pool, s, it, tiles, z):
            for t in tiles:
                x = X[:, it * TG + t, :]
                pool.wait_ge(s.z_ready.h, s.z_ready.done(it, t))
                pool.tensor_tensor(x, x, z(t), ALU.add).then_inc(s.xupd.h, 1)

        def groups(eng, body):
            with eng.Fori(0, NG - 1) as it:
                body(it, False)
            body(NG - 1, True)

        with ExitStack() as mem:
            s = phs[0]
            WA = s.W
            bq = sb(mem, "bias_qkv", [P, 768], F32)
            bd = sb(mem, "bias_dense", [P, H], F32)
            qk = sb(mem, "qk_roped", [P, TG, 640], F32)
            vaug = sb(mem, "v_and_ones", [P, TG, NKV, HD + 1], F32)
            rtmp = sb(mem, "rope_tmp", [P, 640], F32)
            qst = sb(mem, "q_stack", [P, 2, 2, QPK, 2, 64], F32R)
            kst = sb(mem, "k_stack", [P, 2, 2, 2, 64], F32R)
            QT = sb(mem, "qT_stack", [P, 2, 2, H], F32R)
            PT = sb(mem, "probs", [P, 6, H], F32)
            RR = sb(mem, "max_rows", [P, 2, 2, H], BF16)
            mx = sb(mem, "max_q", [P, 2, 2, 8], F32)
            mp = sb(mem, "max_parts", [P, 2, 2, P], BF16)
            rden = sb(mem, "rden", [P, 16], F32)
            ctx = sb(mem, "ctx", [P, 2, H], F32)
            zA = sb(mem, "z_attn", [P, 2, H], F32)
            ctxT = WA[:, 10, :, :].rearrange("p a (c q) -> p a c q", q=P)
            KTp = WA[:, 11, :, :].rearrange("p b (a t k) -> p b a t k", a=2, t=2)
            mT = Ob[2][:, 256:384].bitcast(BF16)
            KTb, PVb = Ob[2], Ob[3]

            ring = []
            for i in range(-1, STEPS):
                if i + 1 < STEPS:
                    ring += [("q", 6 * (i + 1) + n) for n in range(6)]
                if i >= 0:
                    ring += [("k", 6 * i + n) for n in range(6)]
            use_of = {r: u for u, r in enumerate(ring)}

            def ring_wait(pe, it, kind, n):
                u = use_of[(kind, n)]
                if u >= 4:
                    before, m = ring[u - 4]
                    sig = s.red if before == "q" else s.ex
                    pe.wait_ge(sig.h, sig.done(it, m))
                return Hb[u % 4]

            def ring_bank(kind, n):
                return Hb[use_of[(kind, n)] % 4]

            def pe_transposes(pe, it, i):
                for t in range(2):
                    pe.wait_ge(s.stack.h, s.stack.done(it, i))
                    if t == 0 and i >= 1:
                        pe.wait_ge(s.tev.h, s.tev.done(it, i - 1))
                    for j in range(QPK):
                        pe.transpose(Ob[t][:, j * P:(j + 1) * P],
                                     qst[:, i % 2, t, j, :, :].rearrange("p a c -> p (a c)").bitcast(F32), identf)
                for t in range(2):
                    ins = pe.transpose(KTb[:, t * P:(t + 1) * P],
                                       kst[:, i % 2, t, :, :].rearrange("p a c -> p (a c)").bitcast(F32), identf)
                ins.then_inc(s.tr.h, 1)

            def pe_scores_q(pe, it, i):
                pe.wait_ge(s.tev.h, s.tev.done(it, i))
                for ab in range(2):
                    for n, (qt, j0, nk) in enumerate(((0, 0, 1), (1, 0, 2), (1, 2, 2))):
                        bank = ring_wait(pe, it, "q", 6 * i + 3 * ab + n)
                        nj = QPK // nk
                        v = bank[:, :].rearrange("p (j k) -> p j k", j=nj)
                        mrep = mask_qk.unsqueeze(1).broadcast_to([P, nj, P])
                        pe.matmul(v[:, :, (nk - 1) * P:nk * P], identb, mrep, start=True, stop=False,
                                  skip_group_check=True)
                        for j in range(nj):
                            ins = pe.matmul(v[:, j, :], QT[:, i % 2, qt, (j0 + j) * P:(j0 + j + 1) * P],
                                            KTp[:, i % 2, ab, 0:nk, :].rearrange("p t k -> p (t k)"),
                                            start=False, stop=j == nj - 1, skip_group_check=True)
                        ins.then_inc(s.sq.h, 1)

            def pe_max_rows(pe, it, i):
                pe.wait_ge(s.mp.h, s.mp.done(it, i))
                if i >= 1:
                    pe.wait_ge(s.rr.h, s.rr.done(it, i - 1))
                for qt in range(2):
                    ins = pe.transpose(mT[:, qt * P:(qt + 1) * P], mp[:, i % 2, qt, :], identb)
                ins.then_inc(s.mt.h, 1)

            BLOCKS = ((0, 0), (0, 1), (1, 1))

            def pe_scores_k(pe, it, i):
                pe.wait_ge(s.rr.h, s.rr.done(it, i))
                for ab in range(2):
                    for n, (kt, qt) in enumerate(BLOCKS):
                        bank = ring_wait(pe, it, "k", 6 * i + 3 * ab + n)
                        pe.matmul(bank[:, :], sel[:, ab, :], RR[:, i % 2, qt, :], start=True, stop=False)
                        if kt == qt:
                            pe.matmul(bank[:, :].rearrange("p (j q) -> p j q", j=QPK), identb,
                                      mask_kq.unsqueeze(1).broadcast_to([P, QPK, P]), start=False, stop=False)
                        pe.matmul(bank[:, :], KTp[:, i % 2, ab, kt, :], QT[:, i % 2, qt, :],
                                  start=False, stop=True).then_inc(s.st.h, 1)

            def pe_pv(pe, it, i):
                b, p = i // NPAIR, i % NPAIR
                pe.wait_ge(s.nrm.h, s.nrm.free(it, i, 1))
                v = PVb[:, 0:272].rearrange("p (t g j d) -> p t g j d", t=2, g=2, j=QPK)
                for ab in range(2):
                    pe.wait_ge(s.ex.h, s.ex.done(it, 6 * i + 3 * ab + 2))
                    g = 2 * p + ab
                    for j in range(QPK):
                        for n, (kt, qt) in enumerate(BLOCKS):
                            ins = pe.matmul(v[:, qt, ab, j, :], PT[:, 3 * ab + n, j * P:(j + 1) * P],
                                            vaug[:, 2 * b + kt, g, :], start=kt == 0, stop=kt == qt)
                    ins.then_inc(s.pv.h, 1)

            def pe_dense(pe, it, b):
                pe.wait_ge(s.nrm.h, s.nrm.done(it, NPAIR * b + NPAIR - 1))
                last_t = min(NPAIR * b + 5, STEPS - 1)
                pe.wait_ge(s.tev.h, s.tev.done(it, last_t))
                for qt in range(2):
                    if b:
                        pe.wait_ge(s.o_free.h, s.o_free.free(it, 2 + qt, 4) + 2)
                    for c in range(KT):
                        ins = pe.transpose(Ob[qt][:, c * P:(c + 1) * P], ctx[:, qt, c * P:(c + 1) * P], identf)
                    ins.then_inc(s.ct.h, 1)
                    pe.wait_ge(s.clo.h, s.clo.done(it, 2 * b + qt))
                    for c in range(KT):
                        for n, (a, x) in enumerate(PASSES):
                            ins = pe.matmul(Ob[qt][:, :], ctxT[:, x, c, :], WA[:, 6 + c, a, :],
                                            start=c == 0 and n == 0, stop=c == KT - 1 and n == 2)
                    ins.then_inc(s.o_ready.h, 1)

            def pe_attention(pe):
                weights_wait(pe, 0)
                pe.wait_ge(s_const, 16 * 4)
                pe.wait_ge(s_init, 2)
                front_transpose(pe, 0, 0)

                def body(it, last):
                    pe.wait_ge(fr[0]["lo"].h, fr[0]["lo"].done(it, 3))
                    for t in range(TG):
                        pe.wait_ge(s.qkv_free.h, s.qkv_free.free(it, t, 2))
                        q, kv = Hb[2 * t % 4], Hb[(2 * t + 1) % 4]
                        tokens_by_weights(pe, q, 512, t, lambda k: (WA[:, k, 0, :], WA[:, k, 1, :])).then_inc(s.qkv.h, 1)
                        tokens_by_weights(pe, kv, 256, t, lambda k: tuple(
                            WA[:, 4 + k // 2, a, (k % 2) * 256:(k % 2) * 256 + 256] for a in range(2))
                        ).then_inc(s.qkv.h, 1)
                    pe.wait_ge(s.qkv_free.h, s.qkv_free.done(it, 3))
                    fph, fit = nxt(0, it, last)
                    front_transpose(pe, fph, fit)
                    pe_transposes(pe, it, 0)
                    pe_transposes(pe, it, 1)
                    pe.wait_ge(fr[fph]["lo"].h, fr[fph]["lo"].done(fit, 3))
                    pe_scores_q(pe, it, 0)
                    for i in range(STEPS):
                        if i + 1 < STEPS:
                            pe_scores_q(pe, it, i + 1)
                        pe_max_rows(pe, it, i)
                        pe_scores_k(pe, it, i)
                        if i + 2 < STEPS:
                            if i + 2 == 6:
                                pe.wait_ge(s.o_free.h, s.o_free.done(it, 1))
                            pe_transposes(pe, it, i + 2)
                        pe_pv(pe, it, i)
                        if i == NPAIR - 1:
                            pe_dense(pe, it, 0)
                    pe_dense(pe, it, 1)
                    pe.wait_ge(s.o_free.h, s.o_free.done(it, 3))

                groups(pe, body)
                pe.sem_inc(s.pe_end, 1)

            def act_attention(act):
                front_hi(act, 0, 0)

                def keep(it, i):
                    act.wait_ge(s.tr.h, s.tr.done(it, i))
                    for t in range(2):
                        act.activation(QT[:, i % 2, t, :], Ob[t][:, :], ACT.Copy)
                    for ab in range(2):
                        r = slice(64 * ab, 64 * ab + 64)
                        ins = act.activation(KTp[r, i % 2, ab, :, :].rearrange("p t k -> p (t k)"), KTb[r, 0:256],
                                             ACT.Copy)
                    ins.then_inc(s.tev.h, 1)

                def exps(it, i):
                    for ab in range(2):
                        act.wait_ge(s.pv.h, s.pv.free(it, 2 * i + ab, 2))
                        for n in range(3):
                            m = 6 * i + 3 * ab + n
                            act.wait_ge(s.st.h, s.st.done(it, m))
                            act.activation(PT[:, 3 * ab + n, :], ring_bank("k", m)[:, :], ACT.Exp,
                                           scale=1.0 / HD).then_inc(s.ex.h, 1)

                def ctx_hi(it, b):
                    for qt in range(2):
                        act.wait_ge(s.ct.h, s.ct.done(it, 2 * b + qt))
                        act.activation(ctxT[:, 0, :, :].rearrange("p c q -> p (c q)"), Ob[qt][:, :],
                                       ACT.Copy).then_inc(s.chi.h, 1)

                def body(it, last):
                    front_hi(act, *nxt(0, it, last))
                    keep(it, 0)
                    keep(it, 1)
                    for i in range(STEPS):
                        exps(it, i)
                        if i + 2 < STEPS:
                            keep(it, i + 2)
                        if i == NPAIR - 1:
                            ctx_hi(it, 0)
                    ctx_hi(it, 1)

                groups(act, body)

            def dve_attention(dve, ch):
                ch.link(dve.memset(vaug[:, :, :, :], 1.0))
                ch.link(dve.memset(mp[:, :, :, :], 0.0))
                dve.memset(KTp[:, :, :, :, :].bitcast(F32), 0.0).then_inc(s_init, 1)
                dve.wait_ge(s_x[0], 16)
                front_stats(dve, ch, 0, 0)
                front_norm(dve, 0, 0, range(4))
                front_lo(dve, 0, 0)
                ch.commit()
                for g in range(1, NG):
                    dve.wait_ge(s_x[g], 16)

                def evac(it, t):
                    q, kv = Hb[2 * t % 4], Hb[(2 * t + 1) % 4]
                    dve.wait_ge(s.qkv.h, s.qkv.done(it, 2 * t))
                    if t % 2 == 0 and False:
                        pass
                    dve.tensor_tensor(qk[:, t, 0:512], q[:, :], bq[:, 0:512], ALU.add)
                    dve.wait_ge(s.qkv.h, s.qkv.done(it, 2 * t + 1))
                    dve.tensor_tensor(qk[:, t, 512:640], kv[:, 0:128], bq[:, 512:640], ALU.add)
                    dve.tensor_tensor(vaug[:, t, :, 0:HD], kv[:, 128:256].rearrange("p (g d) -> p g d", g=NKV),
                                      bq[:, 640:768].rearrange("p (g d) -> p g d", g=NKV),
                                      ALU.add).then_inc(s.qkv_free.h, 1)

                def rope(it, t):
                    z = qk[:, t, :].rearrange("p (h d) -> p h d", d=HD)
                    r = rtmp[:, :].rearrange("p (h d) -> p h d", d=HD)
                    n, hf = 640 // HD, HD // 2
                    def table(a):
                        return a[:, t % 2, :].unsqueeze(1).broadcast_to([P, n, a.shape[2]])
                    dve.wait_ge(s.qkv_free.h, s.qkv_free.done(it, t))
                    dve.wait_ge(s.rope.h, s.rope.free(it, t, 1))
                    dve.tensor_tensor(r[:, :, 0:hf], z[:, :, hf:HD], table(nsin_t), ALU.mult)
                    ch.link(dve.tensor_tensor(r[:, :, hf:HD], z[:, :, 0:hf], table(sin_t), ALU.mult))
                    ch.link(dve.tensor_tensor(z, z, table(cos_t), ALU.mult))
                    dve.tensor_tensor(z, z, r, ALU.add).then_inc(s.rope.h, 1)

                def maxima(it, i):
                    for ab in range(2):
                        for n, (qt, j0, nj) in enumerate(((0, 0, 4), (1, 0, 2), (1, 2, 2))):
                            m = 6 * i + 3 * ab + n
                            dve.wait_ge(s.sq.h, s.sq.done(it, m))
                            c = 4 * ab + j0
                            dve.tensor_reduce(mx[:, i % 2, qt, c:c + nj],
                                              ring_bank("q", m)[:, :].rearrange("p (j k) -> p j k", j=nj),
                                              AX_X, ALU.max).then_inc(s.red.h, 1)

                def max_parts(it, i):
                    m = mp[:, i % 2, :, :]
                    dve.wait_ge(s.red.h, s.red.done(it, 6 * i + 5))
                    ch.link(dve.tensor_copy(m[:, :, 0:8], mx[:, i % 2, :, :]))
                    dve.tensor_tensor(m[:, :, 8:16], mx[:, i % 2, :, :], m[:, :, 0:8], ALU.subtract).then_inc(s.mp.h, 1)

                def max_rows(it, i):
                    dve.wait_ge(s.mt.h, s.mt.done(it, i))
                    for qt in range(2):
                        ins = dve.tensor_tensor(
                            RR[:, i % 2, qt, :].rearrange("p (j q) -> p j q", j=QPK),
                            mT[:, qt * P:(qt + 1) * P].unsqueeze(1).broadcast_to([P, QPK, P]),
                            headsel.unsqueeze(2).broadcast_to([P, QPK, P]), ALU.mult)
                    ins.then_inc(s.rr.h, 1)

                def normalise(it, i):
                    p = i % NPAIR
                    v = PVb[:, 0:272].rearrange("p (t g d) -> p t g d", t=2, d=HD + 1)
                    dve.wait_ge(s.pv.h, s.pv.done(it, 2 * i + 1))
                    if i % NPAIR == 0:
                        if i:
                            dve.wait_ge(s.ct.h, s.ct.done(it, 1))
                    rd = rden[:, :].rearrange("p (t g) -> p t g", t=2)
                    ch.link(dve.reciprocal(rd, v[:, :, :, HD]))
                    for t in range(2):
                        ins = dve.tensor_tensor(
                            ctx[:, t, p * 128:(p + 1) * 128].rearrange("p (g d) -> p g d", d=HD), v[:, t, :, 0:HD],
                            rd[:, t, :].unsqueeze(2).broadcast_to([P, 8, HD]), ALU.mult)
                    ins.then_inc(s.nrm.h, 1)

                def ctx_lo(it, b):
                    for qt in range(2):
                        dve.wait_ge(s.chi.h, s.chi.done(it, 2 * b + qt))
                        dve.tensor_tensor(ctxT[:, 1, :, :].rearrange("p c q -> p (c q)"), Ob[qt][:, :],
                                          ctxT[:, 0, :, :].rearrange("p c q -> p (c q)").bitcast(F32),
                                          ALU.subtract).then_inc(s.clo.h, 1)

                def take(it, b):
                    for qt in range(2):
                        n = 2 * b + qt
                        dve.wait_ge(s.o_ready.h, s.o_ready.done(it, n))
                        dve.wait_ge(s.xupd.h, s.xupd.free(it, n, 2))
                        ch.link(dve.tensor_tensor(zA[:, qt, :], Ob[qt][:, :], bd[:, :], ALU.add))
                        dve.sem_inc(s.o_free.h, 1)
                    back_stats(dve, ch, s, it, [2 * b, 2 * b + 1], b, lambda t: zA[:, t % 2, :])
                    back_norm(dve, s, it, [2 * b, 2 * b + 1], b, lambda t: zA[:, t % 2, :], lambda t: zA[:, t % 2, :])

                def body(it, last):
                    ch.begin(it, last, DVE_CHAIN_ATTN)
                    fph, fit = nxt(0, it, last)
                    front_stats(dve, ch, fph, fit)
                    front_norm(dve, fph, fit, (0, 1))
                    for t in range(TG):
                        evac(it, t)
                        if t < 2:
                            rope(it, t)
                    front_norm(dve, fph, fit, (2, 3))
                    front_lo(dve, fph, fit)
                    for t in (2, 3):
                        rope(it, t)
                    maxima(it, 0)
                    max_parts(it, 0)
                    for i in range(STEPS):
                        if i + 1 < STEPS:
                            maxima(it, i + 1)
                        if i >= 1 and i != NPAIR:
                            normalise(it, i - 1)
                        max_rows(it, i)
                        if i + 1 < STEPS:
                            max_parts(it, i + 1)
                        if i == NPAIR - 1:
                            normalise(it, i)
                            ctx_lo(it, 0)
                            take(it, 0)
                    normalise(it, STEPS - 1)
                    ctx_lo(it, 1)
                    take(it, 1)
                    ch.end(last)

                groups(dve, body)

            def pool_attention(pool, ch):
                ch.link(pool.memset(mhalf[:, :], -0.5))
                ch.link(pool.memset(qst[:, :, :, :, :, :].bitcast(F32), 0.0))
                pool.memset(kst[:, :, :, :, :].bitcast(F32), 0.0).then_inc(s_init, 1)
                for c in credits:
                    pool.sem_inc(c.h, c.credit)
                pool.sem_inc(s_xntr, 2)
                pool.wait_ge(s_init, 2)
                front_rstd(pool, ch, 0, 0)
                w_split(pool, ch, 0, 0)
                ch.commit()

                def stacks(it, i):
                    b, p = i // NPAIR, i % NPAIR
                    pool.wait_ge(s.rope.h, s.rope.done(it, 2 * b + 1))
                    pool.wait_ge(s.tr.h, s.tr.free(it, i, 2))
                    for t in range(2):
                        lone(pool)
                        zq = qk[:, 2 * b + t, 128 * p:128 * p + 128]
                        zk = qk[:, 2 * b + t, 512 + 32 * p:544 + 32 * p].rearrange("p (a d) -> p a d", a=2)
                        kk = kst[:, i % 2, t, :, :]
                        for ab in range(2):
                            z = zq[:, 64 * ab:64 * ab + 64].rearrange("p (j d) -> p j d", j=QPK)
                            q = qst[:, i % 2, t, :, ab, :]
                            pool.tensor_copy(q[:, :, 0:16], z)
                            pool.tensor_copy(q[:, :, 16:32], z)
                        pool.tensor_copy(kk[:, :, 0:16], zk)
                        ch.link(pool.tensor_copy(kk[:, :, 32:48], zk))
                        for ab in range(2):
                            z = zq[:, 64 * ab:64 * ab + 64].rearrange("p (j d) -> p j d", j=QPK)
                            q = qst[:, i % 2, t, :, ab, :]
                            pool.tensor_tensor(q[:, :, 32:48], z, q[:, :, 0:16].bitcast(F32), ALU.subtract)
                        ins = pool.tensor_tensor(kk[:, :, 16:32], zk, kk[:, :, 0:16].bitcast(F32), ALU.subtract)
                        if t == 0:
                            ch.link(ins)
                    ins.then_inc(s.stack.h, 1)

                def body(it, last):
                    ch.begin(it, last, POOL_CHAIN_ATTN)
                    front_rstd(pool, ch, *nxt(0, it, last))
                    stacks(it, 0)
                    stacks(it, 1)
                    for i in range(STEPS):
                        if i + 2 < STEPS:
                            stacks(it, i + 2)
                        if not last and 2 <= i < 5:
                            w_split(pool, ch, 1, it, [i - 2])
                        if i == NPAIR:
                            back_rstd(pool, ch, s, it, [0, 1], 0)
                            back_update(pool, s, it, [0, 1], lambda t: zA[:, t % 2, :])
                    back_rstd(pool, ch, s, it, [2, 3], 1)
                    back_update(pool, s, it, [2, 3], lambda t: zA[:, t % 2, :])
                    ch.end(last)

                groups(pool, body)

            attn = (bq, bd, pe_attention, act_attention, dve_attention, pool_attention)

        Y = sb(top, "y_taylor_glu", [P, NG * TG, H], F32)
        z4 = sb(top, "z", [P, TG, H], F32)
        sg = sb(top, "silu_gate", [P, 2, H], F32)
        hf = sb(top, "h_full", [P, 2, H], F32)
        hh = sb(top, "h_hi", [P, 2, H], F32R)
        hl = sb(top, "h_lo", [P, 2, H], F32R)

        def z_of(s, it):
            return (lambda t: Y[:, it * TG + t, :]) if s.name == "glu_c" else (lambda t: z4[:, t, :])

        def phase_start(eng, ph, what):
            prev = phs[ph - 1]
            if what == "pe":
                sig = prev.o_free
                eng.wait_ge(sig.h, sig.done(NG - 1, 3))
            if what in ("act", "dve", "pool") and ph == 1:
                eng.wait_ge(prev.xupd.h, prev.xupd.done(NG - 1, 3))
                eng.wait_ge(prev.pe_end, 1)

        def pe_down(pe, s, it, f, nf, chunk, rows=P, opens=True):
            pe.wait_ge(s.hlo.h, s.hlo.done(it, f))
            for t in range(TG):
                if f == 0 and opens:
                    pe.wait_ge(s.o_free.h, s.o_free.free(it, t, 4))
                for n, (a, x) in enumerate(PASSES):
                    h = (hh, hl)[x]
                    ins = pe.matmul(Ob[t][:, :], h[0:rows, f % 2, t * P:(t + 1) * P], s.W[0:rows, chunk, a, :],
                                    start=opens and f == 0 and n == 0, stop=f == nf - 1 and n == 2)
                if f == nf - 1:
                    ins.then_inc(s.o_ready.h, 1)
            if f < nf - 1:
                ins.then_inc(s.hused.h, 1)
            else:
                pe.wait_ge(s.o_ready.h, s.o_ready.done(it, 3))
                pe.sem_inc(s.hused.h, 1)

        def act_split(act, s, it, f, src, dst):
            act.wait_ge(s.hf.h, s.hf.done(it, f))
            act.wait_ge(s.hused.h, s.hused.free(it, f, 2))
            act.activation(dst, src, ACT.Copy).then_inc(s.hhi.h, 1)

        def dve_split(dve, s, it, f, src, hi, dst):
            dve.wait_ge(s.hhi.h, s.hhi.done(it, f))
            dve.tensor_tensor(dst, src, hi.bitcast(F32), ALU.subtract).then_inc(s.hlo.h, 1)

        def dve_back(dve, ch, s, it):
            z = z_of(s, it)
            for t in range(TG):
                dve.wait_ge(s.o_ready.h, s.o_ready.done(it, t))
                if s.name in ("glu_a", "glu_b", "glu_c"):
                    y = Y[:, it * TG + t, :]
                    ins = dve.tensor_tensor(y, y, Ob[t][:, :], ALU.add)
                elif s.name == "glu_d":
                    dve.wait_ge(s.xupd.h, s.xupd.free(it, t, 4))
                    ins = dve.tensor_tensor(z(t), Ob[t][:, :], bias3[:, :], ALU.add)
                elif s.name == "taylor":
                    ins = dve.tensor_copy(Y[:, it * TG + t, :], Ob[t][:, :])
                else:
                    dve.wait_ge(s.xupd.h, s.xupd.free(it, t, 4))
                    ins = dve.tensor_copy(z(t), Ob[t][:, :])
                ins.then_inc(s.o_free.h, 1)
            if s.updates:
                dve.wait_ge(s.o_free.h, s.o_free.done(it, 3))
                back_stats(dve, ch, s, it, range(TG), 0, z)
                back_norm(dve, s, it, range(TG), 0, z, z)

        def pool_back(pool, ch, s, it):
            if s.updates:
                back_rstd(pool, ch, s, it, range(TG), 0)
                back_update(pool, s, it, range(TG), z_of(s, it))

        def pool_phase(pool, ch, ph):
            s = phs[ph]
            phase_start(pool, ph, "pool")
            end = ph == len(PHASES) - 1

            def body(it, last):
                ch.begin(it, last, 1 + (0 if end else wper(ph + 1)) + int(s.updates))
                if not (end and last):
                    front_rstd(pool, ch, *nxt(ph, it, last))
                if not last and not end:
                    if not isinstance(it, int):
                        pool.wait_ge(phs[ph - 1].pe_end, 1)
                    w_split(pool, ch, ph + 1, it)
                pool_back(pool, ch, s, it)
                ch.end(last)

            groups(pool, body)

        def pe_glu(pe, ph):
            s = phs[ph]
            nf = s.nf
            end = ph == len(PHASES) - 1
            weights_wait(pe, ph)
            phase_start(pe, ph, "pe")

            def body(it, last):
                def up(f):
                    for n in range(2):
                        if f == 0 and n == 0:
                            pe.wait_ge(fr[ph]["lo"].h, fr[ph]["lo"].done(it, 3))
                        if f >= 2 and n == 0:
                            pe.wait_ge(s.hf.h, s.hf.done(it, f - 2))
                        features(pe, Hb[(2 * f + n) % 4],
                                 lambda k: tuple(s.W[:, 3 * f + n, a, k * P:(k + 1) * P] for a in range(2))
                                 ).then_inc(s.in_ready.h, 1)

                up(0)
                for f in range(1, nf):
                    up(f)
                    pe_down(pe, s, it, f - 1, nf, 3 * (f - 1) + 2)
                if not (end and last):
                    pe.wait_ge(s.hf.h, s.hf.done(it, nf - 1))
                    front_transpose(pe, *nxt(ph, it, last))
                pe_down(pe, s, it, nf - 1, nf, 3 * (nf - 1) + 2)

            groups(pe, body)
            pe.sem_inc(s.pe_end, 1)

        def act_glu(act, ph):
            s = phs[ph]
            nf = s.nf
            bias = b12 if s.name == "glu_d" else zero8

            def body(it, last):
                for f in range(nf):
                    act.wait_ge(s.in_ready.h, s.in_ready.done(it, 2 * f))
                    act.wait_ge(s.hf.h, s.hf.free(it, f, 2))
                    act.activation(sg[:, f % 2, :], Hb[(2 * f) % 4][:, :], ACT.Silu,
                                   bias=bias[:, f:f + 1]).then_inc(s.sg.h, 1)
                    act_split(act, s, it, f, hf[:, f % 2, :], hh[:, f % 2, :])
                if not (ph == len(PHASES) - 1 and last):
                    front_hi(act, *nxt(ph, it, last))

            groups(act, body)

        def dve_glu(dve, ch, ph):
            s = phs[ph]
            nf = s.nf
            end = ph == len(PHASES) - 1
            bias = b12 if s.name == "glu_d" else zero8

            def body(it, last):
                ch.begin(it, last, TG + (TG if s.updates else 0))
                fph, fit = nxt(ph, it, last)
                go = not (end and last)
                if go:
                    front_stats(dve, ch, fph, fit)
                    front_norm(dve, fph, fit, (0, 1))
                for f in range(nf):
                    dve.wait_ge(s.in_ready.h, s.in_ready.done(it, 2 * f + 1))
                    dve.wait_ge(s.sg.h, s.sg.done(it, f))
                    dve.scalar_tensor_tensor(out=hf[:, f % 2, :], in0=Hb[(2 * f + 1) % 4][:, :],
                                             scalar=bias[:, 4 + f:5 + f], in1=sg[:, f % 2, :],
                                             op0=ALU.add, op1=ALU.mult).then_inc(s.hf.h, 1)
                    dve_split(dve, s, it, f, hf[:, f % 2, :], hh[:, f % 2, :], hl[:, f % 2, :])
                if go:
                    front_norm(dve, fph, fit, (2, 3))
                    front_lo(dve, fph, fit)
                dve_back(dve, ch, s, it)
                ch.end(last)

            groups(dve, body)

        smallm = sb(top, "route_small", [P, 8, TG], F32)
        m8 = sb(top, "route_max8", [P, TG, 8], F32)
        i8 = sb(top, "route_index8", [P, TG, 8], U32)
        idx = sb(top, "route_index", [P, TG, 2], F32)
        gate = sb(top, "route_gate", [P, TG, 2, NE], F32)
        hs = z4

        def pe_moe(pe):
            s = phs[1]
            weights_wait(pe, 1)
            phase_start(pe, 1, "pe")

            def body(it, last):
                pe.wait_ge(fr[1]["lo"].h, fr[1]["lo"].done(it, 3))
                for t in range(TG):
                    tokens_by_weights(pe, Hb[t], 256, t, lambda k: tuple(
                        s.W[:, 4 + k // 2, a, (k % 2) * 256:(k % 2) * 256 + 256] for a in range(2))
                    ).then_inc(s.in_ready.h, 1)
                for t in range(TG):
                    pe.wait_ge(s.o_free.h, s.o_free.free(it, t, 4))
                    tokens_by_weights(pe, Ob[t], 512, t, lambda k: (s.W[:, k, 0, :], s.W[:, k, 1, :]), final=False)
                pe.wait_ge(s.hs.h, s.hs.done(it, 3))
                fph, fit = nxt(1, it, last)
                front_transpose(pe, fph, fit)
                pe.wait_ge(fr[fph]["lo"].h, fr[fph]["lo"].done(fit, 1))
                for t in range(TG):
                    for j in range(2):
                        ins = pe.transpose(Hb[j][0:LH, t * P:(t + 1) * P], hs[:, t, j * LH:(j + 1) * LH], identf)
                ins.then_inc(s.ht.h, 1)
                for f in range(2):
                    pe_down(pe, s, it, f, 2, 6 + f, rows=LH, opens=False)

            groups(pe, body)
            pe.sem_inc(s.pe_end, 1)

        def act_moe(act):
            s = phs[1]
            phase_start(act, 1, "act")
            act.dma_start(bias3[:, :], biases[:, 1280:1792]).then_inc(s_const, 16)

            def body(it, last):
                act.wait_ge(s.rt.h, s.rt.done(it, 0))
                act.activation(smallm[:, 1, :], smallm[:, 0, :], ACT.Exp).then_inc(s.re.h, 1)
                front_hi(act, *nxt(1, it, last))
                act.wait_ge(s.ht.h, s.ht.done(it, 0))
                for f in range(2):
                    act.wait_ge(s.hused.h, s.hused.free(it, f, 2))
                    act.activation(hh[0:LH, f, :], Hb[f][0:LH, :], ACT.Copy).then_inc(s.hhi.h, 1)

            groups(act, body)

        def dve_moe(dve, ch):
            s = phs[1]
            phase_start(dve, 1, "dve")

            def body(it, last):
                ch.begin(it, last, DVE_CHAIN_MOE)
                fph, fit = nxt(1, it, last)
                for t in range(TG):
                    lg = Hb[t][:, LR:LR + NE]
                    dve.wait_ge(s.in_ready.h, s.in_ready.done(it, t))
                    lone(dve)
                    ch.link(dve.max(m8[:, t, :], lg))
                    lone(dve)
                    dve.max_index(i8[:, t, :], m8[:, t, :], lg)
                ch.link(dve.tensor_tensor(smallm[:, 0, :], m8[:, :, 1], m8[:, :, 0], ALU.subtract))
                dve.sem_inc(s.rt.h, 1)
                ch.link(dve.tensor_copy(idx[:, :, :], i8[:, :, 0:2]))
                dve.wait_ge(s.re.h, s.re.done(it, 0))
                ch.link(dve.tensor_scalar(smallm[:, 2, :], smallm[:, 1, :], 1.0, None, ALU.add))
                ch.link(dve.reciprocal(smallm[:, 3, :], smallm[:, 2, :]))
                ch.link(dve.tensor_scalar(smallm[:, 4, :], smallm[:, 3, :], 2.0, None, ALU.mult))
                ch.link(dve.tensor_tensor(smallm[:, 5, :], smallm[:, 4, :], smallm[:, 1, :], ALU.mult))
                for t in range(TG):
                    for c in range(2):
                        ins = dve.tensor_scalar(gate[:, t, c, :], iota, idx[:, t, c:c + 1], smallm[:, 4 + c, t:t + 1],
                                                ALU.is_equal, ALU.mult)
                ch.link(ins)
                ch.link(dve.tensor_tensor(gate[:, :, 0, :], gate[:, :, 0, :], gate[:, :, 1, :], ALU.add))
                for t in range(TG):
                    dve.wait_ge(s.xupd.h, s.xupd.free(it, t, 4))
                    dve.tensor_tensor(hs[:, t, 0:LR].rearrange("p (e r) -> p e r", r=RANK),
                                      Hb[t][:, 0:LR].rearrange("p (e r) -> p e r", r=RANK),
                                      gate[:, t, 0, :].unsqueeze(2).broadcast_to([P, NE, RANK]),
                                      ALU.mult).then_inc(s.hs.h, 1)
                front_stats(dve, ch, fph, fit)
                front_norm(dve, fph, fit, range(4))
                front_lo(dve, fph, fit)
                for f in range(2):
                    dve.wait_ge(s.hhi.h, s.hhi.done(it, f))
                    dve.tensor_tensor(hl[0:LH, f, :], Hb[f][0:LH, :], hh[0:LH, f, :].bitcast(F32),
                                      ALU.subtract).then_inc(s.hlo.h, 1)
                dve_back(dve, ch, s, it)
                ch.end(last)

            groups(dve, body)

        dl = sb(top, "delta", [P, 2, H], F32)

        def pe_taylor(pe):
            s = phs[2]
            weights_wait(pe, 2)
            phase_start(pe, 2, "pe")

            def body(it, last):
                for n in range(2):
                    if n == 0:
                        pe.wait_ge(fr[2]["lo"].h, fr[2]["lo"].done(it, 3))
                        if True:
                            pe.wait_ge(phs[1].hlo.h, phs[1].hlo.done(NG - 1, 1))
                    features(pe, Hb[n], lambda k: tuple(
                        s.W[:, k // 2, a, (k % 2) * 256 + n * P:(k % 2) * 256 + (n + 1) * P] for a in range(2))
                    ).then_inc(s.in_ready.h, 1)
                pe.wait_ge(s.sg.h, s.sg.done(it, 0))
                front_transpose(pe, *nxt(2, it, last))
                for f in range(s.nf):
                    pe_down(pe, s, it, f, s.nf, 2 + f)

            groups(pe, body)
            pe.sem_inc(s.pe_end, 1)

        def act_taylor(act, ch):
            s = phs[2]

            def body(it, last):
                for f in range(s.nf):
                    if f == 1:
                        front_hi(act, *nxt(2, it, last))
                    act_split(act, s, it, f, hf[:, f % 2, :], hh[:, f % 2, :])

            groups(act, body)

        def dve_taylor(dve, ch):
            s = phs[2]

            def body(it, last):
                ch.begin(it, last, DVE_CHAIN_TAYLOR)
                fph, fit = nxt(2, it, last)
                front_stats(dve, ch, fph, fit)
                front_norm(dve, fph, fit, (0, 1))
                dve.wait_ge(s.in_ready.h, s.in_ready.done(it, 0))
                dve.tensor_copy(hf[:, 0, :], Hb[0][:, :]).then_inc(s.hf.h, 1)
                dve.wait_ge(s.in_ready.h, s.in_ready.done(it, 1))
                ch.link(dve.tensor_scalar(dl[:, 0, :], Hb[1][:, :], lp, None, ALU.subtract))
                dve.sem_inc(s.sg.h, 1)
                ch.link(dve.scalar_tensor_tensor(out=dl[:, 1, :], in0=dl[:, 0, :], scalar=-1.0, in1=dl[:, 0, :],
                                                 op0=ALU.mult, op1=ALU.max))
                ch.link(dve.scalar_tensor_tensor(out=dl[:, 1, :], in0=dl[:, 1, :], scalar=THD, in1=dl[:, 0, :],
                                                 op0=ALU.is_le, op1=ALU.mult))
                dve_split(dve, s, it, 0, hf[:, 0, :], hh[:, 0, :], hl[:, 0, :])
                for f in range(1, s.nf):
                    dve.wait_ge(s.hf.h, s.hf.done(it, f - 1))
                    dve.scalar_tensor_tensor(out=hf[:, f % 2, :], in0=hf[:, (f - 1) % 2, :],
                                             scalar=cfac[:, f - 1:f], in1=dl[:, 1 if f == 5 else 0, :],
                                             op0=ALU.mult, op1=ALU.mult).then_inc(s.hf.h, 1)
                    if f == 1:
                        front_norm(dve, fph, fit, (2, 3))
                        front_lo(dve, fph, fit)
                    dve_split(dve, s, it, f, hf[:, f % 2, :], hh[:, f % 2, :], hl[:, f % 2, :])
                dve_back(dve, ch, s, it)
                ch.end(last)

            groups(dve, body)

        bias3 = sb(top, "bias_w3", [P, H], F32)
        bq, bd, pe_attention, act_attention, dve_attention, pool_attention = attn

        DVE_CHAIN_ATTN, DVE_CHAIN_MOE, DVE_CHAIN_TAYLOR, POOL_CHAIN_ATTN = 36, 20, 7, 30

        block = top.enter_context(nc.Block())

        @block.sync
        def _(sp):
            xr = x_in.rearrange("(g t p) n -> g p t n", g=NG, p=P)
            outr = out.rearrange("(g t p) n -> g p t n", g=NG, p=P)
            sp.dma_start(X[:, 0:TG, :], xr[0]).then_inc(s_x[0], 16)
            sp.dma_start(cf[:, :], cons_f).then_inc(s_const, 16)
            sp.dma_start(cb[:, :], cons_b).then_inc(s_const, 16)
            sp.dma_start(bq[:, :], biases[:, 0:768]).then_inc(s_const, 16)
            sp.dma_start(bd[:, :], biases[:, 768:1280]).then_inc(s_const, 16)
            w_load(sp, 0, 0)
            for ph in range(1, len(PHASES)):
                with sp.Fori(0, 3) as it:
                    w_load(sp, ph, it)
            s = phs[-1]
            for g in range(NG):
                sp.wait_ge(s.xupd.h, s.xupd.done(g, 3))
                sp.dma_start(outr[g], X[:, g * TG:(g + 1) * TG, :]).then_inc(s_out, 16)
            sp.wait_ge(s_out, 16 * NG)

        @block.gpsimd
        def _(pool):
            ch = Chain(pool, chain_pool)
            pool_attention(pool, ch)
            for ph in range(1, len(PHASES)):
                pool_phase(pool, ch, ph)

        @block.scalar
        def _(act):
            xr = x_in.rearrange("(g t p) n -> g p t n", g=NG, p=P)
            for g in range(1, NG):
                act.dma_start(X[:, g * TG:(g + 1) * TG, :], xr[g]).then_inc(s_x[g], 16)
            act.wait_ge(s_const, 16 * 4)
            act.wait_ge(chain_act, 1)
            act.activation(cfac[:, 0:NORD], cfac[:, 0:NORD], ACT.Exp).then_inc(chain_act, 1)
            act_attention(act)
            act_moe(act)
            act_taylor(act, None)
            for ph in range(3, 7):
                act_glu(act, ph)

        @block.vector
        def _(dve):
            ch = Chain(dve, chain_dve)
            dve.wait_ge(s_const, 16 * 4)
            dve.tensor_scalar(cfac[:, 0:1], disc[:, 0:1], -1.0, None, ALU.mult)
            dve.tensor_tensor(cfac[:, 1:NORD], disc[:, 0:NORD - 1], disc[:, 1:NORD], ALU.subtract).then_inc(chain_act, 1)
            dve_attention(dve, ch)
            dve_moe(dve, ch)
            dve.wait_ge(chain_act, 2)
            dve_taylor(dve, ch)
            dve.wait_ge(s_const, 16 * 5)
            for ph in range(3, 7):
                dve_glu(dve, ch, ph)

        @block.tensor
        def _(pe):
            pe_attention(pe)
            pe_moe(pe)
            pe_taylor(pe)
            for ph in range(3, 7):
                pe_glu(pe, ph)


def kernel(**inputs):
    import numpy as np
    import ml_dtypes
    import concourse.bacc as bacc
    from concourse.bass_utils import run_bass_kernel_spmd as run

    a = {k: np.asarray(v) for k, v in inputs.items()}
    x = a["L0_attn_hidden_states"]
    B, S, _ = x.shape

    def k_tiles(w, cols):
        wt = w.T
        full = np.zeros((wt.shape[0], cols), np.float32)
        full[:, :wt.shape[1]] = wt
        return full.reshape(-1, P, cols)

    wq = a["L0_attn_w_qkv"].reshape(NKV, QPK + 2, HD, H)
    bqkv = a["L0_attn_b_qkv"].reshape(NKV, QPK + 2, HD)
    q_w = k_tiles(wq[:, :QPK].reshape(-1, H), 512)
    kv_w = k_tiles(np.concatenate([wq[:, QPK].reshape(-1, H), wq[:, QPK + 1].reshape(-1, H)]), 256)
    b_row = np.concatenate([bqkv[:, :QPK].reshape(-1), bqkv[:, QPK].reshape(-1), bqkv[:, QPK + 1].reshape(-1),
                            a["L0_attn_b_dense"], a["L1_ffn_b3"]])

    def two(t):
        return [np.concatenate([t[2 * i], t[2 * i + 1]], axis=1) for i in range(2)]

    def glu(w1, w2, w3, tiles):
        out = []
        for f in tiles:
            for w in (w1, w2):
                wt = np.zeros((P, H), np.float32)
                part = w[f * P:(f + 1) * P]
                wt[:part.shape[0]] = part
                out.append(wt.T.reshape(KT, P, P).transpose(1, 0, 2).reshape(P, H))
            d = np.zeros((P, H), np.float32)
            part = w3.T[f * P:(f + 1) * P]
            d[:part.shape[0]] = part
            out.append(d)
        return out

    zero = np.zeros((P, H), np.float32)
    chunks = list(q_w) + two(kv_w) + list(k_tiles(a["L0_attn_w_dense"], 512))
    la = a["L0_ffn_lora_A"].reshape(LR, H)
    chunks += list(k_tiles(a["L0_ffn_base_W"], 512)) + two(k_tiles(np.concatenate([la, a["L0_ffn_gate_W"]]), 256))
    lb = a["L0_ffn_lora_B"].transpose(0, 2, 1).reshape(2, LH, H)
    for j in range(2):
        c = zero.copy()
        c[:LH] = lb[j]
        chunks.append(c)
    chunks.append(zero)
    chunks += two(k_tiles(np.concatenate([a["L1_attn_up_w"], a["L1_attn_gate_w"]]), 256))
    chunks.append(np.ascontiguousarray(a["L1_attn_local_approx_output"].T))
    chunks += list(a["L1_attn_fuse_weight"].transpose(2, 1, 0))
    gw, uw, dw = a["L1_attn_ffn_gate_w"], a["L1_attn_ffn_up_w"], a["L1_attn_ffn_down_w"]
    for tiles in (range(0, 3), range(3, 7), range(7, 10)):
        chunks += glu(gw, uw, dw, tiles)
    w12 = a["L1_ffn_w12"]
    chunks += glu(w12[:H], w12[H:], a["L1_ffn_w3"], range(4))
    assert len(chunks) == CHUNK0[-1]

    inv = (1.0 / np.float32(1000000.0) ** (np.arange(0, HD, 2, dtype=np.float32) / np.float32(HD))).astype(np.float32)
    fr = np.outer(np.arange(S, dtype=np.float32), inv).astype(np.float32)
    cos, sin = np.cos(fr), np.sin(fr)
    cf = np.zeros((P, 247), np.float32)
    cf[:, 0:128] = np.eye(P)
    cf[:, 128:160] = np.concatenate([cos, cos], 1).reshape(2, P, HD).transpose(1, 0, 2).reshape(P, -1)
    cf[:, 160:176] = sin.reshape(2, P, HD // 2).transpose(1, 0, 2).reshape(P, -1)
    cf[:, 176:192] = -cf[:, 160:176]
    cf[:, 192:192 + NE] = np.arange(NE)
    for r in range(16):
        cf[r, 220 + r % 4] = 1.0
    cf[:, 224] = a["L1_attn_local_point"]
    cf[:, 225:231] = a["L1_attn_discount_factor"]
    cf[:, 231:239] = a["L1_ffn_b12"].reshape(8, P).T
    bf = ml_dtypes.bfloat16
    cb = np.zeros((P, 640), np.float32)
    cb[:, 0:128] = np.eye(P)
    up = np.triu(np.ones((P, P)), 1)
    cb[:, 128:256] = up * MASKED
    cb[:, 256:384] = up.T * MASKED
    for r in range(16):
        cb[r, 384 + 128 * ((r % 8) // 4):512 + 128 * ((r % 8) // 4)] = -1.0
    cb = cb.astype(bf)

    arrays = {
        "x": np.ascontiguousarray(x.reshape(B * S, H)),
        "w": np.ascontiguousarray(np.stack(chunks)),
        "cf": cf, "cb": cb,
        "bias": np.ascontiguousarray(np.broadcast_to(b_row, (P, b_row.size))),
    }
    nc = bacc.Bacc("TRN2", target_bir_lowering=False, num_devices=1)
    aps = [nc.dram_tensor(n, v.shape, mybir.dt.from_np(v.dtype), kind="ExternalInput").ap() for n, v in arrays.items()]
    out = nc.dram_tensor("out", [B * S, H], F32, kind="ExternalOutput").ap()
    build(nc, *aps, out)
    r = run(nc, [arrays], core_ids=[0])
    return r.results[0]["out"].reshape(B, S, H)
```

```python
from contextlib import ExitStack

import concourse.bass as bass
from concourse import mybir

P = 128
F32 = mybir.dt.float32
F32R = mybir.dt.float32r
BF16 = mybir.dt.bfloat16
FP16 = mybir.dt.float16
U32 = mybir.dt.uint32
ALU = mybir.AluOpType
ACT = mybir.ActivationFunctionType
AX_X = mybir.AxisListType.X

H = 512
KT = H // P
NG = 4
TG = 4
NKV, QPK, HD = 8, 4, 16
NPAIR = NKV // 2
STEPS = 2 * NPAIR
NE, RANK = 28, 8
LR = NE * RANK
LH = LR // 2
NORD = 6
THD = 2.5
EPS = 1e-5
MASKED = -1e30
SHIFT = 96.0
VC = 3 * HD + 1

PHASES = [("attn", 10, 0), ("moe", 9, 1), ("taylor", 9, 0), ("glu_a", 9, 1), ("glu_b", 12, 0), ("glu_c", 9, 1),
          ("glu_d", 12, 0)]
CHUNK0 = [sum(n for _, n, _ in PHASES[:i]) for i in range(len(PHASES) + 1)]


class Signal:

    def __init__(self, handle, per, credit=0, base=0):
        self.h, self.per, self.credit, self.base = handle, per, credit, base

    def done(self, it, n):
        return it * self.per + (self.base + self.credit + n + 1)

    def free(self, it, n, bufs):
        assert bufs <= self.credit
        return it * self.per + (self.base + self.credit + n + 1 - bufs)


def lone(eng):
    eng.nop(nofuse=True)


class Chain:

    def __init__(self, eng, handle):
        self.eng, self.h, self.total, self.it, self.per, self.n = eng, handle, 0, 0, 0, 0

    def link(self, ins):
        self.n += 1
        ins.then_inc(self.h, 1)
        self.eng.wait_ge(self.h, self.it * self.per + (self.total + self.n))

    def commit(self):
        self.total, self.n = self.total + self.n, 0

    def begin(self, it, last, per):
        if last:
            self.total, self.it, self.per = self.total + (NG - 1) * per, 0, 0
        else:
            self.it, self.per = it, per

    def end(self, last):
        assert last or self.n == self.per, ("chained in one iteration:", self.n, "expected", self.per)
        self.total, self.n = self.total + (self.n if last else 0), 0


def build(nc, x_in, w_in, cons_f, cons_b, biases, out):
    with ExitStack() as top:
        def sb(stack, name, shape, dt):
            return stack.enter_context(nc.sbuf_tensor(name, shape, dt))

        def sem(name):
            return top.enter_context(nc.semaphore(name))

        def signal(name, per, credit=0, base=0):
            s = Signal(sem(name), per, credit, base)
            if credit:
                credits.append(s)
            return s

        credits = []
        X = sb(top, "x_resident", [P, NG * TG, H], F32)
        W = [sb(top, "weights_even", [P, 12, 2, H], F32R), sb(top, "weights_odd", [P, 9, 2, H], F32R)]
        stage = sb(top, "weight_stage", [P, 2, H], F32)
        xn = sb(top, "x_normed", [P, 2, H], F32)
        xT = sb(top, "xT_hi_lo", [P, 2, KT, H], F32R)
        cf = sb(top, "constants_f32", list(cons_f.shape), F32)
        cb = sb(top, "constants_bf16", list(cons_b.shape), BF16)
        fst = sb(top, "front_stats", [P, 2, 6], F32)
        fmv = sb(top, "front_mean_var", [P, TG, 2], F32)
        frs = sb(top, "front_rstd", [P, 2, TG], F32)
        bst = sb(top, "back_stats", [P, 2, 6], F32)
        bmv = sb(top, "back_mean_var", [P, TG, 2], F32)
        brs = sb(top, "back_rstd", [P, 2, TG], F32)
        mhalf = sb(top, "minus_half", [P, TG], F32)
        zeros = sb(top, "zeros", [P, 2 * P], F32)
        cfac = sb(top, "order_factor", [P, 8], F32)
        banks = [top.enter_context(nc.psum_tensor(f"bank{i}", [P, 512], F32)) for i in range(8)]
        Hb, Ob = banks[:4], banks[4:]

        identf = cf[:, 0:128]
        cos_t = cf[:, 128:160].rearrange("p (t d) -> p t d", t=2)
        sin_t = cf[:, 160:176].rearrange("p (t d) -> p t d", t=2)
        nsin_t = cf[:, 176:192].rearrange("p (t d) -> p t d", t=2)
        iota = cf[:, 192:192 + NE]
        headsel = cf[:, 220:224]
        lp = cf[:, 224:225]
        disc = cf[:, 225:231]
        b12 = cf[:, 231:239]
        zero8 = cf[:, 239:247]
        identb = cb[:, 0:128]
        mask_qk = cb[:, 128:256]
        mask_kq = cb[:, 256:384]
        sel = cb[:, 384:640].rearrange("p (a k) -> p a k", a=2)

        s_x = [sem(f"s_x_loaded{g}") for g in range(NG)]
        s_const = sem("s_const")
        s_init = sem("s_init")
        s_wdma = [sem("s_wdma_even"), sem("s_wdma_odd")]
        s_wsplit = [sem("s_wsplit_even"), sem("s_wsplit_odd")]
        s_out = sem("s_out")
        s_fmv, s_frs = sem("s_front_meanvar"), sem("s_front_rstd")
        s_xn, s_fhi, s_flo = sem("s_xn"), sem("s_front_hi"), sem("s_front_lo")
        s_xntr = sem("s_xn_transposed")
        chain_dve, chain_pool, chain_act = sem("chain_dve"), sem("chain_pool"), sem("chain_act")

        def front_signals(ph):
            b = NG * ph
            return dict(mv=Signal(s_fmv, 1, 0, b), rs=Signal(s_frs, 1, 0, b), xn=Signal(s_xn, 4, 0, 4 * b),
                        tr=Signal(s_xntr, 4, 2, 4 * b), hi=Signal(s_fhi, 4, 0, 4 * b), lo=Signal(s_flo, 4, 0, 4 * b))

        fr = [front_signals(ph) for ph in range(len(PHASES))]

        class Ph:
            pass

        phs = []
        for i, (name, nchunk, wb) in enumerate(PHASES):
            s = Ph()
            s.i, s.name, s.W = i, name, W[wb]
            s.updates = name in ("attn", "moe", "glu_c", "glu_d")
            nf = {"attn": 0, "moe": 2, "taylor": NORD + 1}.get(name, nchunk // 3)
            s.nf = nf
            s.o_ready = signal(f"{name}_o_ready", 4)
            s.o_free = signal(f"{name}_o_free", 4, 4)
            s.bmv = signal(f"{name}_bmv", 2 if name == "attn" else 1)
            s.brs = signal(f"{name}_brs", 2 if name == "attn" else 1)
            s.z_ready = signal(f"{name}_z_ready", 4)
            s.xupd = signal(f"{name}_xupd", 4, 4)
            s.pe_end = sem(f"{name}_pe_end")
            if name == "attn":
                s.qkv = signal("attn_qkv_ready", 8)
                s.qkv_free = signal("attn_qkv_free", 4, 2)
                s.rope = signal("attn_rope", 4, 1)
                s.stack = signal("attn_stack", 16)
                s.tr = signal("attn_stack_transposed", 16, 4)
                s.tev = signal("attn_transposed_kept", 16)
                s.sq = signal("attn_scores_q", 48)
                s.red = signal("attn_reduced", 48)
                s.mp = signal("attn_max_parts", 8)
                s.mt = signal("attn_max_transposed", 8)
                s.rr = signal("attn_max_rows", 8)
                s.st = signal("attn_scores_k", 48)
                s.ex = signal("attn_exp", 48)
                s.pv = signal("attn_pv", 48, 4)
                s.plo = signal("attn_probs_lo", 48, 2)
                s.vp = signal("attn_v_parts", 4)
                s.otaken = signal("attn_out_taken", 4)
                s.nrm = signal("attn_ctx_normed", 8, 1)
                s.ct = signal("attn_ctx_transposed", 4)
                s.chi = signal("attn_ctx_hi", 4)
                s.clo = signal("attn_ctx_lo", 4)
            else:
                s.in_ready = signal(f"{name}_in_ready", {"moe": 4, "taylor": 2}.get(name, 2 * nf))
                s.sg = signal(f"{name}_sg", 1 if name == "taylor" else nf)
                s.hf = signal(f"{name}_hf", nf, 2)
                s.hhi = signal(f"{name}_hhi", nf)
                s.hlo = signal(f"{name}_hlo", nf)
                s.hused = signal(f"{name}_hused", nf, 2)
                if name == "moe":
                    s.rt = signal("moe_route_diff", 1)
                    s.re = signal("moe_route_exp", 1)
                    s.hs = signal("moe_h_scaled", 4)
                    s.ht = signal("moe_h_transposed", 1)
            phs.append(s)

        def x_writer(ph):
            w = [p for p in phs[:ph] if p.updates]
            return w[-1] if w else None

        def wait_x(eng, ph, group, tile):
            w = x_writer(ph)
            if w is not None:
                eng.wait_ge(w.xupd.h, w.xupd.done(group, tile))

        def nxt(ph, it, last):
            return (ph + 1, 0) if last else (ph, it + 1)

        def front_stats(dve, ch, fph, fit):
            for t in range(TG):
                wait_x(dve, fph, fit, t)
                lone(dve)
                ch.link(dve.bn_stats(fst[:, t % 2, :], X[:, fit * TG + t, :]))
                lone(dve)
                ins = dve.bn_aggr(fmv[:, t, :], fst[:, t % 2, :])
            ins.then_inc(fr[fph]["mv"].h, 1)

        def front_norm(dve, fph, fit, tiles):
            f = fr[fph]
            for t in tiles:
                if t == 0:
                    dve.wait_ge(f["rs"].h, f["rs"].done(fit, 0))
                dve.wait_ge(f["tr"].h, f["tr"].free(fit, t, 2))
                dve.tensor_scalar(xn[:, t % 2, :], X[:, fit * TG + t, :], fmv[:, t, 0:1], frs[:, 1, t:t + 1],
                                  ALU.subtract, ALU.mult).then_inc(f["xn"].h, 1)

        def front_rstd(pool, ch, fph, fit):
            f = fr[fph]
            pool.wait_ge(f["mv"].h, f["mv"].done(fit, 0))
            lone(pool)
            ch.link(pool.tensor_scalar(frs[:, 0, :], fmv[:, :, 1], 1.0, EPS, ALU.mult, ALU.add))
            pool.tensor_tensor(frs[:, 1, :], frs[:, 0, :], mhalf[:, :], ALU.pow).then_inc(f["rs"].h, 1)

        def front_transpose(pe, fph, fit):
            f = fr[fph]
            for t in range(TG):
                pe.wait_ge(f["xn"].h, f["xn"].done(fit, t))
                for k in range(KT):
                    ins = pe.transpose(Hb[k][:, t * P:(t + 1) * P], xn[:, t % 2, k * P:(k + 1) * P], identf)
                ins.then_inc(f["tr"].h, 1)

        def front_hi(act, fph, fit):
            f = fr[fph]
            act.wait_ge(f["tr"].h, f["tr"].done(fit, 3))
            for k in range(KT):
                act.activation(xT[:, 0, k, :], Hb[k][:, :], ACT.Copy).then_inc(f["hi"].h, 1)

        def front_lo(dve, fph, fit):
            f = fr[fph]
            for k in range(KT):
                dve.wait_ge(f["hi"].h, f["hi"].done(fit, k))
                dve.tensor_tensor(xT[:, 1, k, :], Hb[k][:, :], xT[:, 0, k, :].bitcast(F32),
                                  ALU.subtract).then_inc(f["lo"].h, 1)

        PASSES = ((0, 0), (0, 1), (1, 0))

        def tokens_by_weights(pe, bank, cols, t, chunk_of, first=True, final=True):
            for k in range(KT):
                w = chunk_of(k)
                for n, (a, b) in enumerate(PASSES):
                    ins = pe.matmul(bank[:, 0:cols], xT[:, b, k, t * P:(t + 1) * P], w[a],
                                    start=first and k == 0 and n == 0, stop=final and k == KT - 1 and n == 2)
            return ins

        def features(pe, bank, chunk_of):
            for k in range(KT):
                w = chunk_of(k)
                for n, (a, b) in enumerate(PASSES):
                    ins = pe.matmul(bank[:, :], w[a], xT[:, b, k, :], start=k == 0 and n == 0,
                                    stop=k == KT - 1 and n == 2)
            return ins

        def weights_wait(pe, ph):
            for s in range(2):
                pe.wait_ge(s_wsplit[s], wcount(ph + 1, s))

        def wper(ph):
            return PHASES[ph][1] if ph == 0 else PHASES[ph][1] // 3

        def wslot(per, s):
            return (per + 1 - s) // 2

        def wcount(ph, s):
            return sum(wslot(wper(p), s) * (1 if p == 0 else 3) for p in range(ph))

        def w_load(sp, ph, it):
            per = wper(ph)
            for j in range(per):
                s, n = j % 2, j // 2
                before = it * wslot(per, s) + (wcount(ph, s) + n)
                if not (ph == 0 and n == 0):
                    sp.wait_ge(s_wsplit[s], before)
                sp.dma_start(stage[:, s, :], w_in[it * per + (CHUNK0[ph] + j)]).then_inc(s_wdma[s], 16)

        def w_split(pool, ch, ph, it, js=None):
            per = wper(ph)
            for j in range(per) if js is None else js:
                s, n = j % 2, j // 2
                now = it * (16 * wslot(per, s)) + 16 * (wcount(ph, s) + n + 1)
                hi, lo = (W[PHASES[ph][2]][:, it * per + j, a, :] for a in range(2))
                pool.wait_ge(s_wdma[s], now)
                lone(pool)
                ch.link(pool.tensor_copy(hi, stage[:, s, :]))
                pool.tensor_tensor(lo, stage[:, s, :], hi.bitcast(F32), ALU.subtract).then_inc(s_wsplit[s], 1)

        def back_stats(dve, ch, s, it, tiles, n, src):
            for t in tiles:
                lone(dve)
                ch.link(dve.bn_stats(bst[:, t % 2, :], src(t)))
                lone(dve)
                ins = dve.bn_aggr(bmv[:, t, :], bst[:, t % 2, :])
            ins.then_inc(s.bmv.h, 1)

        def back_rstd(pool, ch, s, it, tiles, n):
            a, b = tiles[0], tiles[-1] + 1
            pool.wait_ge(s.bmv.h, s.bmv.done(it, n))
            lone(pool)
            ch.link(pool.tensor_scalar(brs[:, 0, a:b], bmv[:, a:b, 1], 1.0, EPS, ALU.mult, ALU.add))
            pool.tensor_tensor(brs[:, 1, a:b], brs[:, 0, a:b], mhalf[:, a:b], ALU.pow).then_inc(s.brs.h, 1)

        def back_norm(dve, s, it, tiles, n, src, dst, frees_o=False):
            dve.wait_ge(s.brs.h, s.brs.done(it, n))
            for t in tiles:
                if frees_o:
                    dve.wait_ge(s.xupd.h, s.xupd.free(it, t, 4))
                ins = dve.tensor_scalar(dst(t), src(t), bmv[:, t, 0:1], brs[:, 1, t:t + 1], ALU.subtract, ALU.mult)
                ins.then_inc(s.z_ready.h, 1)

        def back_update(pool, s, it, tiles, z):
            for t in tiles:
                x = X[:, it * TG + t, :]
                pool.wait_ge(s.z_ready.h, s.z_ready.done(it, t))
                pool.tensor_tensor(x, x, z(t), ALU.add).then_inc(s.xupd.h, 1)

        def groups(eng, body):
            with eng.Fori(0, NG - 1) as it:
                body(it, False)
            body(NG - 1, True)

        with ExitStack() as mem:
            s = phs[0]
            WA = s.W
            bq = sb(mem, "bias_qkv", [P, 768], F32)
            bd = sb(mem, "bias_dense", [P, H], F32)
            qk = sb(mem, "qk_roped", [P, TG, 640], F32)
            vf = sb(mem, "v_full", [P, TG, P], F32)
            vr = sb(mem, "v_rest", [P, 2, P], F32)
            vp = sb(mem, "v_parts_and_one", [P, TG, NKV, VC], BF16)
            rtmp = sb(mem, "rope_tmp", [P, 640], F32)
            qst = sb(mem, "q_stack", [P, 2, 2, QPK, 2, 64], F32R)
            kst = sb(mem, "k_stack", [P, 2, 2, 2, 64], F32R)
            pf = sb(mem, "probs_full", [P, 2, H], F32)
            ph = sb(mem, "probs_hi", [P, 4, H], FP16)
            pl = sb(mem, "probs_lo", [P, 4, H], FP16)
            RR = sb(mem, "max_rows", [P, 2, 2, H], BF16)
            mx = sb(mem, "max_q", [P, 2, 2, 8], F32)
            mp = sb(mem, "max_parts", [P, 2, 2, P], BF16)
            rden = sb(mem, "rden", [P, 16], F32)
            csum = sb(mem, "ctx_sum", [P, 2, P], F32)
            ctx = sb(mem, "ctx", [P, TG, H], F32)
            zA = sb(mem, "z_attn", [P, 2, H], F32)
            ctxT = WA[:, 10, :, :].rearrange("p a (c q) -> p a c q", q=P)
            QT = [xT[:, 0, 0:2, :], xT[:, 0, 2:4, :], xT[:, 1, 0:2, :]]
            KTp = [x.rearrange("p (a t k) -> p a t k", a=2, t=2)
                   for x in (WA[:, 11, 0, :], WA[:, 11, 1, :], xT[:, 1, 2, :])]
            Tb, KTb, PVb = Ob[0], Ob[1], Ob[2:4]
            mT = KTb[:, 256:384].bitcast(BF16)
            BLOCKS = ((0, 0), (0, 1), (1, 1))

            def step_order(i):
                out = []
                nq = [("q", 6 * (i + 1) + n) for n in range(6)] if i + 1 < STEPS else []
                for n in range(3):
                    out += nq[n:n + 1]
                    if i:
                        out.append(("v", 6 * i - 3 + n))
                for n in range(6):
                    out.append(("k", 6 * i + n))
                    if n >= 3:
                        out.append(("v", 6 * i + n - 3))
                    if n < 3:
                        out += nq[n + 3:n + 4]
                    if n in (1, 2) and i + 2 < STEPS:
                        out.append(("t", (i + 2, n - 1)))
                    if i in (NPAIR + 1, NPAIR + 2) and n in (3, 5):
                        out.append(("c" if n == 3 else "d", i - NPAIR - 1))
                return out

            orders = [step_order(i) for i in range(STEPS)]
            ring = [("q", n) for n in range(6)] + [x for o in orders for x in o if x[0] in "qk"]
            use_of = {r: u for u, r in enumerate(ring)}

            def ring_wait(pe, it, kind, n):
                u = use_of[(kind, n)]
                if u >= 4:
                    before, m = ring[u - 4]
                    sig = s.red if before == "q" else s.ex
                    pe.wait_ge(sig.h, sig.done(it, m))
                return Hb[u % 4]

            def ring_bank(kind, n):
                return Hb[use_of[(kind, n)] % 4]

            def pe_transposes(pe, it, i, t):
                n = 2 * i + t
                pe.wait_ge(s.stack.h, s.stack.done(it, n))
                if n:
                    pe.wait_ge(s.tev.h, s.tev.done(it, n - 1))
                for j in range(QPK):
                    pe.transpose(Tb[:, j * P:(j + 1) * P],
                                 qst[:, i % 2, t, j, :, :].rearrange("p a c -> p (a c)").bitcast(F32), identf)
                pe.transpose(KTb[:, t * P:(t + 1) * P],
                             kst[:, i % 2, t, :, :].rearrange("p a c -> p (a c)").bitcast(F32),
                             identf).then_inc(s.tr.h, 1)

            def pe_scores_q(pe, it, m):
                i, ab, n = m // 6, m // 3 % 2, m % 3
                qt, j0, nk = ((0, 0, 1), (1, 0, 2), (1, 2, 2))[n]
                if m % 6 == 0:
                    pe.wait_ge(s.tev.h, s.tev.done(it, 2 * i + 1))
                bank = ring_wait(pe, it, "q", m)
                nj = QPK // nk
                v = bank[:, :].rearrange("p (j k) -> p j k", j=nj)
                pe.matmul(v[:, :, (nk - 1) * P:nk * P], identb, mask_qk.unsqueeze(1).broadcast_to([P, nj, P]),
                          start=True, stop=False, skip_group_check=True)
                for j in range(nj):
                    ins = pe.matmul(v[:, j, :], QT[i % 3][:, qt, (j0 + j) * P:(j0 + j + 1) * P],
                                    KTp[i % 3][:, ab, 0:nk, :].rearrange("p t k -> p (t k)"),
                                    start=False, stop=j == nj - 1, skip_group_check=True)
                ins.then_inc(s.sq.h, 1)

            def pe_max_rows(pe, it, i):
                pe.wait_ge(s.mp.h, s.mp.done(it, i))
                pe.wait_ge(s.tev.h, s.tev.done(it, 2 * min(i + 1, STEPS - 1) + 1))
                if i >= 1:
                    pe.wait_ge(s.rr.h, s.rr.done(it, i - 1))
                for qt in range(2):
                    ins = pe.transpose(mT[:, qt * P:(qt + 1) * P], mp[:, i % 2, qt, :], identb)
                ins.then_inc(s.mt.h, 1)

            def pe_scores_k(pe, it, m):
                i, ab = m // 6, m // 3 % 2
                kt, qt = BLOCKS[m % 3]
                if m % 6 == 0:
                    pe.wait_ge(s.rr.h, s.rr.done(it, i))
                bank = ring_wait(pe, it, "k", m)
                if kt == qt:
                    pe.matmul(bank[:, :].rearrange("p (j q) -> p j q", j=QPK), identb,
                              mask_kq.unsqueeze(1).broadcast_to([P, QPK, P]), start=True, stop=False)
                pe.matmul(bank[:, :], KTp[i % 3][:, ab, kt, :], QT[i % 3][:, qt, :], start=kt != qt, stop=False)
                pe.matmul(bank[:, :], sel[:, ab, :], RR[:, i % 2, qt, :], start=False, stop=True).then_inc(s.st.h, 1)

            def pe_pv(pe, it, m):
                i, ab = m // 6, m // 3 % 2
                kt, qt = BLOCKS[m % 3]
                g, tile = 2 * (i % NPAIR) + ab, 2 * (i // NPAIR) + kt
                if m % 6 == 0:
                    pe.wait_ge(s.nrm.h, s.nrm.free(it, i, 1))
                    if i == 0:
                        pe.wait_ge(s.vp.h, s.vp.done(it, 3))
                pe.wait_ge(s.plo.h, s.plo.done(it, m))
                v = PVb[qt][:, 0:8 * VC].rearrange("p (g j d) -> p g j d", g=2, j=QPK)
                for j in range(QPK):
                    for x, half in enumerate((ph, pl)):
                        ins = pe.matmul(v[:, ab, j, :], half[:, m % 4, j * P:(j + 1) * P], vp[:, tile, g, :],
                                        start=m % 6 == qt and j == 0 and x == 0, stop=kt == qt and x == 1,
                                        skip_group_check=True)
                ins.then_inc(s.pv.h, 1)

            def pe_ctx_transpose(pe, it, n):
                pe.wait_ge(s.nrm.h, s.nrm.done(it, NPAIR * (n // 2) + NPAIR - 1))
                pe.wait_ge(s.tev.h, s.tev.done(it, 2 * STEPS - 1))
                if n:
                    pe.wait_ge(s.otaken.h, s.otaken.done(it, n - 1))
                for c in range(KT):
                    ins = pe.transpose(Tb[:, c * P:(c + 1) * P], ctx[:, n, c * P:(c + 1) * P], identf)
                ins.then_inc(s.ct.h, 1)

            def pe_dense(pe, it, n):
                pe.wait_ge(s.clo.h, s.clo.done(it, n))
                for c in range(KT):
                    for k, (a, x) in enumerate(PASSES):
                        ins = pe.matmul(Tb[:, :], ctxT[:, x, c, :], WA[:, 6 + c, a, :],
                                        start=c == 0 and k == 0, stop=c == KT - 1 and k == 2)
                ins.then_inc(s.o_ready.h, 1)

            def pe_attention(pe):
                weights_wait(pe, 0)
                pe.wait_ge(s_const, 16 * 4)
                pe.wait_ge(s_init, 2)
                front_transpose(pe, 0, 0)

                def body(it, last):
                    pe.wait_ge(fr[0]["lo"].h, fr[0]["lo"].done(it, 3))
                    for t in range(TG):
                        pe.wait_ge(s.qkv_free.h, s.qkv_free.free(it, t, 2))
                        q, kv = Hb[2 * t % 4], Hb[(2 * t + 1) % 4]
                        tokens_by_weights(pe, q, 512, t, lambda k: (WA[:, k, 0, :], WA[:, k, 1, :])).then_inc(s.qkv.h, 1)
                        tokens_by_weights(pe, kv, 256, t, lambda k: tuple(
                            WA[:, 4 + k // 2, a, (k % 2) * 256:(k % 2) * 256 + 256] for a in range(2))
                        ).then_inc(s.qkv.h, 1)
                    for i in range(2):
                        for t in range(2):
                            pe_transposes(pe, it, i, t)
                    pe.wait_ge(s.qkv_free.h, s.qkv_free.done(it, 3))
                    for m in range(6):
                        pe_scores_q(pe, it, m)
                    for i in range(STEPS):
                        pe_max_rows(pe, it, i)
                        for kind, m in orders[i]:
                            if kind == "q":
                                pe_scores_q(pe, it, m)
                            elif kind == "k":
                                pe_scores_k(pe, it, m)
                            elif kind == "v":
                                pe_pv(pe, it, m)
                            elif kind == "t":
                                pe_transposes(pe, it, *m)
                            elif kind == "c":
                                pe_ctx_transpose(pe, it, m)
                            else:
                                pe_dense(pe, it, m)
                    for n in range(3):
                        pe_pv(pe, it, 6 * STEPS - 3 + n)
                    fph, fit = nxt(0, it, last)
                    front_transpose(pe, fph, fit)
                    for n in (2, 3):
                        pe_ctx_transpose(pe, it, n)
                        pe_dense(pe, it, n)
                    pe.wait_ge(s.otaken.h, s.otaken.done(it, 3))

                groups(pe, body)
                pe.wait_ge(s.otaken.h, s.otaken.done(NG - 1, 3))
                pe.sem_inc(s.pe_end, 1)

            def act_attention(act):
                front_hi(act, 0, 0)

                def keep(it, i, t):
                    n = 2 * i + t
                    act.wait_ge(s.tr.h, s.tr.done(it, n))
                    act.activation(QT[i % 3][:, t, :], Tb[:, :], ACT.Copy)
                    for ab in range(2):
                        r = slice(64 * ab, 64 * ab + 64)
                        ins = act.activation(KTp[i % 3][r, ab, t, :], KTb[r, t * P:(t + 1) * P], ACT.Copy)
                    ins.then_inc(s.tev.h, 1)

                def exps(it, m):
                    bank = ring_bank("k", m)
                    act.wait_ge(s.st.h, s.st.done(it, m))
                    act.wait_ge(s.pv.h, s.pv.free(it, m, 4))
                    act.activation(ph[:, m % 4, :], bank[:, :], ACT.Exp, scale=1.0 / HD)
                    act.wait_ge(s.plo.h, s.plo.free(it, m, 2))
                    act.activation(pf[:, m % 2, :], bank[:, :], ACT.Exp, scale=1.0 / HD).then_inc(s.ex.h, 1)

                def ctx_hi(it, n):
                    act.wait_ge(s.ct.h, s.ct.done(it, n))
                    act.activation(ctxT[:, 0, :, :].rearrange("p c q -> p (c q)"), Tb[:, :],
                                   ACT.Copy).then_inc(s.chi.h, 1)

                def body(it, last):
                    act.wait_ge(s.qkv.h, s.qkv.done(it, 7))
                    for ab in range(2):
                        r = slice(64 * (1 - ab), 64 * (1 - ab) + 64)
                        ins = act.activation(KTp[2][r, ab, :, :].rearrange("p t k -> p (t k)"), zeros[r, :], ACT.Copy)
                    for i in range(2):
                        for t in range(2):
                            keep(it, i, t)
                    for i in range(STEPS):
                        for kind, m in orders[i]:
                            if kind == "k":
                                exps(it, m)
                            elif kind == "t":
                                keep(it, *m)
                            elif kind == "c":
                                ctx_hi(it, m)
                    front_hi(act, *nxt(0, it, last))
                    ctx_hi(it, 2)
                    ctx_hi(it, 3)

                groups(act, body)

            def dve_attention(dve, ch):
                ch.link(dve.memset(vp[:, :, :, :], 1.0))
                ch.link(dve.memset(mp[:, :, :, :], 0.0))
                ch.link(dve.memset(zeros[:, :], 0.0))
                for b in range(2):
                    ins = dve.memset(KTp[b][:, :, :, :].bitcast(F32), 0.0)
                ins.then_inc(s_init, 1)
                dve.wait_ge(s_x[0], 16)
                front_stats(dve, ch, 0, 0)
                front_norm(dve, 0, 0, range(4))
                front_lo(dve, 0, 0)
                ch.commit()
                for g in range(1, NG):
                    dve.wait_ge(s_x[g], 16)

                def evac(it, t):
                    q, kv = Hb[2 * t % 4], Hb[(2 * t + 1) % 4]
                    dve.wait_ge(s.qkv.h, s.qkv.done(it, 2 * t))
                    dve.tensor_tensor(qk[:, t, 0:512], q[:, :], bq[:, 0:512], ALU.add)
                    dve.wait_ge(s.qkv.h, s.qkv.done(it, 2 * t + 1))
                    dve.tensor_tensor(qk[:, t, 512:640], kv[:, 0:128], bq[:, 512:640], ALU.add)
                    dve.tensor_tensor(vf[:, t, :], kv[:, 128:256], bq[:, 640:768], ALU.add).then_inc(s.qkv_free.h, 1)

                def rope(it, t):
                    z = qk[:, t, :].rearrange("p (h d) -> p h d", d=HD)
                    r = rtmp[:, :].rearrange("p (h d) -> p h d", d=HD)
                    n, hf = 640 // HD, HD // 2
                    def table(a):
                        return a[:, t % 2, :].unsqueeze(1).broadcast_to([P, n, a.shape[2]])
                    dve.wait_ge(s.qkv_free.h, s.qkv_free.done(it, t))
                    dve.wait_ge(s.rope.h, s.rope.free(it, t, 1))
                    dve.tensor_tensor(r[:, :, 0:hf], z[:, :, hf:HD], table(nsin_t), ALU.mult)
                    ch.link(dve.tensor_tensor(r[:, :, hf:HD], z[:, :, 0:hf], table(sin_t), ALU.mult))
                    ch.link(dve.tensor_tensor(z, z, table(cos_t), ALU.mult))
                    dve.tensor_tensor(z, z, r, ALU.add).then_inc(s.rope.h, 1)

                def maxima(it, m):
                    i, ab, n = m // 6, m // 3 % 2, m % 3
                    qt, j0, nj = ((0, 0, 4), (1, 0, 2), (1, 2, 2))[n]
                    dve.wait_ge(s.sq.h, s.sq.done(it, m))
                    c = 4 * ab + j0
                    dve.tensor_reduce(mx[:, i % 2, qt, c:c + nj],
                                      ring_bank("q", m)[:, :].rearrange("p (j k) -> p j k", j=nj),
                                      AX_X, ALU.max).then_inc(s.red.h, 1)

                def max_parts(it, i):
                    m = mp[:, i % 2, :, :]
                    dve.wait_ge(s.red.h, s.red.done(it, 6 * i + 5))
                    ch.link(dve.tensor_scalar(m[:, :, 0:8], mx[:, i % 2, :, :], SHIFT, None, ALU.subtract))
                    dve.scalar_tensor_tensor(out=m[:, :, 8:16], in0=mx[:, i % 2, :, :], scalar=SHIFT,
                                             in1=m[:, :, 0:8], op0=ALU.subtract, op1=ALU.subtract).then_inc(s.mp.h, 1)

                def max_rows(it, i):
                    dve.wait_ge(s.mt.h, s.mt.done(it, i))
                    for qt in range(2):
                        ins = dve.tensor_tensor(
                            RR[:, i % 2, qt, :].rearrange("p (j q) -> p j q", j=QPK),
                            mT[:, qt * P:(qt + 1) * P].unsqueeze(1).broadcast_to([P, QPK, P]),
                            headsel.unsqueeze(2).broadcast_to([P, QPK, P]), ALU.mult)
                    ins.then_inc(s.rr.h, 1)

                def probs_lo(it, m):
                    dve.wait_ge(s.ex.h, s.ex.done(it, m))
                    dve.tensor_tensor(pl[:, m % 4, :], pf[:, m % 2, :], ph[:, m % 4, :],
                                      ALU.subtract).then_inc(s.plo.h, 1)

                def normalise(it, i):
                    p = i % NPAIR
                    dve.wait_ge(s.pv.h, s.pv.done(it, 6 * i + 5))
                    for t in range(2):
                        v = PVb[t][:, 0:8 * VC].rearrange("p (h d) -> p h d", d=VC)
                        dve.reciprocal(rden[:, 8 * t:8 * t + 8], v[:, :, 3 * HD])
                        ins = dve.tensor_reduce(csum[:, t, :].rearrange("p (h d) -> p h d", d=HD),
                                                v[:, :, 0:3 * HD].rearrange("p h (x d) -> p h d x", d=HD),
                                                AX_X, ALU.add)
                    ch.link(ins)
                    for t in range(2):
                        ins = dve.tensor_tensor(
                            ctx[:, 2 * (i // NPAIR) + t, p * 128:(p + 1) * 128].rearrange("p (g d) -> p g d", d=HD),
                            csum[:, t, :].rearrange("p (h d) -> p h d", d=HD),
                            rden[:, 8 * t:8 * t + 8].unsqueeze(2).broadcast_to([P, 8, HD]), ALU.mult)
                    ins.then_inc(s.nrm.h, 1)

                def ctx_lo(it, n):
                    dve.wait_ge(s.chi.h, s.chi.done(it, n))
                    dve.tensor_tensor(ctxT[:, 1, :, :].rearrange("p c q -> p (c q)"), Tb[:, :],
                                      ctxT[:, 0, :, :].rearrange("p c q -> p (c q)").bitcast(F32),
                                      ALU.subtract).then_inc(s.clo.h, 1)

                def take(it, n):
                    dve.wait_ge(s.o_ready.h, s.o_ready.done(it, n))
                    dve.wait_ge(s.xupd.h, s.xupd.free(it, n, 2))
                    dve.tensor_tensor(zA[:, n % 2, :], Tb[:, :], bd[:, :], ALU.add).then_inc(s.otaken.h, 1)

                def back(it, b):
                    tiles = [2 * b, 2 * b + 1]
                    dve.wait_ge(s.otaken.h, s.otaken.done(it, tiles[1]))
                    z = lambda t: zA[:, t % 2, :]
                    back_stats(dve, ch, s, it, tiles, b, z)
                    back_norm(dve, s, it, tiles, b, z, z)

                def body(it, last):
                    ch.begin(it, last, DVE_CHAIN_ATTN)
                    fph, fit = nxt(0, it, last)
                    for t in range(TG):
                        evac(it, t)
                        if t < 2:
                            rope(it, t)
                    for m in range(6):
                        maxima(it, m)
                    max_parts(it, 0)
                    for i in range(STEPS):
                        if i:
                            probs_lo(it, 6 * i - 3)
                        max_rows(it, i)
                        for n in range(3):
                            if i + 1 < STEPS:
                                maxima(it, 6 * (i + 1) + n)
                            if i and n < 2:
                                probs_lo(it, 6 * i - 2 + n)
                        if i:
                            normalise(it, i - 1)
                        if i >= NPAIR + 2:
                            take(it, i - NPAIR - 2)
                        for n in range(3):
                            if i + 1 < STEPS:
                                maxima(it, 6 * (i + 1) + 3 + n)
                            if i + 1 < STEPS and n == 2:
                                max_parts(it, i + 1)
                            probs_lo(it, 6 * i + n)
                        if i < 2:
                            rope(it, 2 + i)
                        if i in (NPAIR + 1, NPAIR + 2):
                            ctx_lo(it, i - NPAIR - 1)
                        if i == STEPS - 1:
                            back(it, 0)
                        if i == STEPS - 2:
                            front_stats(dve, ch, fph, fit)
                    for n in range(3):
                        probs_lo(it, 6 * STEPS - 3 + n)
                    front_norm(dve, fph, fit, (0, 1))
                    normalise(it, STEPS - 1)
                    front_norm(dve, fph, fit, (2, 3))
                    front_lo(dve, fph, fit)
                    for n in (2, 3):
                        ctx_lo(it, n)
                        take(it, n)
                    back(it, 1)
                    ch.end(last)

                groups(dve, body)

            def pool_attention(pool, ch):
                ch.link(pool.memset(mhalf[:, :], -0.5))
                ch.link(pool.memset(qst[:, :, :, :, :, :].bitcast(F32), 0.0))
                pool.memset(kst[:, :, :, :, :].bitcast(F32), 0.0).then_inc(s_init, 1)
                for c in credits:
                    pool.sem_inc(c.h, c.credit)
                pool.sem_inc(s_xntr, 2)
                pool.wait_ge(s_init, 2)
                front_rstd(pool, ch, 0, 0)
                w_split(pool, ch, 0, 0)
                ch.commit()

                def stacks(it, i):
                    b, p = i // NPAIR, i % NPAIR
                    for t in range(2):
                        pool.wait_ge(s.rope.h, s.rope.done(it, 2 * b + t))
                        pool.wait_ge(s.tr.h, s.tr.free(it, 2 * i + t, 4))
                        lone(pool)
                        zq = qk[:, 2 * b + t, 128 * p:128 * p + 128]
                        zk = qk[:, 2 * b + t, 512 + 32 * p:544 + 32 * p].rearrange("p (a d) -> p a d", a=2)
                        kk = kst[:, i % 2, t, :, :]
                        for ab in range(2):
                            z = zq[:, 64 * ab:64 * ab + 64].rearrange("p (j d) -> p j d", j=QPK)
                            q = qst[:, i % 2, t, :, ab, :]
                            pool.tensor_copy(q[:, :, 0:16], z)
                            pool.tensor_copy(q[:, :, 16:32], z)
                        pool.tensor_copy(kk[:, :, 0:16], zk)
                        ch.link(pool.tensor_copy(kk[:, :, 32:48], zk))
                        for ab in range(2):
                            z = zq[:, 64 * ab:64 * ab + 64].rearrange("p (j d) -> p j d", j=QPK)
                            q = qst[:, i % 2, t, :, ab, :]
                            pool.tensor_tensor(q[:, :, 32:48], z, q[:, :, 0:16].bitcast(F32), ALU.subtract)
                        pool.tensor_tensor(kk[:, :, 16:32], zk, kk[:, :, 0:16].bitcast(F32),
                                           ALU.subtract).then_inc(s.stack.h, 1)

                def v_parts(it, t):
                    part = lambda x: vp[:, t, :, x * HD:(x + 1) * HD]
                    full, rest = (b.rearrange("p (g d) -> p g d", d=HD) for b in (vf[:, t, :], vr[:, t % 2, :]))
                    pool.wait_ge(s.qkv_free.h, s.qkv_free.done(it, t))
                    if t == 0:
                        pool.wait_ge(s.pv.h, s.pv.free(it, 0, 1))
                    if t >= 2:
                        pool.wait_ge(s.vp.h, s.vp.done(it, t - 2))
                    lone(pool)
                    ch.link(pool.tensor_copy(part(0), full))
                    ch.link(pool.tensor_tensor(rest, full, part(0), ALU.subtract))
                    lone(pool)
                    ch.link(pool.tensor_copy(part(1), rest))
                    pool.tensor_tensor(part(2), rest, part(1), ALU.subtract).then_inc(s.vp.h, 1)

                def body(it, last):
                    ch.begin(it, last, POOL_CHAIN_ATTN)
                    stacks(it, 0)
                    stacks(it, 1)
                    for t in range(TG):
                        v_parts(it, t)
                    stacks(it, 2)
                    for i in range(STEPS):
                        if i + 3 < STEPS:
                            stacks(it, i + 3)
                        if not last and 2 <= i < 5:
                            w_split(pool, ch, 1, it, [i - 2])
                        if i == STEPS - 2:
                            front_rstd(pool, ch, *nxt(0, it, last))
                    back_rstd(pool, ch, s, it, [0, 1], 0)
                    back_update(pool, s, it, [0, 1], lambda t: zA[:, t % 2, :])
                    back_rstd(pool, ch, s, it, [2, 3], 1)
                    back_update(pool, s, it, [2, 3], lambda t: zA[:, t % 2, :])
                    ch.end(last)

                groups(pool, body)

            attn = (bq, bd, pe_attention, act_attention, dve_attention, pool_attention)

        Y = sb(top, "y_taylor_glu", [P, NG * TG, H], F32)
        z4 = sb(top, "z", [P, TG, H], F32)
        sg = sb(top, "silu_gate", [P, 2, H], F32)
        hf = sb(top, "h_full", [P, 2, H], F32)
        hh = sb(top, "h_hi", [P, 2, H], F32R)
        hl = sb(top, "h_lo", [P, 2, H], F32R)

        def z_of(s, it):
            return (lambda t: Y[:, it * TG + t, :]) if s.name == "glu_c" else (lambda t: z4[:, t, :])

        def phase_start(eng, ph, what):
            prev = phs[ph - 1]
            if what == "pe":
                sig = prev.otaken if ph == 1 else prev.o_free
                eng.wait_ge(sig.h, sig.done(NG - 1, 3))
            if what in ("act", "dve", "pool") and ph == 1:
                eng.wait_ge(prev.xupd.h, prev.xupd.done(NG - 1, 3))
                eng.wait_ge(prev.pe_end, 1)

        def pe_down(pe, s, it, f, nf, chunk, rows=P, opens=True):
            pe.wait_ge(s.hlo.h, s.hlo.done(it, f))
            for t in range(TG):
                if f == 0 and opens:
                    pe.wait_ge(s.o_free.h, s.o_free.free(it, t, 4))
                for n, (a, x) in enumerate(PASSES):
                    h = (hh, hl)[x]
                    ins = pe.matmul(Ob[t][:, :], h[0:rows, f % 2, t * P:(t + 1) * P], s.W[0:rows, chunk, a, :],
                                    start=opens and f == 0 and n == 0, stop=f == nf - 1 and n == 2)
                if f == nf - 1:
                    ins.then_inc(s.o_ready.h, 1)
            if f < nf - 1:
                ins.then_inc(s.hused.h, 1)
            else:
                pe.wait_ge(s.o_ready.h, s.o_ready.done(it, 3))
                pe.sem_inc(s.hused.h, 1)

        def act_split(act, s, it, f, src, dst):
            act.wait_ge(s.hf.h, s.hf.done(it, f))
            act.wait_ge(s.hused.h, s.hused.free(it, f, 2))
            act.activation(dst, src, ACT.Copy).then_inc(s.hhi.h, 1)

        def dve_split(dve, s, it, f, src, hi, dst):
            dve.wait_ge(s.hhi.h, s.hhi.done(it, f))
            dve.tensor_tensor(dst, src, hi.bitcast(F32), ALU.subtract).then_inc(s.hlo.h, 1)

        def dve_back(dve, ch, s, it):
            z = z_of(s, it)
            for t in range(TG):
                dve.wait_ge(s.o_ready.h, s.o_ready.done(it, t))
                if s.name in ("glu_a", "glu_b", "glu_c"):
                    y = Y[:, it * TG + t, :]
                    ins = dve.tensor_tensor(y, y, Ob[t][:, :], ALU.add)
                elif s.name == "glu_d":
                    dve.wait_ge(s.xupd.h, s.xupd.free(it, t, 4))
                    ins = dve.tensor_tensor(z(t), Ob[t][:, :], bias3[:, :], ALU.add)
                elif s.name == "taylor":
                    ins = dve.tensor_copy(Y[:, it * TG + t, :], Ob[t][:, :])
                else:
                    dve.wait_ge(s.xupd.h, s.xupd.free(it, t, 4))
                    ins = dve.tensor_copy(z(t), Ob[t][:, :])
                ins.then_inc(s.o_free.h, 1)
            if s.updates:
                dve.wait_ge(s.o_free.h, s.o_free.done(it, 3))
                back_stats(dve, ch, s, it, range(TG), 0, z)
                back_norm(dve, s, it, range(TG), 0, z, z)

        def pool_back(pool, ch, s, it):
            if s.updates:
                back_rstd(pool, ch, s, it, range(TG), 0)
                back_update(pool, s, it, range(TG), z_of(s, it))

        def pool_phase(pool, ch, ph):
            s = phs[ph]
            phase_start(pool, ph, "pool")
            end = ph == len(PHASES) - 1

            def body(it, last):
                ch.begin(it, last, 1 + (0 if end else wper(ph + 1)) + int(s.updates))
                if not (end and last):
                    front_rstd(pool, ch, *nxt(ph, it, last))
                if not last and not end:
                    if not isinstance(it, int):
                        pool.wait_ge(phs[ph - 1].pe_end, 1)
                    w_split(pool, ch, ph + 1, it)
                pool_back(pool, ch, s, it)
                ch.end(last)

            groups(pool, body)

        def pe_glu(pe, ph):
            s = phs[ph]
            nf = s.nf
            end = ph == len(PHASES) - 1
            weights_wait(pe, ph)
            phase_start(pe, ph, "pe")

            def body(it, last):
                def up(f):
                    for n in range(2):
                        if f == 0 and n == 0:
                            pe.wait_ge(fr[ph]["lo"].h, fr[ph]["lo"].done(it, 3))
                        if f >= 2 and n == 0:
                            pe.wait_ge(s.hf.h, s.hf.done(it, f - 2))
                        features(pe, Hb[(2 * f + n) % 4],
                                 lambda k: tuple(s.W[:, 3 * f + n, a, k * P:(k + 1) * P] for a in range(2))
                                 ).then_inc(s.in_ready.h, 1)

                up(0)
                for f in range(1, nf):
                    up(f)
                    pe_down(pe, s, it, f - 1, nf, 3 * (f - 1) + 2)
                if not (end and last):
                    pe.wait_ge(s.hf.h, s.hf.done(it, nf - 1))
                    front_transpose(pe, *nxt(ph, it, last))
                pe_down(pe, s, it, nf - 1, nf, 3 * (nf - 1) + 2)

            groups(pe, body)
            pe.sem_inc(s.pe_end, 1)

        def act_glu(act, ph):
            s = phs[ph]
            nf = s.nf
            bias = b12 if s.name == "glu_d" else zero8

            def body(it, last):
                for f in range(nf):
                    act.wait_ge(s.in_ready.h, s.in_ready.done(it, 2 * f))
                    act.wait_ge(s.hf.h, s.hf.free(it, f, 2))
                    act.activation(sg[:, f % 2, :], Hb[(2 * f) % 4][:, :], ACT.Silu,
                                   bias=bias[:, f:f + 1]).then_inc(s.sg.h, 1)
                    act_split(act, s, it, f, hf[:, f % 2, :], hh[:, f % 2, :])
                if not (ph == len(PHASES) - 1 and last):
                    front_hi(act, *nxt(ph, it, last))

            groups(act, body)

        def dve_glu(dve, ch, ph):
            s = phs[ph]
            nf = s.nf
            end = ph == len(PHASES) - 1
            bias = b12 if s.name == "glu_d" else zero8

            def body(it, last):
                ch.begin(it, last, TG + (TG if s.updates else 0))
                fph, fit = nxt(ph, it, last)
                go = not (end and last)
                if go:
                    front_stats(dve, ch, fph, fit)
                    front_norm(dve, fph, fit, (0, 1))
                for f in range(nf):
                    dve.wait_ge(s.in_ready.h, s.in_ready.done(it, 2 * f + 1))
                    dve.wait_ge(s.sg.h, s.sg.done(it, f))
                    dve.scalar_tensor_tensor(out=hf[:, f % 2, :], in0=Hb[(2 * f + 1) % 4][:, :],
                                             scalar=bias[:, 4 + f:5 + f], in1=sg[:, f % 2, :],
                                             op0=ALU.add, op1=ALU.mult).then_inc(s.hf.h, 1)
                    dve_split(dve, s, it, f, hf[:, f % 2, :], hh[:, f % 2, :], hl[:, f % 2, :])
                if go:
                    front_norm(dve, fph, fit, (2, 3))
                    front_lo(dve, fph, fit)
                dve_back(dve, ch, s, it)
                ch.end(last)

            groups(dve, body)

        smallm = sb(top, "route_small", [P, 8, TG], F32)
        m8 = sb(top, "route_max8", [P, TG, 8], F32)
        i8 = sb(top, "route_index8", [P, TG, 8], U32)
        idx = sb(top, "route_index", [P, TG, 2], F32)
        gate = sb(top, "route_gate", [P, TG, 2, NE], F32)
        hs = z4

        def pe_moe(pe):
            s = phs[1]
            weights_wait(pe, 1)
            phase_start(pe, 1, "pe")

            def body(it, last):
                pe.wait_ge(fr[1]["lo"].h, fr[1]["lo"].done(it, 3))
                for t in range(TG):
                    tokens_by_weights(pe, Hb[t], 256, t, lambda k: tuple(
                        s.W[:, 4 + k // 2, a, (k % 2) * 256:(k % 2) * 256 + 256] for a in range(2))
                    ).then_inc(s.in_ready.h, 1)
                for t in range(TG):
                    pe.wait_ge(s.o_free.h, s.o_free.free(it, t, 4))
                    tokens_by_weights(pe, Ob[t], 512, t, lambda k: (s.W[:, k, 0, :], s.W[:, k, 1, :]), final=False)
                pe.wait_ge(s.hs.h, s.hs.done(it, 3))
                fph, fit = nxt(1, it, last)
                front_transpose(pe, fph, fit)
                pe.wait_ge(fr[fph]["lo"].h, fr[fph]["lo"].done(fit, 1))
                for t in range(TG):
                    for j in range(2):
                        ins = pe.transpose(Hb[j][0:LH, t * P:(t + 1) * P], hs[:, t, j * LH:(j + 1) * LH], identf)
                ins.then_inc(s.ht.h, 1)
                for f in range(2):
                    pe_down(pe, s, it, f, 2, 6 + f, rows=LH, opens=False)

            groups(pe, body)
            pe.sem_inc(s.pe_end, 1)

        def act_moe(act):
            s = phs[1]
            phase_start(act, 1, "act")
            act.dma_start(bias3[:, :], biases[:, 1280:1792]).then_inc(s_const, 16)

            def body(it, last):
                act.wait_ge(s.rt.h, s.rt.done(it, 0))
                act.activation(smallm[:, 1, :], smallm[:, 0, :], ACT.Exp).then_inc(s.re.h, 1)
                front_hi(act, *nxt(1, it, last))
                act.wait_ge(s.ht.h, s.ht.done(it, 0))
                for f in range(2):
                    act.wait_ge(s.hused.h, s.hused.free(it, f, 2))
                    act.activation(hh[0:LH, f, :], Hb[f][0:LH, :], ACT.Copy).then_inc(s.hhi.h, 1)

            groups(act, body)

        def dve_moe(dve, ch):
            s = phs[1]
            phase_start(dve, 1, "dve")

            def body(it, last):
                ch.begin(it, last, DVE_CHAIN_MOE)
                fph, fit = nxt(1, it, last)
                for t in range(TG):
                    lg = Hb[t][:, LR:LR + NE]
                    dve.wait_ge(s.in_ready.h, s.in_ready.done(it, t))
                    lone(dve)
                    ch.link(dve.max(m8[:, t, :], lg))
                    lone(dve)
                    dve.max_index(i8[:, t, :], m8[:, t, :], lg)
                ch.link(dve.tensor_tensor(smallm[:, 0, :], m8[:, :, 1], m8[:, :, 0], ALU.subtract))
                dve.sem_inc(s.rt.h, 1)
                ch.link(dve.tensor_copy(idx[:, :, :], i8[:, :, 0:2]))
                dve.wait_ge(s.re.h, s.re.done(it, 0))
                ch.link(dve.tensor_scalar(smallm[:, 2, :], smallm[:, 1, :], 1.0, None, ALU.add))
                ch.link(dve.reciprocal(smallm[:, 3, :], smallm[:, 2, :]))
                ch.link(dve.tensor_scalar(smallm[:, 4, :], smallm[:, 3, :], 2.0, None, ALU.mult))
                ch.link(dve.tensor_tensor(smallm[:, 5, :], smallm[:, 4, :], smallm[:, 1, :], ALU.mult))
                for t in range(TG):
                    for c in range(2):
                        ins = dve.tensor_scalar(gate[:, t, c, :], iota, idx[:, t, c:c + 1], smallm[:, 4 + c, t:t + 1],
                                                ALU.is_equal, ALU.mult)
                ch.link(ins)
                ch.link(dve.tensor_tensor(gate[:, :, 0, :], gate[:, :, 0, :], gate[:, :, 1, :], ALU.add))
                for t in range(TG):
                    dve.wait_ge(s.xupd.h, s.xupd.free(it, t, 4))
                    dve.tensor_tensor(hs[:, t, 0:LR].rearrange("p (e r) -> p e r", r=RANK),
                                      Hb[t][:, 0:LR].rearrange("p (e r) -> p e r", r=RANK),
                                      gate[:, t, 0, :].unsqueeze(2).broadcast_to([P, NE, RANK]),
                                      ALU.mult).then_inc(s.hs.h, 1)
                front_stats(dve, ch, fph, fit)
                front_norm(dve, fph, fit, range(4))
                front_lo(dve, fph, fit)
                for f in range(2):
                    dve.wait_ge(s.hhi.h, s.hhi.done(it, f))
                    dve.tensor_tensor(hl[0:LH, f, :], Hb[f][0:LH, :], hh[0:LH, f, :].bitcast(F32),
                                      ALU.subtract).then_inc(s.hlo.h, 1)
                dve_back(dve, ch, s, it)
                ch.end(last)

            groups(dve, body)

        dl = sb(top, "delta", [P, 2, H], F32)

        def pe_taylor(pe):
            s = phs[2]
            weights_wait(pe, 2)
            phase_start(pe, 2, "pe")

            def body(it, last):
                for n in range(2):
                    if n == 0:
                        pe.wait_ge(fr[2]["lo"].h, fr[2]["lo"].done(it, 3))
                        if True:
                            pe.wait_ge(phs[1].hlo.h, phs[1].hlo.done(NG - 1, 1))
                    features(pe, Hb[n], lambda k: tuple(
                        s.W[:, k // 2, a, (k % 2) * 256 + n * P:(k % 2) * 256 + (n + 1) * P] for a in range(2))
                    ).then_inc(s.in_ready.h, 1)
                pe.wait_ge(s.sg.h, s.sg.done(it, 0))
                front_transpose(pe, *nxt(2, it, last))
                for f in range(s.nf):
                    pe_down(pe, s, it, f, s.nf, 2 + f)

            groups(pe, body)
            pe.sem_inc(s.pe_end, 1)

        def act_taylor(act, ch):
            s = phs[2]

            def body(it, last):
                for f in range(s.nf):
                    if f == 1:
                        front_hi(act, *nxt(2, it, last))
                    act_split(act, s, it, f, hf[:, f % 2, :], hh[:, f % 2, :])

            groups(act, body)

        def dve_taylor(dve, ch):
            s = phs[2]

            def body(it, last):
                ch.begin(it, last, DVE_CHAIN_TAYLOR)
                fph, fit = nxt(2, it, last)
                front_stats(dve, ch, fph, fit)
                front_norm(dve, fph, fit, (0, 1))
                dve.wait_ge(s.in_ready.h, s.in_ready.done(it, 0))
                dve.tensor_copy(hf[:, 0, :], Hb[0][:, :]).then_inc(s.hf.h, 1)
                dve.wait_ge(s.in_ready.h, s.in_ready.done(it, 1))
                ch.link(dve.tensor_scalar(dl[:, 0, :], Hb[1][:, :], lp, None, ALU.subtract))
                dve.sem_inc(s.sg.h, 1)
                ch.link(dve.scalar_tensor_tensor(out=dl[:, 1, :], in0=dl[:, 0, :], scalar=-1.0, in1=dl[:, 0, :],
                                                 op0=ALU.mult, op1=ALU.max))
                ch.link(dve.scalar_tensor_tensor(out=dl[:, 1, :], in0=dl[:, 1, :], scalar=THD, in1=dl[:, 0, :],
                                                 op0=ALU.is_le, op1=ALU.mult))
                dve_split(dve, s, it, 0, hf[:, 0, :], hh[:, 0, :], hl[:, 0, :])
                for f in range(1, s.nf):
                    dve.wait_ge(s.hf.h, s.hf.done(it, f - 1))
                    dve.scalar_tensor_tensor(out=hf[:, f % 2, :], in0=hf[:, (f - 1) % 2, :],
                                             scalar=cfac[:, f - 1:f], in1=dl[:, 1 if f == 5 else 0, :],
                                             op0=ALU.mult, op1=ALU.mult).then_inc(s.hf.h, 1)
                    if f == 1:
                        front_norm(dve, fph, fit, (2, 3))
                        front_lo(dve, fph, fit)
                    dve_split(dve, s, it, f, hf[:, f % 2, :], hh[:, f % 2, :], hl[:, f % 2, :])
                dve_back(dve, ch, s, it)
                ch.end(last)

            groups(dve, body)

        bias3 = sb(top, "bias_w3", [P, H], F32)
        bq, bd, pe_attention, act_attention, dve_attention, pool_attention = attn

        DVE_CHAIN_ATTN, DVE_CHAIN_MOE, DVE_CHAIN_TAYLOR, POOL_CHAIN_ATTN = 32, 20, 7, 34

        block = top.enter_context(nc.Block())

        @block.sync
        def _(sp):
            xr = x_in.rearrange("(g t p) n -> g p t n", g=NG, p=P)
            outr = out.rearrange("(g t p) n -> g p t n", g=NG, p=P)
            sp.dma_start(X[:, 0:TG, :], xr[0]).then_inc(s_x[0], 16)
            sp.dma_start(cf[:, :], cons_f).then_inc(s_const, 16)
            sp.dma_start(cb[:, :], cons_b).then_inc(s_const, 16)
            sp.dma_start(bq[:, :], biases[:, 0:768]).then_inc(s_const, 16)
            sp.dma_start(bd[:, :], biases[:, 768:1280]).then_inc(s_const, 16)
            w_load(sp, 0, 0)
            for ph in range(1, len(PHASES)):
                with sp.Fori(0, 3) as it:
                    w_load(sp, ph, it)
            s = phs[-1]
            for g in range(NG):
                sp.wait_ge(s.xupd.h, s.xupd.done(g, 3))
                sp.dma_start(outr[g], X[:, g * TG:(g + 1) * TG, :]).then_inc(s_out, 16)
            sp.wait_ge(s_out, 16 * NG)

        @block.gpsimd
        def _(pool):
            ch = Chain(pool, chain_pool)
            pool_attention(pool, ch)
            for ph in range(1, len(PHASES)):
                pool_phase(pool, ch, ph)

        @block.scalar
        def _(act):
            xr = x_in.rearrange("(g t p) n -> g p t n", g=NG, p=P)
            for g in range(1, NG):
                act.dma_start(X[:, g * TG:(g + 1) * TG, :], xr[g]).then_inc(s_x[g], 16)
            act.wait_ge(s_const, 16 * 4)
            act.wait_ge(chain_act, 1)
            act.activation(cfac[:, 0:NORD], cfac[:, 0:NORD], ACT.Exp).then_inc(chain_act, 1)
            act_attention(act)
            act_moe(act)
            act_taylor(act, None)
            for ph in range(3, 7):
                act_glu(act, ph)

        @block.vector
        def _(dve):
            ch = Chain(dve, chain_dve)
            dve.wait_ge(s_const, 16 * 4)
            dve.tensor_scalar(cfac[:, 0:1], disc[:, 0:1], -1.0, None, ALU.mult)
            dve.tensor_tensor(cfac[:, 1:NORD], disc[:, 0:NORD - 1], disc[:, 1:NORD], ALU.subtract).then_inc(chain_act, 1)
            dve_attention(dve, ch)
            dve_moe(dve, ch)
            dve.wait_ge(chain_act, 2)
            dve_taylor(dve, ch)
            dve.wait_ge(s_const, 16 * 5)
            for ph in range(3, 7):
                dve_glu(dve, ch, ph)

        @block.tensor
        def _(pe):
            pe_attention(pe)
            pe_moe(pe)
            pe_taylor(pe)
            for ph in range(3, 7):
                pe_glu(pe, ph)


def kernel(**inputs):
    import numpy as np
    import ml_dtypes
    import concourse.bacc as bacc
    from concourse.bass_utils import run_bass_kernel_spmd as run

    a = {k: np.asarray(v) for k, v in inputs.items()}
    x = a["L0_attn_hidden_states"]
    B, S, _ = x.shape

    def k_tiles(w, cols):
        wt = w.T
        full = np.zeros((wt.shape[0], cols), np.float32)
        full[:, :wt.shape[1]] = wt
        return full.reshape(-1, P, cols)

    wq = a["L0_attn_w_qkv"].reshape(NKV, QPK + 2, HD, H)
    bqkv = a["L0_attn_b_qkv"].reshape(NKV, QPK + 2, HD)
    q_w = k_tiles(wq[:, :QPK].reshape(-1, H), 512)
    kv_w = k_tiles(np.concatenate([wq[:, QPK].reshape(-1, H), wq[:, QPK + 1].reshape(-1, H)]), 256)
    b_row = np.concatenate([bqkv[:, :QPK].reshape(-1), bqkv[:, QPK].reshape(-1), bqkv[:, QPK + 1].reshape(-1),
                            a["L0_attn_b_dense"], a["L1_ffn_b3"]])

    def two(t):
        return [np.concatenate([t[2 * i], t[2 * i + 1]], axis=1) for i in range(2)]

    def glu(w1, w2, w3, tiles):
        out = []
        for f in tiles:
            for w in (w1, w2):
                wt = np.zeros((P, H), np.float32)
                part = w[f * P:(f + 1) * P]
                wt[:part.shape[0]] = part
                out.append(wt.T.reshape(KT, P, P).transpose(1, 0, 2).reshape(P, H))
            d = np.zeros((P, H), np.float32)
            part = w3.T[f * P:(f + 1) * P]
            d[:part.shape[0]] = part
            out.append(d)
        return out

    zero = np.zeros((P, H), np.float32)
    chunks = list(q_w) + two(kv_w) + list(k_tiles(a["L0_attn_w_dense"], 512))
    la = a["L0_ffn_lora_A"].reshape(LR, H)
    chunks += list(k_tiles(a["L0_ffn_base_W"], 512)) + two(k_tiles(np.concatenate([la, a["L0_ffn_gate_W"]]), 256))
    lb = a["L0_ffn_lora_B"].transpose(0, 2, 1).reshape(2, LH, H)
    for j in range(2):
        c = zero.copy()
        c[:LH] = lb[j]
        chunks.append(c)
    chunks.append(zero)
    chunks += two(k_tiles(np.concatenate([a["L1_attn_up_w"], a["L1_attn_gate_w"]]), 256))
    chunks.append(np.ascontiguousarray(a["L1_attn_local_approx_output"].T))
    chunks += list(a["L1_attn_fuse_weight"].transpose(2, 1, 0))
    gw, uw, dw = a["L1_attn_ffn_gate_w"], a["L1_attn_ffn_up_w"], a["L1_attn_ffn_down_w"]
    for tiles in (range(0, 3), range(3, 7), range(7, 10)):
        chunks += glu(gw, uw, dw, tiles)
    w12 = a["L1_ffn_w12"]
    chunks += glu(w12[:H], w12[H:], a["L1_ffn_w3"], range(4))
    assert len(chunks) == CHUNK0[-1]

    inv = (1.0 / np.float32(1000000.0) ** (np.arange(0, HD, 2, dtype=np.float32) / np.float32(HD))).astype(np.float32)
    fr = np.outer(np.arange(S, dtype=np.float32), inv).astype(np.float32)
    cos, sin = np.cos(fr), np.sin(fr)
    cf = np.zeros((P, 247), np.float32)
    cf[:, 0:128] = np.eye(P)
    cf[:, 128:160] = np.concatenate([cos, cos], 1).reshape(2, P, HD).transpose(1, 0, 2).reshape(P, -1)
    cf[:, 160:176] = sin.reshape(2, P, HD // 2).transpose(1, 0, 2).reshape(P, -1)
    cf[:, 176:192] = -cf[:, 160:176]
    cf[:, 192:192 + NE] = np.arange(NE)
    for r in range(16):
        cf[r, 220 + r % 4] = 1.0
    cf[:, 224] = a["L1_attn_local_point"]
    cf[:, 225:231] = a["L1_attn_discount_factor"]
    cf[:, 231:239] = a["L1_ffn_b12"].reshape(8, P).T
    bf = ml_dtypes.bfloat16
    cb = np.zeros((P, 640), np.float32)
    cb[:, 0:128] = np.eye(P)
    up = np.triu(np.ones((P, P)), 1)
    cb[:, 128:256] = up * MASKED
    cb[:, 256:384] = up.T * MASKED
    for r in range(16):
        cb[r, 384 + 128 * ((r % 8) // 4):512 + 128 * ((r % 8) // 4)] = -1.0
    cb = cb.astype(bf)

    arrays = {
        "x": np.ascontiguousarray(x.reshape(B * S, H)),
        "w": np.ascontiguousarray(np.stack(chunks)),
        "cf": cf, "cb": cb,
        "bias": np.ascontiguousarray(np.broadcast_to(b_row, (P, b_row.size))),
    }
    nc = bacc.Bacc("TRN2", target_bir_lowering=False, num_devices=1)
    aps = [nc.dram_tensor(n, v.shape, mybir.dt.from_np(v.dtype), kind="ExternalInput").ap() for n, v in arrays.items()]
    out = nc.dram_tensor("out", [B * S, H], F32, kind="ExternalOutput").ap()
    build(nc, *aps, out)
    r = run(nc, [arrays], core_ids=[0])
    return r.results[0]["out"].reshape(B, S, H)
```

```python
from contextlib import ExitStack

import concourse.bass as bass
from concourse import mybir

P = 128
F32 = mybir.dt.float32
F32R = mybir.dt.float32r
BF16 = mybir.dt.bfloat16
FP16 = mybir.dt.float16
U32 = mybir.dt.uint32
ALU = mybir.AluOpType
ACT = mybir.ActivationFunctionType
AX_X = mybir.AxisListType.X

H = 512
KT = H // P
NG = 4
TG = 4
NKV, QPK, HD = 8, 4, 16
NPAIR = NKV // 2
STEPS = 2 * NPAIR
NE, RANK = 28, 8
LR = NE * RANK
LH = LR // 2
NORD = 6
THD = 2.5
EPS = 1e-5
MASKED = -1e30
SHIFT = 96.0
VC = 3 * HD + 1

PHASES = [("attn", 10, 0), ("moe", 9, 1), ("taylor", 9, 0), ("glu_a", 9, 1), ("glu_b", 12, 0), ("glu_c", 9, 1),
          ("glu_d", 12, 0)]
CHUNK0 = [sum(n for _, n, _ in PHASES[:i]) for i in range(len(PHASES) + 1)]


class Signal:

    def __init__(self, handle, per, credit=0, base=0):
        self.h, self.per, self.credit, self.base = handle, per, credit, base

    def done(self, it, n):
        return it * self.per + (self.base + self.credit + n + 1)

    def free(self, it, n, bufs):
        assert bufs <= self.credit
        return it * self.per + (self.base + self.credit + n + 1 - bufs)


def lone(eng):
    eng.nop(nofuse=True)


class Chain:

    def __init__(self, eng, handle):
        self.eng, self.h, self.total, self.it, self.per, self.n = eng, handle, 0, 0, 0, 0

    def link(self, ins):
        self.n += 1
        ins.then_inc(self.h, 1)
        self.eng.wait_ge(self.h, self.it * self.per + (self.total + self.n))

    def commit(self):
        self.total, self.n = self.total + self.n, 0

    def begin(self, it, last, per):
        if last:
            self.total, self.it, self.per = self.total + (NG - 1) * per, 0, 0
        else:
            self.it, self.per = it, per

    def end(self, last):
        assert last or self.n == self.per, ("chained in one iteration:", self.n, "expected", self.per)
        self.total, self.n = self.total + (self.n if last else 0), 0


def build(nc, x_in, w_in, cons_f, cons_b, biases, out):
    with ExitStack() as top:
        def sb(stack, name, shape, dt):
            return stack.enter_context(nc.sbuf_tensor(name, shape, dt))

        def sem(name):
            return top.enter_context(nc.semaphore(name))

        def signal(name, per, credit=0, base=0):
            s = Signal(sem(name), per, credit, base)
            if credit:
                credits.append(s)
            return s

        credits = []
        X = sb(top, "x_resident", [P, NG * TG, H], F32)
        W = [sb(top, "weights_even", [P, 12, 2, H], F32R), sb(top, "weights_odd", [P, 9, 2, H], F32R)]
        stage = sb(top, "weight_stage", [P, 2, H], F32)
        xn = sb(top, "x_normed", [P, 2, H], F32)
        xT = sb(top, "xT_hi_lo", [P, 2, KT, H], F32R)
        cf = sb(top, "constants_f32", list(cons_f.shape), F32)
        cb = sb(top, "constants_bf16", list(cons_b.shape), BF16)
        fst = sb(top, "front_stats", [P, 2, 6], F32)
        fmv = sb(top, "front_mean_var", [P, TG, 2], F32)
        frs = sb(top, "front_rstd", [P, 2, TG], F32)
        bst = sb(top, "back_stats", [P, 2, 6], F32)
        bmv = sb(top, "back_mean_var", [P, TG, 2], F32)
        brs = sb(top, "back_rstd", [P, 2, TG], F32)
        mhalf = sb(top, "minus_half", [P, TG], F32)
        xmv = sb(top, "x_mean_var", [P, NG * TG, 2], F32)
        xrs = sb(top, "x_rstd", [P, NG * TG, 1], F32)
        cfac = sb(top, "order_factor", [P, 8], F32)
        banks = [top.enter_context(nc.psum_tensor(f"bank{i}", [P, 512], F32)) for i in range(8)]
        Hb, Ob = banks[:4], banks[4:]

        identf = cf[:, 0:128]
        cos_t = cf[:, 128:160].rearrange("p (t d) -> p t d", t=2)
        sin_t = cf[:, 160:176].rearrange("p (t d) -> p t d", t=2)
        nsin_t = cf[:, 176:192].rearrange("p (t d) -> p t d", t=2)
        iota = cf[:, 192:192 + NE]
        lp = cf[:, 224:225]
        disc = cf[:, 225:231]
        b12 = cf[:, 231:239]
        zero8 = cf[:, 239:247]
        identb = cb[:, 0:128]
        mask_qk = cb[:, 128:256]
        mask_kq = cb[:, 256:384]
        sel = cb[:, 384:1408].rearrange("p (h k) -> p h k", k=P)

        s_x = [sem(f"s_x_loaded{g}") for g in range(NG)]
        s_cf, s_cb, s_bq, s_bd, s_bias3 = (sem(f"s_{n}_loaded")
                                           for n in ("cf", "cb", "bias_qkv", "bias_dense", "bias3"))
        s_init = sem("s_init")
        s_wdma = [sem("s_wdma_even"), sem("s_wdma_odd")]
        s_wsplit = [sem("s_wsplit_even"), sem("s_wsplit_odd")]
        s_wa = [sem(f"s_attn_weights{j}_loaded") for j in range(PHASES[0][1])]
        s_wa_hi, s_wa_lo = sem("s_attn_weights_hi"), sem("s_attn_weights_lo")
        s_out = sem("s_out")
        s_fmv, s_frs = sem("s_front_meanvar"), sem("s_front_rstd")
        s_xn, s_fhi, s_flo = sem("s_xn"), sem("s_front_hi"), sem("s_front_lo")
        s_xntr = sem("s_xn_transposed")
        chain_dve, chain_pool, chain_act = sem("chain_dve"), sem("chain_pool"), sem("chain_act")

        def front_signals(ph):
            b = NG * ph
            return dict(mv=Signal(s_fmv, 1, 0, b), rs=Signal(s_frs, 1, 0, b), xn=Signal(s_xn, 4, 0, 4 * b),
                        tr=Signal(s_xntr, 4, 2, 4 * b), hi=Signal(s_fhi, 4, 0, 4 * b), lo=Signal(s_flo, 4, 0, 4 * b))

        fr = [front_signals(ph) for ph in range(len(PHASES))]

        class Ph:
            pass

        phs = []
        for i, (name, nchunk, wb) in enumerate(PHASES):
            s = Ph()
            s.i, s.name, s.W = i, name, W[wb]
            s.updates = name in ("attn", "moe", "glu_c", "glu_d")
            nf = {"attn": 0, "moe": 2, "taylor": NORD + 1}.get(name, nchunk // 3)
            s.nf = nf
            s.o_ready = signal(f"{name}_o_ready", 4)
            s.o_free = signal(f"{name}_o_free", 4, 4)
            s.bmv = signal(f"{name}_bmv", 2 if name == "attn" else 1)
            s.brs = signal(f"{name}_brs", 2 if name == "attn" else 1)
            s.z_ready = signal(f"{name}_z_ready", 4)
            s.xupd = signal(f"{name}_xupd", 4, 4)
            s.pe_end = sem(f"{name}_pe_end")
            if name == "attn":
                s.qkv = signal("attn_qkv_ready", 8)
                s.evac = signal("attn_qkv_moved", 8)
                s.rope = signal("attn_rope", 4, 1)
                s.stack = signal("attn_stack", 16)
                s.tr = signal("attn_stack_transposed", 16, 4)
                s.tev = signal("attn_transposed_kept", 16)
                s.sq = signal("attn_scores_q", 48)
                s.red = signal("attn_reduced", 48)
                s.mp = signal("attn_max_parts", 8)
                s.mt = signal("attn_max_transposed", 8)
                s.rr = signal("attn_max_rows", 8)
                s.st = signal("attn_scores_k", 48)
                s.ex = signal("attn_exp", 48)
                s.pv = signal("attn_pv", 48, 4)
                s.plo = signal("attn_probs_lo", 48)
                s.vp = signal("attn_v_parts", 4, 2)
                s.otaken = signal("attn_out_taken", 4, 1)
                s.nrm = signal("attn_ctx_normed", 8, 1)
                s.ct = signal("attn_ctx_transposed", 4)
                s.chi = signal("attn_ctx_hi", 4)
                s.clo = signal("attn_ctx_lo", 4)
            else:
                s.in_ready = signal(f"{name}_in_ready", {"moe": 4, "taylor": 2}.get(name, 2 * nf))
                s.sg = signal(f"{name}_sg", 1 if name == "taylor" else nf)
                s.hf = signal(f"{name}_hf", nf, 2)
                s.hhi = signal(f"{name}_hhi", nf)
                s.hlo = signal(f"{name}_hlo", nf)
                s.hused = signal(f"{name}_hused", nf, 2)
                if name == "moe":
                    s.rt = signal("moe_route_diff", 1)
                    s.re = signal("moe_route_exp", 1)
                    s.hs = signal("moe_h_scaled", 4)
                    s.ht = signal("moe_h_transposed", 1)
            phs.append(s)

        def x_writer(ph):
            w = [p for p in phs[:ph] if p.updates]
            return w[-1] if w else None

        def wait_x(eng, ph, group, tile):
            w = x_writer(ph)
            if w is not None:
                eng.wait_ge(w.xupd.h, w.xupd.done(group, tile))

        def nxt(ph, it, last):
            return (ph + 1, 0) if last else (ph, it + 1)

        def front_stats(dve, ch, fph, fit, tiles=range(TG)):
            for t in tiles:
                wait_x(dve, fph, fit, t)
                lone(dve)
                ch.link(dve.bn_stats(fst[:, t % 2, :], X[:, fit * TG + t, :]))
                lone(dve)
                ins = dve.bn_aggr(fmv[:, t, :], fst[:, t % 2, :])
            if t == TG - 1:
                ins.then_inc(fr[fph]["mv"].h, 1)

        def front_norm(dve, fph, fit, tiles):
            f = fr[fph]
            for t in tiles:
                if t == 0:
                    dve.wait_ge(f["rs"].h, f["rs"].done(fit, 0))
                dve.wait_ge(f["tr"].h, f["tr"].free(fit, t, 2))
                dve.tensor_scalar(xn[:, t % 2, :], X[:, fit * TG + t, :], fmv[:, t, 0:1], frs[:, 1, t:t + 1],
                                  ALU.subtract, ALU.mult).then_inc(f["xn"].h, 1)

        def front_rstd(pool, ch, fph, fit):
            f = fr[fph]
            pool.wait_ge(f["mv"].h, f["mv"].done(fit, 0))
            lone(pool)
            ch.link(pool.tensor_scalar(frs[:, 0, :], fmv[:, :, 1], 1.0, EPS, ALU.mult, ALU.add))
            pool.tensor_tensor(frs[:, 1, :], frs[:, 0, :], mhalf[:, :], ALU.pow).then_inc(f["rs"].h, 1)

        def front_transpose(pe, fph, fit):
            f = fr[fph]
            for t in range(TG):
                pe.wait_ge(f["xn"].h, f["xn"].done(fit, t))
                for k in range(KT):
                    ins = pe.transpose(Hb[k][:, t * P:(t + 1) * P], xn[:, t % 2, k * P:(k + 1) * P], identf)
                ins.then_inc(f["tr"].h, 1)

        def front_hi(act, fph, fit):
            f = fr[fph]
            act.wait_ge(f["tr"].h, f["tr"].done(fit, 3))
            for k in range(KT):
                act.activation(xT[:, 0, k, :], Hb[k][:, :], ACT.Copy).then_inc(f["hi"].h, 1)

        def front_lo(dve, fph, fit):
            f = fr[fph]
            for k in range(KT):
                dve.wait_ge(f["hi"].h, f["hi"].done(fit, k))
                dve.tensor_tensor(xT[:, 1, k, :], Hb[k][:, :], xT[:, 0, k, :].bitcast(F32),
                                  ALU.subtract).then_inc(f["lo"].h, 1)

        PASSES = ((0, 0), (0, 1), (1, 0))

        def tokens_by_weights(pe, bank, cols, t, chunk_of, first=True, final=True):
            for k in range(KT):
                w = chunk_of(k)
                for n, (a, b) in enumerate(PASSES):
                    ins = pe.matmul(bank[:, 0:cols], xT[:, b, k, t * P:(t + 1) * P], w[a],
                                    start=first and k == 0 and n == 0, stop=final and k == KT - 1 and n == 2)
            return ins

        def features(pe, bank, chunk_of):
            for k in range(KT):
                w = chunk_of(k)
                for n, (a, b) in enumerate(PASSES):
                    ins = pe.matmul(bank[:, :], w[a], xT[:, b, k, :], start=k == 0 and n == 0,
                                    stop=k == KT - 1 and n == 2)
            return ins

        def weights_wait(pe, ph):
            for s in range(2):
                pe.wait_ge(s_wsplit[s], wcount(ph + 1, s) + 1)

        def wper(ph):
            return PHASES[ph][1] // 3

        def wslot(per, s):
            return (per + 1 - s) // 2

        def wcount(ph, s):
            return sum(3 * wslot(wper(p), s) for p in range(1, ph))

        def w_load(sp, ph, it):
            per = wper(ph)
            for j in range(per):
                s, n = j % 2, j // 2
                sp.wait_ge(s_wsplit[s], it * wslot(per, s) + (wcount(ph, s) + n + 1))
                sp.dma_start(stage[:, s, :], w_in[it * per + (CHUNK0[ph] + j)]).then_inc(s_wdma[s], 16)

        def w_split(pool, ch, ph, it, js=None):
            per = wper(ph)
            for j in range(per) if js is None else js:
                s, n = j % 2, j // 2
                now = it * (16 * wslot(per, s)) + 16 * (wcount(ph, s) + n + 1)
                hi, lo = (W[PHASES[ph][2]][:, it * per + j, a, :] for a in range(2))
                pool.wait_ge(s_wdma[s], now)
                lone(pool)
                ch.link(pool.tensor_copy(hi, stage[:, s, :]))
                pool.tensor_tensor(lo, stage[:, s, :], hi.bitcast(F32), ALU.subtract).then_inc(s_wsplit[s], 1)

        def back_stats(dve, ch, s, it, tiles, n, src):
            for t in tiles:
                lone(dve)
                ch.link(dve.bn_stats(bst[:, t % 2, :], src(t)))
                lone(dve)
                ins = dve.bn_aggr(bmv[:, t, :], bst[:, t % 2, :])
            ins.then_inc(s.bmv.h, 1)

        def back_rstd(pool, ch, s, it, tiles, n):
            a, b = tiles[0], tiles[-1] + 1
            pool.wait_ge(s.bmv.h, s.bmv.done(it, n))
            lone(pool)
            ch.link(pool.tensor_scalar(brs[:, 0, a:b], bmv[:, a:b, 1], 1.0, EPS, ALU.mult, ALU.add))
            pool.tensor_tensor(brs[:, 1, a:b], brs[:, 0, a:b], mhalf[:, a:b], ALU.pow).then_inc(s.brs.h, 1)

        def back_norm(dve, s, it, tiles, n, src, dst):
            dve.wait_ge(s.brs.h, s.brs.done(it, n))
            for t in tiles:
                ins = dve.tensor_scalar(dst(t), src(t), bmv[:, t, 0:1], brs[:, 1, t:t + 1], ALU.subtract, ALU.mult)
                ins.then_inc(s.z_ready.h, 1)

        def back_update(pool, s, it, tiles, z):
            for t in tiles:
                x = X[:, it * TG + t, :]
                pool.wait_ge(s.z_ready.h, s.z_ready.done(it, t))
                pool.tensor_tensor(x, x, z(t), ALU.add).then_inc(s.xupd.h, 1)

        def groups(eng, body):
            with eng.Fori(0, NG - 1) as it:
                body(it, False)
            body(NG - 1, True)

        with ExitStack() as mem:
            s = phs[0]
            WA = s.W
            bq = sb(mem, "bias_qkv", [P, 768], F32)
            bd = sb(mem, "bias_dense", [P, H], F32)
            xt = sb(mem, "x_tile_transposed_hi_lo", [P, 2, KT, P], F32R)
            qk = sb(mem, "qk_roped", [P, TG, 640], F32)
            vf = sb(mem, "v_full", [P, 2, P], F32)
            vr = sb(mem, "v_rest", [P, P], F32)
            vp = sb(mem, "v_parts_and_one", [P, TG, NKV, VC], BF16)
            rtmp = sb(mem, "rope_tmp", [P, 640], F32)
            qst = sb(mem, "q_stack", [P, 2, 2, QPK, 2, 64], F32R)
            kst = sb(mem, "k_stack", [P, 2, 2, 2, 64], F32R)
            pf = sb(mem, "probs_full_then_lo", [P, 4, H], F32)
            ph = sb(mem, "probs_hi", [P, 4, H], FP16)
            RR = sb(mem, "max_rows", [P, 2, 2 * P], BF16)
            mx = sb(mem, "max_q", [P, 2, 2, 8], F32)
            mp = sb(mem, "max_parts", [P, 2, 2, 16], BF16)
            rden = sb(mem, "rden", [P, 16], F32)
            csum = sb(mem, "ctx_sum", [P, 2, P], F32)
            ctx = sb(mem, "ctx", [P, TG, H], F32)
            zA = sb(mem, "z_attn", [P, 2, H], F32)
            ctxT = WA[:, 10, :, :].rearrange("p a (c q) -> p a c q", q=P)
            QT = [xT[:, n // 2, 2 * (n % 2):2 * (n % 2) + 2, :] for n in range(4)]
            KTr = [WA[:, 11, n // 2, 256 * (n % 2):256 * (n % 2) + 256].rearrange("p (t k) -> p t k", t=2)
                   for n in range(4)]
            pl = pf[:, :, 0:H // 2].bitcast(FP16)
            Tb, KTb, PVb = Ob[0], Ob[1], Ob[2:4]
            mT = KTb[:, 256:384].bitcast(BF16)
            def first_weights(j):
                return (ctx, pf, zA)[j // 4][:, j % 4, :]

            def first_hi(act, chunks):
                for j in chunks:
                    act.wait_ge(s_wa[j], 16)
                    act.activation(W[0][:, j, 0, :], first_weights(j), ACT.Copy).then_inc(s_wa_hi, 1)

            def first_lo(dve, chunks):
                for j in chunks:
                    dve.wait_ge(s_wa_hi, j + 1)
                    dve.tensor_tensor(W[0][:, j, 1, :], first_weights(j), W[0][:, j, 0, :].bitcast(F32),
                                      ALU.subtract).then_inc(s_wa_lo, 1)

            BLOCKS = ((0, 0), (0, 1), (1, 1))

            def step_order(i, feed, prev):
                j, a, b = i % 4, 2 * (i // 4) + 2, 2 * (i // 4) + 3
                at = {(0, "v1"): ("f", a), (0, "k3"): ("wq", a), (0, "v3"): ("wq+", a), (0, "k5"): ("wk", a),
                      (0, "v5"): ("f", b), (1, "v1"): ("wq", b), (1, "v2"): ("wq+", b),
                      (1, "v4"): ("wk", b)} if feed else {}
                if prev:
                    at.update({(2, "q0"): ("c", a - 4), (2, "k2"): ("d", a - 4), (2, "v2"): ("d+", a - 4),
                               (3, "q0"): ("c", a - 3), (3, "k2"): ("d", a - 3), (3, "v2"): ("d+", a - 3)})
                out = []
                for step in "q0 k0 v0 q1 k1 v1 q2 k2 v2 q3 k3 q4 v3 t0 k4 v4 q5 t1 k5 v5".split():
                    kind, n = step[0], int(step[1])
                    if kind == "q" and (feed or j < 3):
                        out.append(("q", 6 * (i + 1) + n))
                    elif kind == "k":
                        out.append(("k", 6 * i + n))
                    elif kind == "v" and (i > 0 or n > 2):
                        out.append(("v", 6 * i - 3 + n))
                    elif kind == "t" and (feed or j < 2):
                        out.append(("t", 2 * (i + 2) + n))
                    out += [at[(j, step)]] if (j, step) in at else []
                return out

            PER = {"q": 48, "k": 48, "f": 4, "wq": 4, "wk": 4}
            ring = [(kind, n) for n in range(2) for kind in ("f", "wq", "wk")] + [("q", n) for n in range(6)]
            for i in range(STEPS * NG):
                ring += [x for x in step_order(i, i < STEPS * NG - 4, i > 3) if x[0] in PER]
            use_of = {r: u for u, r in enumerate(ring)}

            def use(it, kind, n):
                def at(g):
                    u = use_of[(kind, n + PER[kind] * g)]
                    if u < 4:
                        return u, None
                    k, m = ring[u - 4]
                    return u % 4, (k, m - PER[k] * g)
                if isinstance(it, int):
                    return at(it)
                assert at(0) == at(1) == at(2)
                return at(1)

            def ring_bank(it, kind, n):
                return Hb[use(it, kind, n)[0]]

            def ring_wait(pe, it, kind, n):
                b, before = use(it, kind, n)
                if before is not None:
                    k, m = before
                    if k == "q":
                        pe.wait_ge(s.red.h, s.red.done(it, m))
                    elif k == "k":
                        pe.wait_ge(s.ex.h, s.ex.done(it, m))
                    elif k == "f":
                        pe.wait_ge(fr[0]["lo"].h, fr[0]["lo"].done(it, m))
                    else:
                        e = 2 * m + (k == "wk")
                        pe.wait_ge(s.evac.h, s.evac.done(it, e))
                return Hb[b]

            def pe_front(pe, it, n):
                bank = ring_wait(pe, it, "f", n)
                pe.wait_ge(fr[0]["xn"].h, fr[0]["xn"].done(it, n))
                for k in range(KT):
                    ins = pe.transpose(bank[:, k * P:(k + 1) * P], xn[:, n % 2, k * P:(k + 1) * P], identf)
                ins.then_inc(fr[0]["tr"].h, 1)

            def pe_project(pe, it, kind, n):
                bank = ring_bank(it, "wq", n) if kind == "wq+" else ring_wait(pe, it, kind, n)
                if kind == "wq":
                    pe.wait_ge(fr[0]["lo"].h, fr[0]["lo"].done(it, n))
                for k in {"wq": (0, 1), "wq+": (2, 3), "wk": range(KT)}[kind]:
                    for x, (a, b) in enumerate(PASSES):
                        w = WA[:, 4 + k // 2, a, 256 * (k % 2):256 * (k % 2) + 256] if kind == "wk" else WA[:, k, a, :]
                        ins = pe.matmul(bank[:, 0:256 if kind == "wk" else 512], xt[:, b, k, :], w,
                                        start=k == 0 and x == 0, stop=k == KT - 1 and x == 2, skip_group_check=True)
                if kind != "wq":
                    ins.then_inc(s.qkv.h, 1)

            def pe_transposes(pe, it, n):
                i, t = n // 2, n % 2
                pe.wait_ge(s.stack.h, s.stack.done(it, n))
                if n:
                    pe.wait_ge(s.tev.h, s.tev.done(it, n - 1))
                h = (i - 2) // 4
                if t == 0 and (i - 2) % 4 in (2, 3) and h > 0:
                    pe.wait_ge(s.otaken.h, s.otaken.done(it, 2 * h - 4 + (i - 2) % 4))
                for j in range(QPK):
                    pe.transpose(Tb[:, j * P:(j + 1) * P],
                                 qst[:, i % 2, t, j, :, :].rearrange("p a c -> p (a c)").bitcast(F32), identf)
                pe.transpose(KTb[:, t * P:(t + 1) * P],
                             kst[:, i % 2, t, :, :].rearrange("p a c -> p (a c)").bitcast(F32),
                             identf).then_inc(s.tr.h, 1)

            def pe_scores_q(pe, it, m):
                i, ab, n = m // 6, m // 3 % 2, m % 3
                rows = slice(64 * ab, 64 * ab + 64)
                qt, j0, nk = ((0, 0, 1), (1, 0, 2), (1, 2, 2))[n]
                if m % 6 < 2:
                    pe.wait_ge(s.tev.h, s.tev.done(it, 2 * i + m % 6))
                bank = ring_wait(pe, it, "q", m)
                nj = QPK // nk
                v = bank[:, :].rearrange("p (j k) -> p j k", j=nj)
                pe.matmul(v[:, :, (nk - 1) * P:nk * P], identb, mask_qk.unsqueeze(1).broadcast_to([P, nj, P]),
                          start=True, stop=False, skip_group_check=True)
                for j in range(nj):
                    ins = pe.matmul(v[:, j, :], QT[i % 4][rows, qt, (j0 + j) * P:(j0 + j + 1) * P],
                                    KTr[i % 4][rows, 0:nk, :].rearrange("p t k -> p (t k)"),
                                    start=False, stop=j == nj - 1, skip_group_check=True)
                ins.then_inc(s.sq.h, 1)

            def pe_max_rows(pe, it, i, last_pair):
                pe.wait_ge(s.mp.h, s.mp.done(it, i))
                pe.wait_ge(s.tev.h, s.tev.done(it, 2 * last_pair + 1))
                if i >= 1:
                    pe.wait_ge(s.rr.h, s.rr.done(it, i - 1))
                for qt in range(2):
                    ins = pe.transpose(mT[0:16, qt * P:(qt + 1) * P], mp[:, i % 2, qt, :], identb)
                ins.then_inc(s.mt.h, 1)

            def pe_scores_k(pe, it, m):
                i, ab = m // 6, m // 3 % 2
                rows = slice(64 * ab, 64 * ab + 64)
                kt, qt = BLOCKS[m % 3]
                if m % 6 == 0:
                    pe.wait_ge(s.rr.h, s.rr.done(it, i))
                bank = ring_wait(pe, it, "k", m)
                if kt == qt:
                    pe.matmul(bank[:, :].rearrange("p (j q) -> p j q", j=QPK), identb,
                              mask_kq.unsqueeze(1).broadcast_to([P, QPK, P]), start=True, stop=False,
                              skip_group_check=True)
                pe.matmul(bank[:, :], KTr[i % 4][rows, kt, :], QT[i % 4][rows, qt, :], start=kt != qt, stop=False,
                          skip_group_check=True)
                for j in range(QPK):
                    ins = pe.matmul(bank[:, j * P:(j + 1) * P], sel[0:16, 4 * ab + j, :],
                                    RR[0:16, i % 2, qt * P:(qt + 1) * P], start=False, stop=j == QPK - 1,
                                    skip_group_check=True)
                ins.then_inc(s.st.h, 1)

            def pe_pv(pe, it, m):
                i, ab = m // 6, m // 3 % 2
                kt, qt = BLOCKS[m % 3]
                g, tile = 2 * (i % NPAIR) + ab, (2 * (i // NPAIR) + kt) % TG
                if m % 6 == 0:
                    pe.wait_ge(s.nrm.h, s.nrm.free(it, i, 1))
                if m % 24 == 0:
                    pe.wait_ge(s.vp.h, s.vp.done(it, 2 * (m // 24) + 1))
                pe.wait_ge(s.plo.h, s.plo.done(it, m))
                v = PVb[qt][:, 0:8 * VC].rearrange("p (g j d) -> p g j d", g=2, j=QPK)
                for j in range(QPK):
                    for x, half in enumerate((ph, pl)):
                        ins = pe.matmul(v[:, ab, j, :], half[:, m % 4, j * P:(j + 1) * P], vp[:, tile, g, :],
                                        start=m % 6 == qt and j == 0 and x == 0, stop=kt == qt and x == 1,
                                        skip_group_check=True)
                ins.then_inc(s.pv.h, 1)

            def pe_ctx_transpose(pe, it, n, last_pair):
                pe.wait_ge(s.nrm.h, s.nrm.done(it, NPAIR * (n // 2) + NPAIR - 1))
                pe.wait_ge(s.tev.h, s.tev.done(it, 2 * last_pair + 1))
                pe.wait_ge(s.otaken.h, s.otaken.free(it, n, 1))
                for c in range(KT):
                    ins = pe.transpose(Tb[:, c * P:(c + 1) * P], ctx[:, n % TG, c * P:(c + 1) * P], identf)
                ins.then_inc(s.ct.h, 1)

            def pe_dense(pe, it, n, part):
                pe.wait_ge(s.clo.h, s.clo.done(it, n))
                for c in (2 * part, 2 * part + 1):
                    for k, (a, x) in enumerate(PASSES):
                        ins = pe.matmul(Tb[:, :], ctxT[:, x, c, :], WA[:, 6 + c, a, :],
                                        start=c == 0 and k == 0, stop=c == KT - 1 and k == 2,
                                        skip_group_check=True)
                if part == 1:
                    ins.then_inc(s.o_ready.h, 1)

            def pe_attention(pe):
                pe.wait_ge(s_cf, 16)
                pe.wait_ge(s_init, 2)

                def steps(it, first, feed=True, prev=True):
                    for i in range(first, first + 4):
                        final = 1000 if feed else first + 3
                        pe_max_rows(pe, it, i, min(i + 1, final))
                        for kind, n in step_order(i, feed, prev):
                            if kind == "q":
                                pe_scores_q(pe, it, n)
                            elif kind == "k":
                                pe_scores_k(pe, it, n)
                            elif kind == "v":
                                pe_pv(pe, it, n)
                            elif kind == "t":
                                pe_transposes(pe, it, n)
                            elif kind == "f":
                                pe_front(pe, it, n)
                            elif kind in ("wq", "wq+", "wk"):
                                pe_project(pe, it, kind, n)
                            elif kind == "c":
                                pe_ctx_transpose(pe, it, n, min(i + 1, final))
                            else:
                                pe_dense(pe, it, n, int(kind == "d+"))

                for n in range(2):
                    pe_front(pe, 0, n)
                    pe.wait_ge(s_wa_lo, 6)
                    pe_project(pe, 0, "wq", n)
                    pe_project(pe, 0, "wq+", n)
                    pe_project(pe, 0, "wk", n)
                for n in range(4):
                    pe_transposes(pe, 0, n)
                pe.wait_ge(s_cb, 16)
                pe.wait_ge(s_wa_lo, PHASES[0][1])
                for m in range(6):
                    pe_scores_q(pe, 0, m)
                steps(0, 0, prev=False)
                with pe.Fori(0, NG - 1) as it:
                    steps(it, 4)
                    steps(it, 8)
                it = NG - 1
                steps(it, 4, feed=False)
                for n in range(3):
                    pe_pv(pe, it, 6 * STEPS - 3 + n)
                for n in (2, 3):
                    pe_ctx_transpose(pe, it, n, STEPS - 1)
                    if n == 2:
                        front_transpose(pe, 1, 0)
                    pe_dense(pe, it, n, 0)
                    pe_dense(pe, it, n, 1)
                pe.wait_ge(s.otaken.h, s.otaken.done(it, 3))
                pe.sem_inc(s.pe_end, 1)

            def act_attention(act):
                def front(it, n):
                    f = fr[0]
                    act.wait_ge(f["tr"].h, f["tr"].done(it, n))
                    if n:
                        act.wait_ge(s.qkv.h, s.qkv.done(it, 2 * n - 1))
                    act.activation(xt[:, 0, :, :].rearrange("p k q -> p (k q)"), ring_bank(it, "f", n)[:, :],
                                   ACT.Copy).then_inc(f["hi"].h, 1)

                def keep(it, n):
                    i, t = n // 2, n % 2
                    act.wait_ge(s.tr.h, s.tr.done(it, n))
                    act.activation(QT[i % 4][:, t, :], Tb[:, :], ACT.Copy)
                    act.activation(KTr[i % 4][:, t, :], KTb[:, t * P:(t + 1) * P], ACT.Copy).then_inc(s.tev.h, 1)

                def max_rows(it, i):
                    act.wait_ge(s.mt.h, s.mt.done(it, i))
                    act.activation(RR[0:16, i % 2, :], mT[0:16, :], ACT.Copy).then_inc(s.rr.h, 1)

                def exps(it, m):
                    bank = ring_bank(it, "k", m)
                    act.wait_ge(s.st.h, s.st.done(it, m))
                    act.wait_ge(s.pv.h, s.pv.free(it, m, 4))
                    act.activation(ph[:, m % 4, :], bank[:, :], ACT.Exp, scale=1.0 / HD)
                    act.activation(pf[:, m % 4, :], bank[:, :], ACT.Exp, scale=1.0 / HD).then_inc(s.ex.h, 1)

                def ctx_hi(it, n):
                    act.wait_ge(s.ct.h, s.ct.done(it, n))
                    act.activation(ctxT[:, 0, :, :].rearrange("p c q -> p (c q)"), Tb[:, :],
                                   ACT.Copy).then_inc(s.chi.h, 1)

                def steps(it, first, feed=True, prev=True):
                    for i in range(first, first + 4):
                        max_rows(it, i)
                        for kind, n in step_order(i, feed, prev):
                            if kind == "k":
                                exps(it, n)
                            elif kind == "t":
                                keep(it, n)
                            elif kind == "f":
                                front(it, n)
                            elif kind == "c":
                                ctx_hi(it, n)

                first_hi(act, range(6))
                front(0, 0)
                first_hi(act, range(6, PHASES[0][1]))
                act.wait_ge(chain_act, 1)
                act.activation(cfac[:, 0:NORD], cfac[:, 0:NORD], ACT.Exp).then_inc(chain_act, 1)
                front(0, 1)
                for n in range(4):
                    keep(0, n)
                steps(0, 0, prev=False)
                with act.Fori(0, NG - 1) as it:
                    steps(it, 4)
                    steps(it, 8)
                it = NG - 1
                steps(it, 4, feed=False)
                ctx_hi(it, 2)
                front_hi(act, 1, 0)
                ctx_hi(it, 3)

            def dve_attention(dve, ch):
                dve.memset(vp[:, :, :, :], 1.0).then_inc(s_init, 1)

                def stats(g):
                    dve.wait_ge(s_x[g], 16)
                    for t in range(g * TG, (g + 1) * TG):
                        lone(dve)
                        ch.link(dve.bn_stats(fst[:, t % 2, :], X[:, t, :]))
                        lone(dve)
                        ins = dve.bn_aggr(xmv[:, t, :], fst[:, t % 2, :])
                    ins.then_inc(fr[0]["mv"].h, 1)

                def front_lo_tile(it, n):
                    f = fr[0]
                    dve.wait_ge(f["hi"].h, f["hi"].done(it, n))
                    dve.tensor_tensor(xt[:, 1, :, :].rearrange("p k q -> p (k q)"), ring_bank(it, "f", n)[:, :],
                                      xt[:, 0, :, :].rearrange("p k q -> p (k q)").bitcast(F32),
                                      ALU.subtract).then_inc(f["lo"].h, 1)

                def evac_q(it, n):
                    dve.wait_ge(s.qkv.h, s.qkv.done(it, 2 * n))
                    if n >= TG:
                        dve.wait_ge(s.stack.h, s.stack.done(it, 2 * (4 * ((n - TG) // 2) + 3) + n % 2))
                    dve.tensor_tensor(qk[:, n % TG, 0:512], ring_bank(it, "wq", n)[:, :], bq[:, 0:512],
                                      ALU.add).then_inc(s.evac.h, 1)

                def evac_kv(it, n):
                    bank = ring_bank(it, "wk", n)
                    dve.wait_ge(s.qkv.h, s.qkv.done(it, 2 * n + 1))
                    dve.wait_ge(s.vp.h, s.vp.free(it, n, 2))
                    dve.tensor_tensor(qk[:, n % TG, 512:640], bank[:, 0:128], bq[:, 512:640], ALU.add)
                    dve.tensor_tensor(vf[:, n % 2, :], bank[:, 128:256], bq[:, 640:768], ALU.add).then_inc(s.evac.h, 1)

                def rope(it, n):
                    z = qk[:, n % TG, :].rearrange("p (h d) -> p h d", d=HD)
                    r = rtmp[:, :].rearrange("p (h d) -> p h d", d=HD)
                    nh, hf = 640 // HD, HD // 2
                    def table(a):
                        return a[:, n % 2, :].unsqueeze(1).broadcast_to([P, nh, a.shape[2]])
                    dve.wait_ge(s.evac.h, s.evac.done(it, 2 * n + 1))
                    dve.wait_ge(s.rope.h, s.rope.free(it, n, 1))
                    dve.tensor_tensor(r[:, :, 0:hf], z[:, :, hf:HD], table(nsin_t), ALU.mult)
                    ch.link(dve.tensor_tensor(r[:, :, hf:HD], z[:, :, 0:hf], table(sin_t), ALU.mult))
                    ch.link(dve.tensor_tensor(z, z, table(cos_t), ALU.mult))
                    dve.tensor_tensor(z, z, r, ALU.add).then_inc(s.rope.h, 1)

                def maxima(it, m):
                    i, ab, n = m // 6, m // 3 % 2, m % 3
                    qt, j0, nj = ((0, 0, 4), (1, 0, 2), (1, 2, 2))[n]
                    dve.wait_ge(s.sq.h, s.sq.done(it, m))
                    c = 4 * ab + j0
                    dve.tensor_reduce(mx[:, i % 2, qt, c:c + nj],
                                      ring_bank(it, "q", m)[:, :].rearrange("p (j k) -> p j k", j=nj),
                                      AX_X, ALU.max).then_inc(s.red.h, 1)

                def max_parts(it, i):
                    m = mp[:, i % 2, :, :]
                    dve.wait_ge(s.red.h, s.red.done(it, 6 * i + 5))
                    ch.link(dve.tensor_scalar(m[:, :, 0:8], mx[:, i % 2, :, :], SHIFT, None, ALU.subtract))
                    dve.scalar_tensor_tensor(out=m[:, :, 8:16], in0=mx[:, i % 2, :, :], scalar=SHIFT,
                                             in1=m[:, :, 0:8], op0=ALU.subtract, op1=ALU.subtract).then_inc(s.mp.h, 1)

                def probs_lo(it, m):
                    dve.wait_ge(s.ex.h, s.ex.done(it, m))
                    dve.tensor_tensor(pl[:, m % 4, :], pf[:, m % 4, :], ph[:, m % 4, :],
                                      ALU.subtract).then_inc(s.plo.h, 1)

                def normalise(it, i):
                    p = i % NPAIR
                    dve.wait_ge(s.pv.h, s.pv.done(it, 6 * i + 5))
                    for t in range(2):
                        v = PVb[t][:, 0:8 * VC].rearrange("p (h d) -> p h d", d=VC)
                        dve.reciprocal(rden[:, 8 * t:8 * t + 8], v[:, :, 3 * HD])
                        ins = dve.tensor_reduce(csum[:, t, :].rearrange("p (h d) -> p h d", d=HD),
                                                v[:, :, 0:3 * HD].rearrange("p h (x d) -> p h d x", d=HD),
                                                AX_X, ALU.add)
                    ch.link(ins)
                    for t in range(2):
                        ins = dve.tensor_tensor(
                            ctx[:, (2 * (i // NPAIR) + t) % TG, p * 128:(p + 1) * 128].rearrange(
                                "p (g d) -> p g d", d=HD),
                            csum[:, t, :].rearrange("p (h d) -> p h d", d=HD),
                            rden[:, 8 * t:8 * t + 8].unsqueeze(2).broadcast_to([P, 8, HD]), ALU.mult)
                    ins.then_inc(s.nrm.h, 1)

                def ctx_lo(it, n):
                    dve.wait_ge(s.chi.h, s.chi.done(it, n))
                    dve.tensor_tensor(ctxT[:, 1, :, :].rearrange("p c q -> p (c q)"), Tb[:, :],
                                      ctxT[:, 0, :, :].rearrange("p c q -> p (c q)").bitcast(F32),
                                      ALU.subtract).then_inc(s.clo.h, 1)

                def take(it, n):
                    dve.wait_ge(s.o_ready.h, s.o_ready.done(it, n))
                    dve.wait_ge(s.xupd.h, s.xupd.free(it, n, 2))
                    dve.tensor_tensor(zA[:, n % 2, :], Tb[:, :], bd[:, :], ALU.add).then_inc(s.otaken.h, 1)

                def back(it, b):
                    dve.wait_ge(s.otaken.h, s.otaken.done(it, 2 * b + 1))
                    for t in range(2):
                        lone(dve)
                        ch.link(dve.bn_stats(bst[:, t, :], zA[:, t, :]))
                        lone(dve)
                        ins = dve.bn_aggr(bmv[:, 2 * (b % 2) + t, :], bst[:, t, :])
                    ins.then_inc(s.bmv.h, 1)

                def back_z(it, b):
                    dve.wait_ge(s.brs.h, s.brs.done(it, b))
                    for t in range(2):
                        c = 2 * (b % 2) + t
                        dve.tensor_scalar(zA[:, t, :], zA[:, t, :], bmv[:, c, 0:1], brs[:, 1, c:c + 1],
                                          ALU.subtract, ALU.mult).then_inc(s.z_ready.h, 1)

                def steps(it, first, feed=True, prev=True):
                    a, b, before = first // 2 + 2, first // 2 + 3, first // 4 - 1
                    for i in range(first, first + 4):
                        j = i % 4
                        q = feed or j < 3
                        for n in range(6):
                            if n == 3 and i:
                                normalise(it, i - 1)
                            if q:
                                maxima(it, 6 * (i + 1) + n)
                                if n == 5:
                                    max_parts(it, i + 1)
                            if n == 3 and prev and j >= 2:
                                take(it, a - 6 + j)
                            m = 6 * i - 2 + n
                            if m >= 0:
                                probs_lo(it, m)
                            if feed and (j, n) == (0, 1):
                                front_lo_tile(it, a)
                            if feed and (j, n) == (0, 4):
                                evac_q(it, a)
                            if feed and (j, n) == (0, 5):
                                evac_kv(it, a)
                            if feed and (j, n) == (1, 0):
                                front_lo_tile(it, b)
                            if feed and (j, n) == (1, 2):
                                evac_q(it, b)
                            if feed and (j, n) == (1, 4):
                                evac_kv(it, b)
                            if feed and j == 1 and n == 1:
                                rope(it, a)
                            if prev and j >= 2 and n == 0:
                                ctx_lo(it, a - 6 + j)
                            if feed and j == 2 and n == 1:
                                rope(it, b)
                            if feed and (j, n) == (0, 0):
                                norm(dve, it, a)
                                norm(dve, it, b)
                            if prev and (j, n) == (3, 3):
                                back(it, before)
                        if prev and j == 3:
                            back_z(it, before)
                        if not feed and j == 2:
                            front_stats(dve, ch, 1, 0)
                        if not feed and j == 3:
                            front_norm(dve, 1, 0, (0, 1))

                stats(0)
                for n in range(2):
                    norm(dve, 0, n)
                first_lo(dve, range(6))
                front_lo_tile(0, 0)
                first_lo(dve, range(6, PHASES[0][1]))
                dve.wait_ge(s_bq, 16)
                evac_q(0, 0)
                evac_kv(0, 0)
                front_lo_tile(0, 1)
                rope(0, 0)
                stats(1)
                evac_q(0, 1)
                evac_kv(0, 1)
                rope(0, 1)
                stats(2)
                dve.wait_ge(s_bd, 16)
                for m in range(6):
                    maxima(0, m)
                max_parts(0, 0)
                stats(3)
                steps(0, 0, prev=False)
                ch.commit()
                with dve.Fori(0, NG - 1) as it:
                    ch.begin(it, False, DVE_CHAIN_ATTN)
                    steps(it, 4)
                    steps(it, 8)
                    ch.end(False)
                it = NG - 1
                ch.begin(it, True, DVE_CHAIN_ATTN)
                steps(it, 4, feed=False)
                probs_lo(it, 6 * STEPS - 2)
                probs_lo(it, 6 * STEPS - 1)
                normalise(it, STEPS - 1)
                ctx_lo(it, 2)
                front_norm(dve, 1, 0, (2, 3))
                front_lo(dve, 1, 0)
                take(it, 2)
                ctx_lo(it, 3)
                take(it, 3)
                back(it, 1)
                back_z(it, 1)
                ch.end(True)

            def norm(dve, it, n):
                f = fr[0]
                dve.wait_ge(f["rs"].h, f["rs"].done(it, n // TG))
                dve.wait_ge(f["tr"].h, f["tr"].free(it, n, 2))
                dve.tensor_scalar(xn[:, n % 2, :], X[:, it * TG + n, :], xmv[:, it * TG + n, 0:1], xrs[:, it * TG + n, :],
                                  ALU.subtract, ALU.mult).then_inc(f["xn"].h, 1)

            def pool_attention(pool, ch):
                ch.link(pool.memset(mhalf[:, :], -0.5))
                ch.link(pool.memset(qst[:, :, :, :, :, :].bitcast(F32), 0.0))
                pool.memset(kst[:, :, :, :, :].bitcast(F32), 0.0).then_inc(s_init, 1)
                for c in credits:
                    pool.sem_inc(c.h, c.credit)
                pool.sem_inc(s_xntr, 2)
                pool.wait_ge(s_init, 2)
                rstd(pool, ch, 0)
                for h in s_wsplit:
                    pool.sem_inc(h, 1)

                def stack(it, i, t):
                    n, p = 2 * (i // NPAIR) + t, i % NPAIR
                    pool.wait_ge(s.rope.h, s.rope.done(it, n))
                    pool.wait_ge(s.tr.h, s.tr.free(it, 2 * i + t, 4))
                    lone(pool)
                    zq = qk[:, n % TG, 128 * p:128 * p + 128]
                    zk = qk[:, n % TG, 512 + 32 * p:544 + 32 * p].rearrange("p (a d) -> p a d", a=2)
                    kk = kst[:, i % 2, t, :, :]
                    for ab in range(2):
                        z = zq[:, 64 * ab:64 * ab + 64].rearrange("p (j d) -> p j d", j=QPK)
                        q = qst[:, i % 2, t, :, ab, :]
                        pool.tensor_copy(q[:, :, 0:16], z)
                        pool.tensor_copy(q[:, :, 16:32], z)
                    pool.tensor_copy(kk[:, :, 0:16], zk)
                    ch.link(pool.tensor_copy(kk[:, :, 32:48], zk))
                    for ab in range(2):
                        z = zq[:, 64 * ab:64 * ab + 64].rearrange("p (j d) -> p j d", j=QPK)
                        q = qst[:, i % 2, t, :, ab, :]
                        pool.tensor_tensor(q[:, :, 32:48], z, q[:, :, 0:16].bitcast(F32), ALU.subtract)
                    pool.tensor_tensor(kk[:, :, 16:32], zk, kk[:, :, 0:16].bitcast(F32),
                                       ALU.subtract).then_inc(s.stack.h, 1)

                def v_parts(it, n):
                    part = lambda x: vp[:, n % TG, :, x * HD:(x + 1) * HD]
                    full, rest = (b.rearrange("p (g d) -> p g d", d=HD) for b in (vf[:, n % 2, :], vr[:, :]))
                    pool.wait_ge(s.evac.h, s.evac.done(it, 2 * n + 1))
                    pool.wait_ge(s.vp.h, s.vp.free(it, n, 1))
                    if n >= TG:
                        pool.wait_ge(s.pv.h, s.pv.done(it, 24 * ((n - TG) // 2 + 1) - 1))
                    lone(pool)
                    ch.link(pool.tensor_copy(part(0), full))
                    ch.link(pool.tensor_tensor(rest, full, part(0), ALU.subtract))
                    lone(pool)
                    ch.link(pool.tensor_copy(part(1), rest))
                    pool.tensor_tensor(part(2), rest, part(1), ALU.subtract).then_inc(s.vp.h, 1)

                def rstd_back(it, b):
                    c = 2 * (b % 2)
                    pool.wait_ge(s.bmv.h, s.bmv.done(it, b))
                    lone(pool)
                    ch.link(pool.tensor_scalar(brs[:, 0, c:c + 2], bmv[:, c:c + 2, 1], 1.0, EPS, ALU.mult, ALU.add))
                    pool.tensor_tensor(brs[:, 1, c:c + 2], brs[:, 0, c:c + 2], mhalf[:, c:c + 2],
                                       ALU.pow).then_inc(s.brs.h, 1)

                def update(it, b):
                    for n in (2 * b, 2 * b + 1):
                        x = X[:, it * TG + n, :]
                        pool.wait_ge(s.z_ready.h, s.z_ready.done(it, n))
                        pool.tensor_tensor(x, x, zA[:, n % 2, :], ALU.add).then_inc(s.xupd.h, 1)

                def steps(it, first, feed=True, prev=True, chunks=()):
                    a, b, before = first // 2 + 2, first // 2 + 3, first // 4 - 1
                    for i in range(first, first + 4):
                        j = i % 4
                        if feed or j < 1:
                            stack(it, i + 3, 0)
                        if prev and j == 3:
                            rstd_back(it, before)
                        if feed or j < 1:
                            stack(it, i + 3, 1)
                        if feed and j in (1, 2):
                            v_parts(it, a + j - 1)
                        if not feed and j == 2:
                            front_rstd(pool, ch, 1, 0)
                        if i in chunks:
                            w_split(pool, ch, 1, it, [chunks.index(i)])
                        if prev and j == 3:
                            update(it, before)

                for t in range(2):
                    stack(0, 0, t)
                for t in range(2):
                    stack(0, 1, t)
                for n in range(2):
                    v_parts(0, n)
                for t in range(2):
                    stack(0, 2, t)
                for g in range(1, NG):
                    rstd(pool, ch, g)
                steps(0, 0, prev=False)
                ch.commit()
                with pool.Fori(0, NG - 1) as it:
                    ch.begin(it, False, POOL_CHAIN_ATTN)
                    steps(it, 4, chunks=(4, 8, 9))
                    steps(it, 8, chunks=(4, 8, 9))
                    ch.end(False)
                it = NG - 1
                ch.begin(it, True, POOL_CHAIN_ATTN)
                steps(it, 4, feed=False)
                rstd_back(it, 1)
                update(it, 1)
                ch.end(True)

            def rstd(pool, ch, g):
                f, c = fr[0], slice(g * TG, (g + 1) * TG)
                pool.wait_ge(f["mv"].h, f["mv"].done(g, 0))
                lone(pool)
                ch.link(pool.tensor_scalar(frs[:, 0, :], xmv[:, c, 1], 1.0, EPS, ALU.mult, ALU.add))
                ch.link(pool.tensor_tensor(xrs[:, c, 0], frs[:, 0, :], mhalf[:, :], ALU.pow))
                pool.sem_inc(f["rs"].h, 1)

            attn = (bq, bd, first_weights, pe_attention, act_attention, dve_attention, pool_attention)

        Y = sb(top, "y_taylor_glu", [P, NG * TG, H], F32)
        z4 = sb(top, "z", [P, TG, H], F32)
        sg = sb(top, "silu_gate", [P, 2, H], F32)
        hf = sb(top, "h_full", [P, 2, H], F32)
        hh = sb(top, "h_hi", [P, 2, H], F32R)
        hl = sb(top, "h_lo", [P, 2, H], F32R)

        def z_of(s, it):
            return (lambda t: Y[:, it * TG + t, :]) if s.name == "glu_c" else (lambda t: z4[:, t, :])

        def phase_start(eng, ph, what):
            prev = phs[ph - 1]
            if what == "pe":
                sig = prev.otaken if ph == 1 else prev.o_free
                eng.wait_ge(sig.h, sig.done(NG - 1, 3))
            if what in ("act", "dve", "pool") and ph == 1:
                eng.wait_ge(prev.xupd.h, prev.xupd.done(NG - 1, 3))
                eng.wait_ge(prev.pe_end, 1)

        def pe_down(pe, s, it, f, nf, chunk, rows=P, opens=True):
            pe.wait_ge(s.hlo.h, s.hlo.done(it, f))
            for t in range(TG):
                if f == 0 and opens:
                    pe.wait_ge(s.o_free.h, s.o_free.free(it, t, 4))
                for n, (a, x) in enumerate(PASSES):
                    h = (hh, hl)[x]
                    ins = pe.matmul(Ob[t][:, :], h[0:rows, f % 2, t * P:(t + 1) * P], s.W[0:rows, chunk, a, :],
                                    start=opens and f == 0 and n == 0, stop=f == nf - 1 and n == 2)
                if f == nf - 1:
                    ins.then_inc(s.o_ready.h, 1)
            if f < nf - 1:
                ins.then_inc(s.hused.h, 1)
            else:
                pe.wait_ge(s.o_ready.h, s.o_ready.done(it, 3))
                pe.sem_inc(s.hused.h, 1)

        def act_split(act, s, it, f, src, dst):
            act.wait_ge(s.hf.h, s.hf.done(it, f))
            act.wait_ge(s.hused.h, s.hused.free(it, f, 2))
            act.activation(dst, src, ACT.Copy).then_inc(s.hhi.h, 1)

        def dve_split(dve, s, it, f, src, hi, dst):
            dve.wait_ge(s.hhi.h, s.hhi.done(it, f))
            dve.tensor_tensor(dst, src, hi.bitcast(F32), ALU.subtract).then_inc(s.hlo.h, 1)

        def act_back(act, s, it):
            for t in range(TG):
                act.wait_ge(s.o_ready.h, s.o_ready.done(it, t))
                if s.updates:
                    act.wait_ge(s.xupd.h, s.xupd.free(it, t, 4))
                    dst = z4[:, t, :]
                else:
                    dst = Y[:, it * TG + t, :]
                act.activation(dst, Ob[t][:, :], ACT.Copy).then_inc(s.o_free.h, 1)

        def dve_back(dve, ch, s, it):
            z = z_of(s, it)
            if s.name not in ("moe", "taylor"):
                for t in range(TG):
                    dve.wait_ge(s.o_ready.h, s.o_ready.done(it, t))
                    if s.name == "glu_d":
                        dve.wait_ge(s.xupd.h, s.xupd.free(it, t, 4))
                        ins = dve.tensor_tensor(z(t), Ob[t][:, :], bias3[:, :], ALU.add)
                    else:
                        y = Y[:, it * TG + t, :]
                        ins = dve.tensor_tensor(y, y, Ob[t][:, :], ALU.add)
                    ins.then_inc(s.o_free.h, 1)
            if s.updates:
                dve.wait_ge(s.o_free.h, s.o_free.done(it, 3))
                back_stats(dve, ch, s, it, range(TG), 0, z)
                back_norm(dve, s, it, range(TG), 0, z, z)

        def pool_back(pool, ch, s, it):
            if s.updates:
                back_rstd(pool, ch, s, it, range(TG), 0)
                back_update(pool, s, it, range(TG), z_of(s, it))

        def pool_phase(pool, ch, ph):
            s = phs[ph]
            phase_start(pool, ph, "pool")
            end = ph == len(PHASES) - 1

            def body(it, last):
                ch.begin(it, last, 1 + (0 if end else wper(ph + 1)) + int(s.updates))
                if not (end and last):
                    front_rstd(pool, ch, *nxt(ph, it, last))
                if not last and not end:
                    if not isinstance(it, int):
                        pool.wait_ge(phs[ph - 1].pe_end, 1)
                    w_split(pool, ch, ph + 1, it)
                pool_back(pool, ch, s, it)
                ch.end(last)

            groups(pool, body)

        def pe_glu(pe, ph):
            s = phs[ph]
            nf = s.nf
            end = ph == len(PHASES) - 1
            weights_wait(pe, ph)
            phase_start(pe, ph, "pe")

            def body(it, last):
                def up(f):
                    for n in range(2):
                        if f == 0 and n == 0:
                            pe.wait_ge(fr[ph]["lo"].h, fr[ph]["lo"].done(it, 3))
                        if f >= 2 and n == 0:
                            pe.wait_ge(s.hf.h, s.hf.done(it, f - 2))
                        features(pe, Hb[(2 * f + n) % 4],
                                 lambda k: tuple(s.W[:, 3 * f + n, a, k * P:(k + 1) * P] for a in range(2))
                                 ).then_inc(s.in_ready.h, 1)

                up(0)
                for f in range(1, nf):
                    up(f)
                    pe_down(pe, s, it, f - 1, nf, 3 * (f - 1) + 2)
                if not (end and last):
                    pe.wait_ge(s.hf.h, s.hf.done(it, nf - 1))
                    front_transpose(pe, *nxt(ph, it, last))
                pe_down(pe, s, it, nf - 1, nf, 3 * (nf - 1) + 2)

            groups(pe, body)
            pe.sem_inc(s.pe_end, 1)

        def act_glu(act, ph):
            s = phs[ph]
            nf = s.nf
            bias = b12 if s.name == "glu_d" else zero8

            def body(it, last):
                for f in range(nf):
                    act.wait_ge(s.in_ready.h, s.in_ready.done(it, 2 * f))
                    act.wait_ge(s.hf.h, s.hf.free(it, f, 2))
                    act.activation(sg[:, f % 2, :], Hb[(2 * f) % 4][:, :], ACT.Silu,
                                   bias=bias[:, f:f + 1]).then_inc(s.sg.h, 1)
                    act_split(act, s, it, f, hf[:, f % 2, :], hh[:, f % 2, :])
                if not (ph == len(PHASES) - 1 and last):
                    front_hi(act, *nxt(ph, it, last))

            groups(act, body)

        def dve_glu(dve, ch, ph):
            s = phs[ph]
            nf = s.nf
            end = ph == len(PHASES) - 1
            bias = b12 if s.name == "glu_d" else zero8

            def body(it, last):
                ch.begin(it, last, TG + (TG if s.updates else 0))
                fph, fit = nxt(ph, it, last)
                go = not (end and last)
                for f in range(nf):
                    dve.wait_ge(s.in_ready.h, s.in_ready.done(it, 2 * f + 1))
                    dve.wait_ge(s.sg.h, s.sg.done(it, f))
                    dve.scalar_tensor_tensor(out=hf[:, f % 2, :], in0=Hb[(2 * f + 1) % 4][:, :],
                                             scalar=bias[:, 4 + f:5 + f], in1=sg[:, f % 2, :],
                                             op0=ALU.add, op1=ALU.mult).then_inc(s.hf.h, 1)
                    dve_split(dve, s, it, f, hf[:, f % 2, :], hh[:, f % 2, :], hl[:, f % 2, :])
                    if go and f == 0:
                        front_stats(dve, ch, fph, fit)
                    if go and f == 1:
                        front_norm(dve, fph, fit, (0, 1))
                if go:
                    front_norm(dve, fph, fit, (2, 3))
                    front_lo(dve, fph, fit)
                dve_back(dve, ch, s, it)
                ch.end(last)

            groups(dve, body)

        smallm = sb(top, "route_small", [P, 8, TG], F32)
        m8 = sb(top, "route_max8", [P, TG, 8], F32)
        i8 = sb(top, "route_index8", [P, TG, 8], U32)
        idx = sb(top, "route_index", [P, TG, 2], F32)
        gate = sb(top, "route_gate", [P, TG, 2, NE], F32)
        hs = z4

        def pe_moe(pe):
            s = phs[1]
            weights_wait(pe, 1)
            phase_start(pe, 1, "pe")

            def body(it, last):
                pe.wait_ge(fr[1]["lo"].h, fr[1]["lo"].done(it, 3))
                for t in range(TG):
                    tokens_by_weights(pe, Hb[t], 256, t, lambda k: tuple(
                        s.W[:, 4 + k // 2, a, (k % 2) * 256:(k % 2) * 256 + 256] for a in range(2))
                    ).then_inc(s.in_ready.h, 1)
                for t in range(TG):
                    pe.wait_ge(s.o_free.h, s.o_free.free(it, t, 4))
                    tokens_by_weights(pe, Ob[t], 512, t, lambda k: (s.W[:, k, 0, :], s.W[:, k, 1, :]), final=False)
                pe.wait_ge(s.hs.h, s.hs.done(it, 3))
                for t in range(TG):
                    for j in range(2):
                        ins = pe.transpose(Hb[j][0:LH, t * P:(t + 1) * P], hs[:, t, j * LH:(j + 1) * LH], identf)
                ins.then_inc(s.ht.h, 1)
                for f in range(2):
                    pe_down(pe, s, it, f, 2, 6 + f, rows=LH, opens=False)
                front_transpose(pe, *nxt(1, it, last))

            groups(pe, body)
            pe.sem_inc(s.pe_end, 1)

        def act_moe(act):
            s = phs[1]
            phase_start(act, 1, "act")
            act.dma_start(bias3[:, :], biases[:, 1280:1792]).then_inc(s_bias3, 16)

            def body(it, last):
                act.wait_ge(s.rt.h, s.rt.done(it, 0))
                act.activation(smallm[:, 1, :], smallm[:, 0, :], ACT.Exp).then_inc(s.re.h, 1)
                act.wait_ge(s.ht.h, s.ht.done(it, 0))
                for f in range(2):
                    act.wait_ge(s.hused.h, s.hused.free(it, f, 2))
                    act.activation(hh[0:LH, f, :], Hb[f][0:LH, :], ACT.Copy).then_inc(s.hhi.h, 1)
                act_back(act, s, it)
                front_hi(act, *nxt(1, it, last))

            groups(act, body)

        def dve_moe(dve, ch):
            s = phs[1]
            phase_start(dve, 1, "dve")

            def body(it, last):
                ch.begin(it, last, DVE_CHAIN_MOE)
                fph, fit = nxt(1, it, last)
                for t in range(TG):
                    lg = Hb[t][:, LR:LR + NE]
                    dve.wait_ge(s.in_ready.h, s.in_ready.done(it, t))
                    lone(dve)
                    ch.link(dve.max(m8[:, t, :], lg))
                    lone(dve)
                    dve.max_index(i8[:, t, :], m8[:, t, :], lg)
                ch.link(dve.tensor_tensor(smallm[:, 0, :], m8[:, :, 1], m8[:, :, 0], ALU.subtract))
                dve.sem_inc(s.rt.h, 1)
                ch.link(dve.tensor_copy(idx[:, :, :], i8[:, :, 0:2]))
                dve.wait_ge(s.re.h, s.re.done(it, 0))
                ch.link(dve.tensor_scalar(smallm[:, 2, :], smallm[:, 1, :], 1.0, None, ALU.add))
                ch.link(dve.reciprocal(smallm[:, 3, :], smallm[:, 2, :]))
                ch.link(dve.tensor_scalar(smallm[:, 4, :], smallm[:, 3, :], 2.0, None, ALU.mult))
                ch.link(dve.tensor_tensor(smallm[:, 5, :], smallm[:, 4, :], smallm[:, 1, :], ALU.mult))
                for t in range(TG):
                    for c in range(2):
                        ins = dve.tensor_scalar(gate[:, t, c, :], iota, idx[:, t, c:c + 1], smallm[:, 4 + c, t:t + 1],
                                                ALU.is_equal, ALU.mult)
                ch.link(ins)
                ch.link(dve.tensor_tensor(gate[:, :, 0, :], gate[:, :, 0, :], gate[:, :, 1, :], ALU.add))
                for t in range(TG):
                    dve.wait_ge(s.xupd.h, s.xupd.free(it, t, 4))
                    dve.tensor_tensor(hs[:, t, 0:LR].rearrange("p (e r) -> p e r", r=RANK),
                                      Hb[t][:, 0:LR].rearrange("p (e r) -> p e r", r=RANK),
                                      gate[:, t, 0, :].unsqueeze(2).broadcast_to([P, NE, RANK]),
                                      ALU.mult).then_inc(s.hs.h, 1)
                front_stats(dve, ch, fph, fit, (0, 1))
                for f in range(2):
                    dve.wait_ge(s.hhi.h, s.hhi.done(it, f))
                    dve.tensor_tensor(hl[0:LH, f, :], Hb[f][0:LH, :], hh[0:LH, f, :].bitcast(F32),
                                      ALU.subtract).then_inc(s.hlo.h, 1)
                front_stats(dve, ch, fph, fit, (2, 3))
                front_norm(dve, fph, fit, range(4))
                front_lo(dve, fph, fit)
                dve_back(dve, ch, s, it)
                ch.end(last)

            groups(dve, body)

        dl = sb(top, "delta", [P, 2, H], F32)

        def pe_taylor(pe):
            s = phs[2]
            weights_wait(pe, 2)
            phase_start(pe, 2, "pe")

            def body(it, last):
                for n in range(2):
                    if n == 0:
                        pe.wait_ge(fr[2]["lo"].h, fr[2]["lo"].done(it, 3))
                        pe.wait_ge(phs[1].hlo.h, phs[1].hlo.done(NG - 1, 1))
                    features(pe, Hb[n], lambda k: tuple(
                        s.W[:, k // 2, a, (k % 2) * 256 + n * P:(k % 2) * 256 + (n + 1) * P] for a in range(2))
                    ).then_inc(s.in_ready.h, 1)
                for f in range(s.nf):
                    pe_down(pe, s, it, f, s.nf, 2 + f)
                    if f == s.nf - 2:
                        front_transpose(pe, *nxt(2, it, last))

            groups(pe, body)
            pe.sem_inc(s.pe_end, 1)

        def act_taylor(act):
            s = phs[2]

            def body(it, last):
                for f in range(s.nf):
                    act_split(act, s, it, f, hf[:, f % 2, :], hh[:, f % 2, :])
                front_hi(act, *nxt(2, it, last))
                act_back(act, s, it)

            groups(act, body)

        def dve_taylor(dve, ch):
            s = phs[2]

            def body(it, last):
                ch.begin(it, last, DVE_CHAIN_TAYLOR)
                fph, fit = nxt(2, it, last)
                dve.wait_ge(s.in_ready.h, s.in_ready.done(it, 0))
                dve.tensor_copy(hf[:, 0, :], Hb[0][:, :]).then_inc(s.hf.h, 1)
                dve_split(dve, s, it, 0, hf[:, 0, :], hh[:, 0, :], hl[:, 0, :])
                dve.wait_ge(s.in_ready.h, s.in_ready.done(it, 1))
                ch.link(dve.tensor_scalar(dl[:, 0, :], Hb[1][:, :], lp, None, ALU.subtract))
                dve.sem_inc(s.sg.h, 1)
                ch.link(dve.scalar_tensor_tensor(out=dl[:, 1, :], in0=dl[:, 0, :], scalar=-1.0, in1=dl[:, 0, :],
                                                 op0=ALU.mult, op1=ALU.max))
                ch.link(dve.scalar_tensor_tensor(out=dl[:, 1, :], in0=dl[:, 1, :], scalar=THD, in1=dl[:, 0, :],
                                                 op0=ALU.is_le, op1=ALU.mult))
                for f in range(1, s.nf):
                    dve.wait_ge(s.hf.h, s.hf.done(it, f - 1))
                    dve.scalar_tensor_tensor(out=hf[:, f % 2, :], in0=hf[:, (f - 1) % 2, :],
                                             scalar=cfac[:, f - 1:f], in1=dl[:, 1 if f == 5 else 0, :],
                                             op0=ALU.mult, op1=ALU.mult).then_inc(s.hf.h, 1)
                    if f <= TG:
                        front_stats(dve, ch, fph, fit, (f - 1,))
                    dve_split(dve, s, it, f, hf[:, f % 2, :], hh[:, f % 2, :], hl[:, f % 2, :])
                    if f == 5:
                        front_norm(dve, fph, fit, (0, 1))
                front_norm(dve, fph, fit, (2, 3))
                front_lo(dve, fph, fit)
                dve_back(dve, ch, s, it)
                ch.end(last)

            groups(dve, body)

        bias3 = sb(top, "bias_w3", [P, H], F32)
        bq, bd, first_weights, pe_attention, act_attention, dve_attention, pool_attention = attn

        DVE_CHAIN_ATTN, DVE_CHAIN_MOE, DVE_CHAIN_TAYLOR, POOL_CHAIN_ATTN = 28, 20, 7, 33

        block = top.enter_context(nc.Block())

        @block.sync
        def _(sp):
            xr = x_in.rearrange("(g t p) n -> g p t n", g=NG, p=P)
            outr = out.rearrange("(g t p) n -> g p t n", g=NG, p=P)
            sp.dma_start(X[:, 0:TG, :], xr[0]).then_inc(s_x[0], 16)
            sp.dma_start(cf[:, :], cons_f).then_inc(s_cf, 16)
            for j in range(6):
                sp.dma_start(first_weights(j), w_in[j]).then_inc(s_wa[j], 16)
            sp.dma_start(bq[:, :], biases[:, 0:768]).then_inc(s_bq, 16)
            sp.dma_start(cb[:, :], cons_b).then_inc(s_cb, 16)
            for g in range(1, NG):
                sp.dma_start(X[:, g * TG:(g + 1) * TG, :], xr[g]).then_inc(s_x[g], 16)
                if g == 1:
                    for j in range(6, PHASES[0][1]):
                        sp.dma_start(first_weights(j), w_in[j]).then_inc(s_wa[j], 16)
                    sp.dma_start(bd[:, :], biases[:, 768:1280]).then_inc(s_bd, 16)
            for ph in range(1, len(PHASES)):
                with sp.Fori(0, 3) as it:
                    w_load(sp, ph, it)
            s = phs[-1]
            for g in range(NG):
                sp.wait_ge(s.xupd.h, s.xupd.done(g, 3))
                sp.dma_start(outr[g], X[:, g * TG:(g + 1) * TG, :]).then_inc(s_out, 16)
            sp.wait_ge(s_out, 16 * NG)

        @block.gpsimd
        def _(pool):
            ch = Chain(pool, chain_pool)
            pool_attention(pool, ch)
            for ph in range(1, len(PHASES)):
                pool_phase(pool, ch, ph)

        @block.scalar
        def _(act):
            act_attention(act)
            act_moe(act)
            act_taylor(act)
            for ph in range(3, 7):
                act_glu(act, ph)

        @block.vector
        def _(dve):
            ch = Chain(dve, chain_dve)
            dve.wait_ge(s_cf, 16)
            dve.tensor_scalar(cfac[:, 0:1], disc[:, 0:1], -1.0, None, ALU.mult)
            dve.tensor_tensor(cfac[:, 1:NORD], disc[:, 0:NORD - 1], disc[:, 1:NORD], ALU.subtract).then_inc(chain_act, 1)
            dve_attention(dve, ch)
            dve_moe(dve, ch)
            dve.wait_ge(chain_act, 2)
            dve_taylor(dve, ch)
            dve.wait_ge(s_bias3, 16)
            for ph in range(3, 7):
                dve_glu(dve, ch, ph)

        @block.tensor
        def _(pe):
            pe_attention(pe)
            pe_moe(pe)
            pe_taylor(pe)
            for ph in range(3, 7):
                pe_glu(pe, ph)


def kernel(**inputs):
    import numpy as np
    import ml_dtypes
    import concourse.bacc as bacc
    from concourse.bass_utils import run_bass_kernel_spmd as run

    a = {k: np.asarray(v) for k, v in inputs.items()}
    x = a["L0_attn_hidden_states"]
    B, S, _ = x.shape

    def k_tiles(w, cols):
        wt = w.T
        full = np.zeros((wt.shape[0], cols), np.float32)
        full[:, :wt.shape[1]] = wt
        return full.reshape(-1, P, cols)

    wq = a["L0_attn_w_qkv"].reshape(NKV, QPK + 2, HD, H)
    bqkv = a["L0_attn_b_qkv"].reshape(NKV, QPK + 2, HD)
    q_w = k_tiles(wq[:, :QPK].reshape(-1, H), 512)
    kv_w = k_tiles(np.concatenate([wq[:, QPK].reshape(-1, H), wq[:, QPK + 1].reshape(-1, H)]), 256)
    b_row = np.concatenate([bqkv[:, :QPK].reshape(-1), bqkv[:, QPK].reshape(-1), bqkv[:, QPK + 1].reshape(-1),
                            a["L0_attn_b_dense"], a["L1_ffn_b3"]])

    def two(t):
        return [np.concatenate([t[2 * i], t[2 * i + 1]], axis=1) for i in range(2)]

    def glu(w1, w2, w3, tiles):
        out = []
        for f in tiles:
            for w in (w1, w2):
                wt = np.zeros((P, H), np.float32)
                part = w[f * P:(f + 1) * P]
                wt[:part.shape[0]] = part
                out.append(wt.T.reshape(KT, P, P).transpose(1, 0, 2).reshape(P, H))
            d = np.zeros((P, H), np.float32)
            part = w3.T[f * P:(f + 1) * P]
            d[:part.shape[0]] = part
            out.append(d)
        return out

    zero = np.zeros((P, H), np.float32)
    chunks = list(q_w) + two(kv_w) + list(k_tiles(a["L0_attn_w_dense"], 512))
    la = a["L0_ffn_lora_A"].reshape(LR, H)
    chunks += list(k_tiles(a["L0_ffn_base_W"], 512)) + two(k_tiles(np.concatenate([la, a["L0_ffn_gate_W"]]), 256))
    lb = a["L0_ffn_lora_B"].transpose(0, 2, 1).reshape(2, LH, H)
    for j in range(2):
        c = zero.copy()
        c[:LH] = lb[j]
        chunks.append(c)
    chunks.append(zero)
    chunks += two(k_tiles(np.concatenate([a["L1_attn_up_w"], a["L1_attn_gate_w"]]), 256))
    chunks.append(np.ascontiguousarray(a["L1_attn_local_approx_output"].T))
    chunks += list(a["L1_attn_fuse_weight"].transpose(2, 1, 0))
    gw, uw, dw = a["L1_attn_ffn_gate_w"], a["L1_attn_ffn_up_w"], a["L1_attn_ffn_down_w"]
    for tiles in (range(0, 3), range(3, 7), range(7, 10)):
        chunks += glu(gw, uw, dw, tiles)
    w12 = a["L1_ffn_w12"]
    chunks += glu(w12[:H], w12[H:], a["L1_ffn_w3"], range(4))
    assert len(chunks) == CHUNK0[-1]

    inv = (1.0 / np.float32(1000000.0) ** (np.arange(0, HD, 2, dtype=np.float32) / np.float32(HD))).astype(np.float32)
    fr = np.outer(np.arange(S, dtype=np.float32), inv).astype(np.float32)
    cos, sin = np.cos(fr), np.sin(fr)
    cf = np.zeros((P, 247), np.float32)
    cf[:, 0:128] = np.eye(P)
    cf[:, 128:160] = np.concatenate([cos, cos], 1).reshape(2, P, HD).transpose(1, 0, 2).reshape(P, -1)
    cf[:, 160:176] = sin.reshape(2, P, HD // 2).transpose(1, 0, 2).reshape(P, -1)
    cf[:, 176:192] = -cf[:, 160:176]
    cf[:, 192:192 + NE] = np.arange(NE)
    cf[:, 224] = a["L1_attn_local_point"]
    cf[:, 225:231] = a["L1_attn_discount_factor"]
    cf[:, 231:239] = a["L1_ffn_b12"].reshape(8, P).T
    bf = ml_dtypes.bfloat16
    cb = np.zeros((P, 1408), np.float32)
    cb[:, 0:128] = np.eye(P)
    up = np.triu(np.ones((P, P)), 1)
    cb[:, 128:256] = up * MASKED
    cb[:, 256:384] = up.T * MASKED
    for r in range(16):
        cb[r, 384 + 128 * (r % 8):512 + 128 * (r % 8)] = -1.0
    cb = cb.astype(bf)

    arrays = {
        "x": np.ascontiguousarray(x.reshape(B * S, H)),
        "w": np.ascontiguousarray(np.stack(chunks)),
        "cf": cf, "cb": cb,
        "bias": np.ascontiguousarray(np.broadcast_to(b_row, (P, b_row.size))),
    }
    nc = bacc.Bacc("TRN2", target_bir_lowering=False, num_devices=1)
    aps = [nc.dram_tensor(n, v.shape, mybir.dt.from_np(v.dtype), kind="ExternalInput").ap() for n, v in arrays.items()]
    out = nc.dram_tensor("out", [B * S, H], F32, kind="ExternalOutput").ap()
    build(nc, *aps, out)
    r = run(nc, [arrays], core_ids=[0])
    return r.results[0]["out"].reshape(B, S, H)
```
